# Optimizing a Trainium2 kernel written in Bass

```python
import numpy as np
import jax
import jax.numpy as jnp

def _softmax(x, axis=-1):
    return jax.nn.softmax(x, axis=axis)

def _gelu(x):
    return jax.nn.gelu(x, approximate=True)

def _silu(x):
    return jax.nn.silu(x)

def _sigmoid(x):
    return jax.nn.sigmoid(x)

def _layernorm(x, axis=-1, eps=1e-05):
    m = jnp.mean(x, axis=axis, keepdims=True)
    v = jnp.var(x, axis=axis, keepdims=True)
    return (x - m) / jnp.sqrt(v + eps)

def _scatter_add(tgt, idx, src, axis=0):
    return tgt.at[idx].add(src)

def _segment_sum(src, seg, n):
    return jax.ops.segment_sum(src, seg, n)
kernel_name = 'mk_gps_d1_gnn_r64_573845'

def setup_inputs(seed: int=0):
    np.random.seed(seed)
    _w = jnp.asarray

    def _rec_inputs():
        import jax
        import jax.numpy as jnp
        _gk = jax.random.key(seed)
        x = -0.0002117 + 1 * jax.random.normal(jax.random.fold_in(_gk, 1), (10000, 512), jnp.float32)
        src = jax.random.randint(jax.random.fold_in(_gk, 2), (2500,), 0, 10000, jnp.int32)
        dst = jnp.minimum((10000 * jax.random.uniform(jax.random.fold_in(_gk, 3), (2500,)) ** 2.0).astype(jnp.int32), 9999)
        _o = jnp.argsort(dst, stable=True)
        src = src[_o]
        dst = dst[_o]
        return (x, src, dst)
    x, src, dst = _rec_inputs()

    def _L0_gnn_setup():
        import jax, jax.numpy as jnp
        import numpy as np
        N_NODES = 50000
        N_EDGES = 12500
        D = 512
        N_LAYERS = 3
        EPS = 1e-12
        key = jax.random.key(seed)
        ks = jax.random.split(key, 6)
        x = jax.random.normal(ks[0], (N_NODES, D), dtype=jnp.float32)
        src = jax.random.randint(ks[1], (N_EDGES,), 0, N_NODES, dtype=jnp.int64)
        dst = jax.random.randint(ks[2], (N_EDGES,), 0, N_NODES, dtype=jnp.int64)
        scale = 1.0 / np.sqrt(D)
        W_self = jax.random.normal(ks[3], (N_LAYERS, D, D), dtype=jnp.float32) * scale
        W_neigh = jax.random.normal(ks[4], (N_LAYERS, D, D), dtype=jnp.float32) * scale
        b = jax.random.normal(ks[5], (N_LAYERS, D), dtype=jnp.float32) * 0.01
        return {'x': x, 'src': src, 'dst': dst, 'W_self': W_self, 'W_neigh': W_neigh, 'b': b}
    _L0_gnn_all = _L0_gnn_setup()
    _L0_gnn_in = {k: v for k, v in _L0_gnn_all.items() if k in ('W_self', 'W_neigh', 'b')}
    del _L0_gnn_all

    def _L0_mix_setup():
        import jax, jax.numpy as jnp
        import numpy as np
        B, S, D, H, R, P = (4, 128, 512, 8, 64, 4)
        HD = D // H
        EPS = 1e-06

        def _sketch_p4(z, G1, G2):
            inv_sqrt_r = 1.0 / np.sqrt(R).astype(np.float32)
            half = inv_sqrt_r * (z @ G1 * (z @ G2))
            return half * half
        key = jax.random.key(seed)
        ks = jax.random.split(key, 16)
        lin = lambda k: jax.random.normal(k, (D, D), jnp.float32) * (1.0 / np.sqrt(D))
        g = lambda k: jax.random.normal(k, (HD, R), jnp.float32) * (1.0 / np.sqrt(R))
        return {'x': jax.random.normal(ks[0], (B, S, D), jnp.float32), 'Wq': lin(ks[1]), 'bq': jnp.zeros((D,), jnp.float32), 'Wk': lin(ks[2]), 'bk': jnp.zeros((D,), jnp.float32), 'Wv': lin(ks[3]), 'bv': jnp.zeros((D,), jnp.float32), 'Wp': lin(ks[4]), 'bp': jnp.zeros((D,), jnp.float32), 'gamma_q': jnp.ones((1,), jnp.float32), 'beta_q': jnp.zeros((1,), jnp.float32), 'gamma_k': jnp.ones((1,), jnp.float32), 'beta_k': jnp.zeros((1,), jnp.float32), 'qG1': g(ks[5]), 'qG2': g(ks[6]), 'kG1': g(ks[7]), 'kG2': g(ks[8])}
    _L0_mix_all = _L0_mix_setup()
    _L0_mix_in = {k: v for k, v in _L0_mix_all.items() if k in ('Wq', 'bq', 'Wk', 'bk', 'Wv', 'bv', 'Wp', 'bp', 'gamma_q', 'beta_q', 'gamma_k', 'beta_k', 'qG1', 'qG2', 'kG1', 'kG2')}
    del _L0_mix_all

    def _L0_ffn_setup():
        import jax, jax.numpy as jnp
        import numpy as np
        B, L, D, H, E, K = (8, 128, 512, 32, 8, 2)
        SCALE = 0.02
        key = jax.random.key(seed)
        ks = jax.random.split(key, 6)
        return {'x': jax.random.normal(ks[0], (B, L, D), dtype=jnp.float32), 'Wg': jax.random.normal(ks[1], (D, E), dtype=jnp.float32) * SCALE, 'W1': jax.random.normal(ks[2], (E, D, H), dtype=jnp.float32) * SCALE, 'b1': jax.random.normal(ks[3], (E, H), dtype=jnp.float32) * SCALE, 'W2': jax.random.normal(ks[4], (E, H, D), dtype=jnp.float32) * SCALE, 'b2': jax.random.normal(ks[5], (E, D), dtype=jnp.float32) * SCALE}
    _L0_ffn_all = _L0_ffn_setup()
    _L0_ffn_in = {k: v for k, v in _L0_ffn_all.items() if k in ('Wg', 'W1', 'b1', 'W2', 'b2')}
    del _L0_ffn_all
    return {'x': x, 'src': src, 'dst': dst, 'L0_gnn_W_self': _L0_gnn_in['W_self'], 'L0_gnn_W_neigh': _L0_gnn_in['W_neigh'], 'L0_gnn_b': _L0_gnn_in['b'], 'L0_mix_Wq': _L0_mix_in['Wq'], 'L0_mix_bq': _L0_mix_in['bq'], 'L0_mix_Wk': _L0_mix_in['Wk'], 'L0_mix_bk': _L0_mix_in['bk'], 'L0_mix_Wv': _L0_mix_in['Wv'], 'L0_mix_bv': _L0_mix_in['bv'], 'L0_mix_Wp': _L0_mix_in['Wp'], 'L0_mix_bp': _L0_mix_in['bp'], 'L0_mix_gamma_q': _L0_mix_in['gamma_q'], 'L0_mix_beta_q': _L0_mix_in['beta_q'], 'L0_mix_gamma_k': _L0_mix_in['gamma_k'], 'L0_mix_beta_k': _L0_mix_in['beta_k'], 'L0_mix_qG1': _L0_mix_in['qG1'], 'L0_mix_qG2': _L0_mix_in['qG2'], 'L0_mix_kG1': _L0_mix_in['kG1'], 'L0_mix_kG2': _L0_mix_in['kG2'], 'L0_ffn_Wg': _L0_ffn_in['Wg'], 'L0_ffn_W1': _L0_ffn_in['W1'], 'L0_ffn_b1': _L0_ffn_in['b1'], 'L0_ffn_W2': _L0_ffn_in['W2'], 'L0_ffn_b2': _L0_ffn_in['b2']}

def reference(x, src, dst, L0_gnn_W_self, L0_gnn_W_neigh, L0_gnn_b, L0_mix_Wq, L0_mix_bq, L0_mix_Wk, L0_mix_bk, L0_mix_Wv, L0_mix_bv, L0_mix_Wp, L0_mix_bp, L0_mix_gamma_q, L0_mix_beta_q, L0_mix_gamma_k, L0_mix_beta_k, L0_mix_qG1, L0_mix_qG2, L0_mix_kG1, L0_mix_kG2, L0_ffn_Wg, L0_ffn_W1, L0_ffn_b1, L0_ffn_W2, L0_ffn_b2):
    import jax
    import jax.numpy as jnp

    def _L0_gnn_ref(x, src, dst, W_self, W_neigh, b):
        import jax, jax.numpy as jnp
        import numpy as np
        N_NODES = 50000
        N_EDGES = 12500
        D = 512
        N_LAYERS = 3
        EPS = 1e-12
        n = x.shape[0]
        deg = jax.ops.segment_sum(jnp.ones_like(dst, dtype=x.dtype), dst, num_segments=n)
        deg = jnp.maximum(deg, 1.0)[:, None]
        h = x
        for l in range(N_LAYERS):
            h_neigh = jax.ops.segment_sum(h[src], dst, num_segments=n) / deg
            rst = h @ W_self[l] + h_neigh @ W_neigh[l] + b[l]
            rst = jax.nn.relu(rst)
            nrm = jnp.sqrt(jnp.sum(rst * rst, axis=-1, keepdims=True))
            h = rst / jnp.maximum(nrm, EPS)
        return h

    def _L0_mix_ref(x, Wq, bq, Wk, bk, Wv, bv, Wp, bp, gamma_q, beta_q, gamma_k, beta_k, qG1, qG2, kG1, kG2):
        import jax, jax.numpy as jnp
        import numpy as np
        B, S, D, H, R, P = (4, 128, 512, 8, 64, 4)
        HD = D // H
        EPS = 1e-06

        def _sketch_p4(z, G1, G2):
            inv_sqrt_r = 1.0 / np.sqrt(R).astype(np.float32)
            half = inv_sqrt_r * (z @ G1 * (z @ G2))
            return half * half
        b, s, d = x.shape
        split = lambda t: t.reshape(b, s, H, HD).transpose(0, 2, 1, 3)
        q = split(x @ Wq + bq)
        k = split(x @ Wk + bk)
        v = split(x @ Wv + bv)
        q = gamma_q * q + beta_q
        k = gamma_k * k + beta_k
        phi_q = _sketch_p4(q, qG1, qG2)
        phi_k = _sketch_p4(k, kG1, kG2)
        kv = jnp.einsum('bhsr,bhsd->bhrd', phi_k, v)
        ksum = phi_k.sum(axis=2)
        num = jnp.einsum('bhqr,bhrd->bhqd', phi_q, kv)
        den = jnp.einsum('bhqr,bhr->bhq', phi_q, ksum) + EPS
        out = num / den[..., None]
        out = out.transpose(0, 2, 1, 3).reshape(b, s, d)
        return out @ Wp + bp

    def _L0_ffn_ref(x, Wg, W1, b1, W2, b2):
        import jax, jax.numpy as jnp
        import numpy as np
        B, L, D, H, E, K = (8, 128, 512, 32, 8, 2)
        SCALE = 0.02
        b, l, d = x.shape
        xt = x.reshape(-1, d)
        T = xt.shape[0]
        gate = jax.nn.softmax(xt @ Wg, axis=-1)
        topv, topi = jax.lax.top_k(gate, K)
        topv = topv / (jnp.sum(topv, axis=-1, keepdims=True) + 1e-06)
        scores = jnp.zeros((T, E), dtype=xt.dtype).at[jnp.arange(T)[:, None], topi].set(topv)
        out = jnp.zeros_like(xt)
        for e in range(E):
            h = jax.nn.gelu(xt @ W1[e] + b1[e], approximate=False)
            ye = h @ W2[e] + b2[e]
            out = out + ye * scores[:, e:e + 1]
        return out.reshape(b, l, d)
    xn = _layernorm(x, axis=-1)
    x = x + _L0_gnn_ref(xn, src, dst, L0_gnn_W_self, L0_gnn_W_neigh, L0_gnn_b) + _L0_mix_ref(xn[None], L0_mix_Wq, L0_mix_bq, L0_mix_Wk, L0_mix_bk, L0_mix_Wv, L0_mix_bv, L0_mix_Wp, L0_mix_bp, L0_mix_gamma_q, L0_mix_beta_q, L0_mix_gamma_k, L0_mix_beta_k, L0_mix_qG1, L0_mix_qG2, L0_mix_kG1, L0_mix_kG2)[0]
    x = x + _L0_ffn_ref(_layernorm(x, axis=-1)[None], L0_ffn_Wg, L0_ffn_W1, L0_ffn_b1, L0_ffn_W2, L0_ffn_b2)[0]
    return x

_drawn_inputs = setup_inputs


def setup_inputs(seed=0):
    import zlib

    import numpy as np

    out = dict(_drawn_inputs(seed))
    spreads = {'L0_mix_bq': (0.0, 2.0),
     'L0_mix_bk': (0.0, 0.8),
     'L0_mix_bv': (0.0, 0.1),
     'L0_mix_bp': (0.0, 0.1)}
    factors = {'L0_gnn_W_neigh': 3.934,
     'L0_gnn_b': 4.427,
     'L0_mix_Wq': 5.819,
     'L0_mix_Wk': 5.052,
     'L0_mix_Wv': 3.722,
     'L0_mix_qG1': 6.773,
     'L0_mix_qG2': 6.705,
     'L0_mix_kG1': 6.324,
     'L0_mix_kG2': 6.265,
     'L0_ffn_W1': 2.859,
     'L0_ffn_b1': 8.0,
     'L0_ffn_W2': 2.737,
     'L0_ffn_b2': 3.885}
    for name, (base, spread) in spreads.items():
        noise = np.random.default_rng([zlib.crc32(name.encode()), seed]).standard_normal(out[name].shape)
        drawn = base * np.exp(spread * noise) if base else spread * noise
        out[name] = jnp.asarray(drawn.astype(out[name].dtype))
    for name, factor in factors.items():
        out[name] = (out[name] * factor).astype(out[name].dtype)
    return out
```

```python
from contextlib import ExitStack

import numpy as np

import concourse.bass as bass
from concourse import mybir

F32 = mybir.dt.float32
F32R = mybir.dt.float32r
I32 = mybir.dt.int32
U32 = mybir.dt.uint32
ACT = mybir.ActivationFunctionType
ALU = mybir.AluOpType
AX = mybir.AxisListType

P = 128
PT = 125
J = 4
GT = PT * J
PA = 112
D = 512
C = D // P
H = 8
R = 64
NE = 8
HE = 32
FE = NE * HE
FG = FE + NE
LN_EPS = 1e-5
NORM_EPS2 = 1e-24
DEN_EPS = 1e-6


def need(eng, sem, value):
    if isinstance(value, int) and value <= 0:
        return
    eng.wait_ge(sem, value)


def alone(eng, waited):
    eng.sem_inc(waited, 1)


def tile_steps(eng, body, first, end, groups):
    for s in range(first, 2 * J):
        body(s, s % J)
    with eng.Fori(2, groups - 2) as g:
        for j in range(J):
            body(g * J + j, j)
    for s in range((groups - 2) * J, end):
        body(s, s % J)


def three(pe, out, a_hi, a_lo, b_hi, b_lo, first, last):
    pe.matmul(out, a_hi, b_hi, start=first, stop=False)
    pe.matmul(out, a_hi, b_lo, start=False, stop=False)
    return pe.matmul(out, a_lo, b_hi, start=False, stop=last)


def rows_of(dram, g, j0, j1):
    v = dram.rearrange("(q j) d -> q j d", j=J)
    for a, b in ((0, PA), (PA, PT)):
        yield slice(a, b), v[bass.ds(g * PT + a, b - a), j0:j1, :]


def load_group(eng, tile, dram, g, sem):
    for part, view in rows_of(dram, g, 0, J):
        eng.dma_start(tile[part, :, :], view).then_inc(sem, 16)


def load_pair(eng, tile, dram, g, j0, sem):
    for part, view in rows_of(dram, g, j0, j0 + 2):
        eng.dma_start(tile[part, j0:j0 + 2, :], view).then_inc(sem, 16)


def store_pair(eng, dram, tile, g, j0, sem):
    for part, view in rows_of(dram, g, j0, j0 + 2):
        eng.dma_start(view, tile[part, j0:j0 + 2, :]).then_inc(sem, 16)


class Pass:

    def __init__(self, nc, name):
        self.nc, self.name, self.ctx, self.sems = nc, name, ExitStack(), []

    def __enter__(self):
        self.ctx.__enter__()
        self.ctx.enter_context(self.nc.allow_non_contiguous_dma(reason="a few thousand words of indices and biases"))
        self.pool_waited, self.dve_waited, self.sp_waited = (self.sem(n) for n in ("pool_waited", "dve_waited", "sp_waited"))
        return self

    def __exit__(self, *a):
        self.ctx.__exit__(*a)
        self.nc.clear_and_free_semaphores(self.sems)
        self.nc.all_engine_barrier()

    def sb(self, name, shape, dt=F32):
        return self.ctx.enter_context(self.nc.sbuf_tensor(f"{self.name}_{name}", shape, dt))

    def ps(self, name, shape=(P, 512), dt=F32):
        return self.ctx.enter_context(self.nc.psum_tensor(f"{self.name}_{name}", list(shape), dt))

    def sem(self, name):
        self.sems.append(self.nc.alloc_semaphore(f"{self.name}_{name}"))
        return self.sems[-1]

    def block(self):
        return self.ctx.enter_context(self.nc.Block())


class Weights:

    def __init__(self, w, drams, scales=None, raw=None):
        self.drams, self.scales = drams, scales or [1.0] * len(drams)
        self.hi = [w.sb(f"w{i}_hi", [P, C, D], F32R) for i in range(len(drams))]
        self.lo = [w.sb(f"w{i}_lo", [P, C, D], F32R) for i in range(len(drams))]
        self.raw = [w.sb(f"w_raw{i}", [P, C, D]) for i in range(min(2, len(drams)))]
        self.loaded = [w.sem(f"w_loaded{i}") for i in range(len(self.raw))]
        self.hi_done, self.lo_done = w.sem("w_hi_done"), w.sem("w_lo_done")

    def load(self, sp):
        for i, dram in enumerate(self.drams):
            if i >= 2:
                sp.wait_ge(self.lo_done, i - 1)
            sp.dma_start(self.raw[i % 2][:, :, :], dram.rearrange("(c p) n -> p c n", p=P)).then_inc(self.loaded[i % 2], 16)

    def split_hi(self, act, i):
        act.wait_ge(self.loaded[i % 2], 16 * (i // 2 + 1))
        act.activation(self.hi[i][:, :, :], self.raw[i % 2][:, :, :], ACT.Identity, scale=self.scales[i]).then_inc(self.hi_done, 1)

    def split_lo(self, dve, i):
        dve.wait_ge(self.hi_done, i + 1)
        dve.scalar_tensor_tensor(self.lo[i][:, :, :], self.raw[i % 2][:, :, :], self.scales[i],
                                 self.hi[i][:, :, :].bitcast(F32), ALU.mult, ALU.subtract).then_inc(self.lo_done, 1)

    def wait(self, pe, i):
        pe.wait_ge(self.lo_done, i + 1)


def build_constants(nc, k, arg, N, E):
    with Pass(nc, "const") as w:
        ones_set, id_done, rows_in = w.sem("ones_set"), w.sem("id_done"), w.sem("rows_in")
        block = w.block()

        @block.sync
        def _(sp):
            for l in range(3):
                sp.dma_start(k.bias[:, l, :], arg["L0_gnn_b"][l:l + 1, :].partition_broadcast(P)).then_inc(rows_in, 16)
            sp.dma_start(k.bp[:, :], arg["L0_mix_bp"].rearrange("(o n) -> o n", o=1).partition_broadcast(P)).then_inc(rows_in, 16)
            sp.wait_ge(rows_in, 64)

        @block.gpsimd
        def _(pool):
            pool.memset(k.ident[:, :], 1.0).then_inc(ones_set, 1)
            pool.memset(k.ones[:, :], 1.0).then_inc(ones_set, 1)
            pool.memset(k.minus_half[:, :], -0.5).then_inc(ones_set, 1)
            pool.wait_ge(ones_set, 3)
            pool.affine_select(out=k.ident[:, :], in_=k.ident[:, :], compare_op=ALU.is_equal, fill=0.0, base=0,
                               pattern=[[1, P]], channel_multiplier=-1).then_inc(id_done, 1)
            pool.wait_ge(id_done, 1)


def build_sort(nc, k, arg, N, E):
    T = E // PT
    with Pass(nc, "sort") as w:
        row_i, row = w.sb("row_i", [PT, E], I32), w.sb("row", [PT, E])
        dcol_i, scol_i = w.sb("dcol_i", [PT, T], I32), w.sb("scol_i", [PT, T], I32)
        dcol = w.sb("dcol", [PT, T])
        junk = w.sb("junk", [PT, E])
        tri = w.sb("tri", [PT, PT])
        less, same, diag = w.sb("less", [PT, T]), w.sb("same", [PT, T]), w.sb("diag", [PT, T])
        before, rank = w.sb("before", [PT, T]), w.sb("rank", [PT, T])
        rank_i = w.sb("rank_i", [PT, T], I32)
        edge = w.sb("edge", [PT, T, 4])
        dsort = w.sb("dsort", [PT, T])
        absent = w.sb("absent", [PT, N // PT], I32)
        no_dst = w.sb("no_dst", [1, 2])
        inputs_in, tri_set, tri_done, cast = w.sem("inputs_in"), w.sem("tri_set"), w.sem("tri_done"), w.sem("cast")
        counted, counts_done, ranked = w.sem("counted"), w.sem("counts_done"), w.sem("ranked")
        scattered, filled, fills_out = w.sem("scattered"), w.sem("filled"), w.sem("fills_out")
        block = w.block()

        @block.sync
        def _(sp):
            sp.dma_start(row_i[:, :], arg["dst"].rearrange("(o e) -> o e", o=1).partition_broadcast(PT)).then_inc(inputs_in, 16)
            sp.dma_start(dcol_i[:, :], arg["dst"].rearrange("(t p) -> p t", p=PT)).then_inc(inputs_in, 16)
            sp.dma_start(scol_i[:, :], arg["src"].rearrange("(t p) -> p t", p=PT)).then_inc(inputs_in, 16)
            sp.wait_ge(filled, 2)
            sp.dma_start(k.slot_map[0:N, :].rearrange("(p q) o -> p (q o)", p=PT), absent[:, :]).then_inc(fills_out, 16)
            sp.dma_start(k.dst_sorted[E:E + 2, :].rearrange("(a e) o -> a (e o)", a=1), no_dst[:, :]).then_inc(fills_out, 16)
            sp.wait_ge(fills_out, 32)

        @block.gpsimd
        def _(pool):
            pool.memset(tri[:, :], 1.0).then_inc(tri_set, 1)
            pool.memset(absent[:, :], E).then_inc(filled, 1)
            pool.memset(no_dst[:, :], -1.0).then_inc(filled, 1)
            pool.wait_ge(tri_set, 1)
            pool.affine_select(out=tri[:, :], in_=tri[:, :], compare_op=ALU.is_gt, fill=0.0, base=0,
                               pattern=[[-1, PT]], channel_multiplier=1).then_inc(tri_done, 1)
            pool.wait_ge(ranked, 1)
            for t in range(T):
                at = bass.IndirectOffsetOnAxis(ap=rank_i[:, t:t + 1], axis=0)
                pool.indirect_dma_start(out=k.edges_sorted[:, :], out_offset=at, in_=edge[:, t, :], in_offset=None).then_inc(scattered, 16)
                pool.indirect_dma_start(out=k.dst_sorted[:, :], out_offset=at, in_=dsort[:, t:t + 1], in_offset=None).then_inc(scattered, 16)
            pool.wait_ge(scattered, 32 * T)

        @block.vector
        def _(dve):
            dve.wait_ge(inputs_in, 48)
            dve.tensor_copy(row[:, :], row_i[:, :]).then_inc(cast, 1)
            dve.tensor_copy(dcol[:, :], dcol_i[:, :]).then_inc(cast, 1)
            dve.tensor_copy(edge[:, :, 0], scol_i[:, :]).then_inc(cast, 1)
            dve.wait_ge(cast, 3)
            dve.tensor_copy(edge[:, :, 1], dcol[:, :]).then_inc(cast, 1)
            dve.tensor_copy(edge[:, :, 3], dcol[:, :]).then_inc(cast, 1)
            dve.tensor_copy(dsort[:, :], dcol[:, :]).then_inc(cast, 1)
            dve.memset(same[:, 0:1], 0.0).then_inc(counted, 1)
            dve.wait_ge(tri_done, 1)
            for t in range(T):
                if t:
                    dve.wait_ge(counted, 3 * t)
                dve.tensor_scalar(junk[:, :], row[:, :], dcol[:, t:t + 1], 0.0, ALU.is_lt, ALU.add,
                                  accum_out=less[:, t:t + 1]).then_inc(counted, 1)
                if t:
                    dve.wait_ge(counted, 3 * t + 1)
                    dve.tensor_scalar(junk[:, 0:t * PT], row[:, 0:t * PT], dcol[:, t:t + 1], 0.0, ALU.is_equal, ALU.add,
                                      accum_out=same[:, t:t + 1]).then_inc(counted, 1)
                dve.wait_ge(counted, 3 * t + 2)
                dve.scalar_tensor_tensor(junk[:, 0:PT], row[:, t * PT:(t + 1) * PT], dcol[:, t:t + 1], tri[:, :],
                                         ALU.is_equal, ALU.mult, accum_out=diag[:, t:t + 1]).then_inc(counted, 1)
            dve.wait_ge(counted, 3 * T)
            dve.tensor_tensor(before[:, :], same[:, :], diag[:, :], ALU.add).then_inc(counts_done, 1)
            dve.wait_ge(counts_done, 1)
            dve.tensor_tensor(rank[:, :], less[:, :], before[:, :], ALU.add).then_inc(counts_done, 1)
            dve.tensor_scalar(edge[:, :, 2], before[:, :], 1.0, None, ALU.add).then_inc(counts_done, 1)
            dve.wait_ge(counts_done, 3)
            dve.wait_ge(cast, 6)
            dve.tensor_copy(rank_i[:, :], rank[:, :]).then_inc(ranked, 1)


def build_slots(nc, k, arg, N, E):
    T = E // PT
    with Pass(nc, "slots") as w:
        cols = w.sb("cols", [PT, T, 4])
        after = w.sb("after", [PT, T])
        own = w.sb("own", [PT, T])
        own_i = w.sb("own_i", [PT, T], I32)
        is_last, inner, shift, target = w.sb("is_last", [PT, T]), w.sb("inner", [PT, T]), w.sb("shift", [PT, T]), w.sb("target", [PT, T])
        target_i = w.sb("target_i", [PT, T], I32)
        edges_in, own_done, step, target_ready = w.sem("edges_in"), w.sem("own_done"), w.sem("step"), w.sem("target_ready")
        scattered, slots_in = w.sem("scattered"), w.sem("slots_in")
        block = w.block()

        @block.sync
        def _(sp):
            sp.dma_start(cols[:, :, :], k.edges_sorted.rearrange("(t p) c -> p t c", p=PT)).then_inc(edges_in, 16)
            sp.dma_start(after[:, :], k.dst_sorted[1:E + 1, :].rearrange("(t p) o -> p (t o)", p=PT)).then_inc(edges_in, 16)
            sp.dma_start(k.drow[:, :], k.dst_sorted.rearrange("e o -> o e").partition_broadcast(P)).then_inc(edges_in, 16)
            sp.wait_ge(edges_in, 48)
            sp.wait_ge(scattered, 16 * T)
            sp.dma_start(k.slots[:, :, :], k.slot_map[0:N, :].rearrange("(g p j) o -> p g (j o)", p=PT, j=J)).then_inc(slots_in, 16)
            sp.wait_ge(slots_in, 16)

        @block.gpsimd
        def _(pool):
            pool.iota(own_i[:, :], pattern=[[PT, T]], base=0, channel_multiplier=1).then_inc(own_done, 1)
            pool.wait_ge(target_ready, 1)
            pool.wait_ge(own_done, 1)
            for t in range(T):
                pool.indirect_dma_start(out=k.slot_map[:, :], in_offset=None, in_=own_i[:, t:t + 1],
                                        out_offset=bass.IndirectOffsetOnAxis(ap=target_i[:, t:t + 1], axis=0)).then_inc(scattered, 16)
            pool.wait_ge(scattered, 16 * T)

        @block.vector
        def _(dve):
            dve.wait_ge(edges_in, 48)
            dve.wait_ge(own_done, 1)
            dve.tensor_copy(own[:, :], own_i[:, :]).then_inc(step, 1)
            dve.tensor_copy(k.src[:, :], cols[:, :, 0]).then_inc(step, 1)
            dve.tensor_copy(k.dst[:, :], cols[:, :, 1]).then_inc(step, 1)
            dve.reciprocal(k.rdeg[:, :], cols[:, :, 2]).then_inc(step, 1)
            dve.tensor_tensor(inner[:, :], cols[:, :, 1], after[:, :], ALU.is_equal).then_inc(step, 1)
            dve.wait_ge(step, 5)
            dve.tensor_scalar(is_last[:, :], inner[:, :], -1.0, 1.0, ALU.mult, ALU.add).then_inc(step, 1)
            dve.scalar_tensor_tensor(shift[:, :], k.dst[:, :], float(-N), own[:, :], ALU.add, ALU.subtract).then_inc(step, 1)
            dve.wait_ge(step, 7)
            dve.tensor_tensor(target[:, :], shift[:, :], is_last[:, :], ALU.mult).then_inc(step, 1)
            dve.wait_ge(step, 8)
            dve.scalar_tensor_tensor(shift[:, :], target[:, :], float(N), own[:, :], ALU.add, ALU.add).then_inc(step, 1)
            dve.wait_ge(step, 9)
            dve.tensor_copy(target_i[:, :], shift[:, :]).then_inc(target_ready, 1)


def build_pass_a(nc, k, arg, N, acc):
    G = N // GT
    with Pass(nc, "a") as w:
        gam = w.sb("gam", [P, 4])
        wt = Weights(w, [arg["L0_mix_Wk"], arg["L0_gnn_W_self"][0], arg["L0_mix_Wq"]],
                     [gam[:, 0:1], 1.0, gam[:, 2:3]])
        WK, WS, WQ = 0, 1, 2
        g_raw = w.sb("g_raw", [P, 2, 2 * P])
        g_hi, g_lo = w.sb("g_hi", [P, 2, 2 * P], F32R), w.sb("g_lo", [P, 2, 2 * P], F32R)
        x, xn = w.sb("x", [PT, J, D]), w.sb("xn", [PT, J, D])
        xs = [w.sb(f"xs{i}", [PT, J, D], F32R) for i in "hl"]
        xt = [w.sb(f"xt{i}", [P, C, GT], F32R) for i in "hl"]
        zt = [w.sb(f"zt{i}", [P, C, GT], F32R) for i in "hl"]
        ph = [w.sb(f"ph{i}", [PT, J, D], F32R) for i in "hl"]
        gz = w.sb("gz", [PT, 2, 2 * P])
        half = w.sb("half", [PT, 2, D])
        phk = w.sb("phk", [PT, 2, D])
        phq, pout = w.sb("phq", [PT, J, D]), w.sb("pout", [PT, J, D])
        stat, mv = w.sb("stat", [PT, J, 6]), w.sb("mv", [PT, J, 2])
        var, rstd = w.sb("var", [PT, J]), w.sb("rstd", [PT, J])
        zb_raw, zb = w.sb("zb_raw", [P, 2, C]), w.sb("zb", [P, 2, C])
        ring = [w.ps(f"ring{i}") for i in range(4)]
        k_full, p1_full, sk_full, q_full, t_full = (w.sem(n) for n in ("k_full", "p1_full", "sk_full", "q_full", "t_full"))
        small_in, g_zero, g_in, g_hi_done, g_lo_done = w.sem("small_in"), w.sem("g_zero"), w.sem("g_in"), w.sem("g_hi_done"), w.sem("g_lo_done")
        zb_done, kacc_zero = w.sem("zb_done"), w.sem("kacc_zero")
        x_in, stats, aggr, var_done, rstd_done, xn_done = (w.sem(n) for n in ("x_in", "stats", "aggr", "var_done", "rstd_done", "xn_done"))
        xs_hi, xs_lo, t_hi, t_done, k_hi, k_done, q_hi, q_done = (w.sem(n) for n in (
            "xs_hi", "xs_lo", "t_hi", "t_done", "k_hi", "k_done", "q_hi", "q_done"))
        gz_done, half_done, phi_done, ph_hi, ph_lo, kacc_done, acc_done, p1_done = (w.sem(n) for n in (
            "gz_done", "half_done", "phi_done", "ph_hi", "ph_lo", "kacc_done", "acc_done", "p1_done"))
        p_out = [w.sem(f"p_out{i}") for i in range(2)]
        q_out = [w.sem(f"q_out{i}") for i in range(2)]
        JK, JP, JSK, JQ, JT, JSQ = 0, 4, 8, 16, 20, 24

        def wait_emptied(pe, g, job):
            if isinstance(g, int) and g == 0 and job < JP:
                pe.wait_ge(t_done, job + 1)
                return
            if job < JP:
                g, job = g - 1, job + JSQ + 8
            if isinstance(g, int) and g == G - 1 and JSQ <= job < JSQ + 4:
                job -= 4
            last = job - 4
            if last >= JSQ:
                pe.wait_ge(half_done, 4 * J * g + 2 * J + last - JSQ + 1)
            elif last >= JT:
                pe.wait_ge(t_done, J * (g + 1) + last - JT + 1)
            elif last >= JQ:
                pe.wait_ge(q_done, C * g + last - JQ + 1)
            elif last >= JSK:
                pe.wait_ge(half_done, 4 * J * g + last - JSK + 1)
            elif last >= JP:
                pe.wait_ge(p1_done, J * g + last - JP + 1)
            else:
                pe.wait_ge(k_done, C * g + last + 1)

        def groups(eng, body):
            body(0)
            with eng.Fori(1, G - 1) as g:
                body(g)
            body(G - 1)

        def is_last(g):
            return isinstance(g, int) and g == G - 1

        block = w.block()

        @block.sync
        def _(sp):
            for i, name in enumerate(("gamma_k", "beta_k", "gamma_q", "beta_q")):
                sp.dma_start(gam[:, i:i + 1], arg["L0_mix_" + name].rearrange("(o n) -> o n", o=1).partition_broadcast(P)).then_inc(small_in, 16)
            for i, name in enumerate(("bk", "bq")):
                sp.dma_start(zb_raw[:, i, :], arg["L0_mix_" + name].rearrange("(c p) -> p c", p=P)).then_inc(small_in, 16)
            load_group(sp, x, arg["x"], 0, x_in)
            sp.wait_ge(g_zero, 1)
            for i, z in enumerate("kq"):
                for m in range(2):
                    for d in range(2):
                        sp.dma_start(g_raw[d * R:(d + 1) * R, i, m * P + d * R:m * P + (d + 1) * R],
                                     arg[f"L0_mix_{z}G{m + 1}"]).then_inc(g_in, 16)
            wt.load(sp)

            def body(g):
                if not is_last(g):
                    sp.wait_ge(xn_done, J * (g + 1))
                    alone(sp, w.sp_waited)
                    load_group(sp, x, arg["x"], g + 1, x_in)
                for i in range(2):
                    sp.wait_ge(p1_done, J * g + 2 * i + 2)
                    alone(sp, w.sp_waited)
                    store_pair(sp, k.ps[0], pout, g, 2 * i, p_out[i])
                for i in range(2):
                    sp.wait_ge(phi_done, 2 * J * g + J + 2 * i + 2)
                    alone(sp, w.sp_waited)
                    store_pair(sp, k.phi_q, phq, g, 2 * i, q_out[i])
            groups(sp, body)
            for i in range(2):
                sp.wait_ge(p_out[i], 32 * G)
                sp.wait_ge(q_out[i], 32 * G)

        @block.gpsimd
        def _(pool):
            pool.memset(g_raw[:, :, :], 0.0).then_inc(g_zero, 1)
            pool.memset(k.kacc[:, :], 0.0).then_inc(kacc_zero, 1)
            pool.wait_ge(kacc_zero, 1)
            def rstds(g):
                pool.wait_ge(aggr, J * (g + 1))
                alone(pool, w.pool_waited)
                pool.tensor_scalar(var[:, :], mv[:, :, 1], LN_EPS, None, ALU.add).then_inc(var_done, 1)
                pool.wait_ge(var_done, g + 1)
                pool.tensor_tensor(rstd[:, :], var[:, :], k.minus_half[0:PT, 0:J], ALU.pow).then_inc(rstd_done, 1)

            def body(g):
                for j in range(J):
                    pool.wait_ge(xn_done, J * g + j + 1)
                    need(pool, acc_done, J * (g - 1) + j + 1)
                    alone(pool, w.pool_waited)
                    pool.tensor_copy(xs[0][:, j, :], xn[:, j, :]).then_inc(xs_hi, 1)
                    pool.wait_ge(xs_hi, J * g + j + 1)
                    pool.tensor_tensor(xs[1][:, j, :], xn[:, j, :], xs[0][:, j, :].bitcast(F32), ALU.subtract).then_inc(xs_lo, 1)
                if not is_last(g):
                    rstds(g + 1)
                for j in range(J):
                    pool.wait_ge(phi_done, 2 * J * g + j + 1)
                    need(pool, acc_done, J * (g - 1) + j + 1)
                    alone(pool, w.pool_waited)
                    pool.tensor_copy(ph[0][:, j, :], phk[:, j % 2, :]).then_inc(ph_hi, 1)
                    pool.wait_ge(ph_hi, J * g + j + 1)
                    pool.tensor_tensor(ph[1][:, j, :], phk[:, j % 2, :], ph[0][:, j, :].bitcast(F32), ALU.subtract).then_inc(ph_lo, 1)
                    need(pool, kacc_done, J * g + j)
                    pool.tensor_tensor(k.kacc[:, :], k.kacc[:, :], phk[:, j % 2, :], ALU.add).then_inc(kacc_done, 1)
            rstds(0)
            groups(pool, body)

        @block.tensor
        def _(pe):
            def turn(g, at):
                for j in range(J):
                    if j == 0:
                        pe.wait_ge(xn_done, J * (g + 1))
                    if at is not None:
                        wait_emptied(pe, at, JT + j)
                    for c in range(C):
                        mm = pe.transpose(ring[j][:, c * PT:(c + 1) * PT], xn[:, j, c * P:(c + 1) * P], k.ident[0:PT, 0:PT])
                    mm.then_inc(t_full, 1)

            def project(g, job, i, filled):
                for m in range(C):
                    wait_emptied(pe, g, job + m)
                    for c in range(C):
                        mm = three(pe, ring[m][:, 0:GT], wt.hi[i][:, c, m * P:(m + 1) * P], wt.lo[i][:, c, m * P:(m + 1) * P],
                                   xt[0][:, c, :], xt[1][:, c, :], c == 0, c == C - 1)
                    mm.then_inc(filled, 1)

            def sketch(g, job, i):
                for j in range(J):
                    for b in range(2):
                        n = (2 * j + b) % 4
                        wait_emptied(pe, g, job + 2 * j + b)
                        for a in range(2):
                            c = 2 * b + a
                            mm = three(pe, ring[n][0:PT, a * 2 * P:(a + 1) * 2 * P], zt[0][:, c, j * PT:(j + 1) * PT],
                                       zt[1][:, c, j * PT:(j + 1) * PT], g_hi[:, i, :], g_lo[:, i, :], True, True)
                        mm.then_inc(sk_full, 1)

            def body(g):
                pe.wait_ge(t_done, J * (g + 1))
                if isinstance(g, int) and g == 0:
                    wt.wait(pe, WK)
                project(g, JK, WK, k_full)
                if isinstance(g, int) and g == 0:
                    wt.wait(pe, WS)
                for j in range(J):
                    wait_emptied(pe, g, JP + j)
                    for c in range(C):
                        mm = three(pe, ring[j][0:PT, :], xt[0][:, c, j * PT:(j + 1) * PT], xt[1][:, c, j * PT:(j + 1) * PT],
                                   wt.hi[WS][:, c, :], wt.lo[WS][:, c, :], c == 0, c == C - 1)
                    mm.then_inc(p1_full, 1)
                if isinstance(g, int) and g == 0:
                    pe.wait_ge(g_lo_done, 1)
                pe.wait_ge(k_done, C * (g + 1))
                sketch(g, JSK, 0)
                if isinstance(g, int) and g == 0:
                    wt.wait(pe, WQ)
                project(g, JQ, WQ, q_full)
                for j in range(J):
                    pe.wait_ge(ph_lo, J * g + j + 1)
                    pe.wait_ge(xs_lo, J * g + j + 1)
                    for c in range(C):
                        mm = three(pe, acc[c][:, :], ph[0][:, j, c * P:(c + 1) * P], ph[1][:, j, c * P:(c + 1) * P],
                                   xs[0][:, j, :], xs[1][:, j, :], isinstance(g, int) and g == 0 and j == 0,
                                   is_last(g) and j == J - 1)
                    mm.then_inc(acc_done, 1)
                if not is_last(g):
                    turn(g + 1, g)
                pe.wait_ge(q_done, C * (g + 1))
                sketch(g, JSQ, 1)
            turn(0, None)
            groups(pe, body)

        def sketch_at(g, q, j):
            return 2 * J * g + J * q + j

        @block.scalar
        def _(act):
            def turn(g):
                for j in range(J):
                    act.wait_ge(t_full, J * g + j + 1)
                    act.activation(xt[0][:, :, j * PT:(j + 1) * PT], ring[j][:, 0:GT].rearrange("p (c t) -> p c t", c=C),
                                   ACT.Copy).then_inc(t_hi, 1)

            def project(g, i, filled, done):
                for m in range(C):
                    act.wait_ge(filled, C * g + m + 1)
                    act.activation(zt[0][:, m, :], ring[m][:, 0:GT], ACT.Identity, bias=zb[:, i, m:m + 1]).then_inc(done, 1)

            def sketch(g, q):
                def square(j):
                    at = sketch_at(g, q, j)
                    act.wait_ge(half_done, 2 * at + 2)
                    if q:
                        if j % 2 == 0:
                            need(act, q_out[j // 2], 32 * g)
                        out = phq[:, j, :]
                    else:
                        need(act, kacc_done, J * g + j - 1)
                        out = phk[:, j % 2, :]
                    act.activation(out, half[:, j % 2, :], ACT.Square, scale=float(R) ** -0.5).then_inc(phi_done, 1)
                for j in range(J):
                    for b in range(2):
                        n = (2 * j + b) % 4
                        act.wait_ge(sk_full, 2 * sketch_at(g, q, j) + b + 1)
                        need(act, half_done, 2 * sketch_at(g, q, j) + b - 1)
                        act.activation(gz[:, b, :].rearrange("p (a r) -> p a r", a=2),
                                       ring[n][0:PT, :].rearrange("p (a m r) -> p a m r", a=2, m=2)[:, :, 0, :],
                                       ACT.Copy).then_inc(gz_done, 1)
                    if j:
                        square(j - 1)
                square(J - 1)

            def body(g):
                project(g, 0, k_full, k_hi)
                if isinstance(g, int) and g == 0:
                    wt.split_hi(act, WS)
                for j in range(J):
                    act.wait_ge(p1_full, J * g + j + 1)
                    if j % 2 == 0:
                        need(act, p_out[j // 2], 32 * g)
                    act.activation(pout[:, j, :], ring[j][0:PT, :], ACT.Copy).then_inc(p1_done, 1)
                if isinstance(g, int) and g == 0:
                    wt.split_hi(act, WQ)
                sketch(g, 0)
                project(g, 1, q_full, q_hi)
                if not is_last(g):
                    turn(g + 1)
                sketch(g, 1)
            act.wait_ge(small_in, 96)
            wt.split_hi(act, WK)
            act.wait_ge(g_in, 128)
            act.activation(g_hi[:, :, :], g_raw[:, :, :], ACT.Copy).then_inc(g_hi_done, 1)
            act.wait_ge(zb_done, 4)
            turn(0)
            groups(act, body)

        @block.vector
        def _(dve):
            def norm(g):
                dve.wait_ge(x_in, 32 * (g + 1))
                for j in range(J):
                    dve.bn_stats(stat[:, j, :], x[:, j, :]).then_inc(stats, 1)
                    if j:
                        dve.wait_ge(stats, J * g + j)
                        alone(dve, w.dve_waited)
                        dve.bn_aggr(mv[:, j - 1, :], stat[:, j - 1, :]).then_inc(aggr, 1)
                dve.wait_ge(stats, J * (g + 1))
                alone(dve, w.dve_waited)
                dve.bn_aggr(mv[:, J - 1, :], stat[:, J - 1, :]).then_inc(aggr, 1)
                dve.wait_ge(rstd_done, g + 1)
                need(dve, xs_lo, J * g)
                need(dve, t_hi, J * g)
                for j in range(J):
                    dve.tensor_scalar(xn[:, j, :], x[:, j, :], mv[:, j, 0:1], rstd[:, j:j + 1], ALU.subtract, ALU.mult).then_inc(xn_done, 1)

            def turn(g):
                for j in range(J):
                    dve.wait_ge(t_hi, J * g + j + 1)
                    dve.tensor_tensor(xt[1][:, :, j * PT:(j + 1) * PT], ring[j][:, 0:GT].rearrange("p (c t) -> p c t", c=C),
                                      xt[0][:, :, j * PT:(j + 1) * PT].bitcast(F32), ALU.subtract).then_inc(t_done, 1)

            def project(g, i, hi_done, done):
                for m in range(C):
                    dve.wait_ge(hi_done, C * g + m + 1)
                    dve.scalar_tensor_tensor(zt[1][:, m, :], ring[m][:, 0:GT], zb[:, i, m:m + 1], zt[0][:, m, :].bitcast(F32),
                                             ALU.add, ALU.subtract).then_inc(done, 1)

            def sketch(g, q):
                for j in range(J):
                    at = sketch_at(g, q, j)
                    for b in range(2):
                        n = (2 * j + b) % 4
                        dve.wait_ge(gz_done, 2 * at + b + 1)
                        if b == 0:
                            need(dve, phi_done, at - 1)
                        dve.tensor_tensor(half[:, j % 2, b * 2 * P:(b + 1) * 2 * P].rearrange("p (a r) -> p a r", a=2),
                                          ring[n][0:PT, :].rearrange("p (a m r) -> p a m r", a=2, m=2)[:, :, 1, :],
                                          gz[:, b, :].rearrange("p (a r) -> p a r", a=2), ALU.mult).then_inc(half_done, 1)

            def body(g):
                project(g, 0, k_hi, k_done)
                if isinstance(g, int) and g == 0:
                    wt.split_lo(dve, WS)
                if not is_last(g):
                    norm(g + 1)
                if isinstance(g, int) and g == 0:
                    wt.split_lo(dve, WQ)
                sketch(g, 0)
                project(g, 1, q_hi, q_done)
                if not is_last(g):
                    turn(g + 1)
                sketch(g, 1)
            dve.wait_ge(small_in, 96)
            for i in range(2):
                dve.tensor_scalar(zb[:, i, :], zb_raw[:, i, :], gam[:, 2 * i:2 * i + 1], gam[:, 2 * i + 1:2 * i + 2],
                                  ALU.mult, ALU.add).then_inc(zb_done, 2)
            wt.split_lo(dve, WK)
            dve.wait_ge(g_hi_done, 1)
            dve.tensor_tensor(g_lo[:, :, :], g_raw[:, :, :], g_hi[:, :, :].bitcast(F32), ALU.subtract).then_inc(g_lo_done, 1)
            norm(0)
            turn(0)
            groups(dve, body)


def build_neighbours(nc, k, arg, l, h_in, E):
    T = E // PT
    PE1 = PT + 1
    with Pass(nc, f"z{l}") as w:
        wt = Weights(w, [arg["L0_gnn_W_neigh"][l]])
        got = w.sb("got", [PT, 2, D])
        rows = w.sb("rows", [PT, 2, D]) if l == 0 else got
        split = [w.sb(f"split{i}", [PT, 2, D], F32R) for i in "hl"]
        index = w.sb("index", [PT, 2], I32)
        same = w.sb("same", [PT, 2, PE1], F32R)
        first_run = w.sb("first_run", [P, 2, PE1])
        agg = w.sb("agg", [P, 2, C, PE1])
        aggs = [w.sb(f"aggs{i}", [P, 2, C, PE1], F32R) for i in "hl"]
        z = w.sb("z", [PT, 2, D])
        stat, mv, var, rstd = w.sb("stat", [PT, 2, 6]), w.sb("mv", [PT, 2, 2]), w.sb("var", [PT, 2]), w.sb("rstd", [PT, 2])
        pagg = [w.ps(f"pagg{i}") for i in range(2)]
        pz = [w.ps(f"pz{i}") for i in range(2)]
        index_done, gathered = w.sem("index_done"), [w.sem(f"gathered{i}") for i in range(2)]
        stats, aggr, var_done, rstd_done, rows_done = (w.sem(n) for n in ("stats", "aggr", "var_done", "rstd_done", "rows_done"))
        split_hi, split_lo, same_done, first_done, sum_full, carry_zero, agg_done, agg_hi, agg_lo, z_full, z_done = (w.sem(n) for n in (
            "split_hi", "split_lo", "same_done", "first_done", "sum_full", "carry_zero", "agg_done", "agg_hi", "agg_lo", "z_full", "z_done"))
        z_out = [w.sem(f"z_out{i}") for i in range(2)]
        block = w.block()

        def pairs(eng, body):
            for t in range(2):
                body(t, t)
            if T > 4:
                with eng.Fori(1, T // 2 - 1) as u:
                    for r in range(2):
                        body(2 * u + r, r)
            for t in range(T - 2, T):
                body(t, t % 2)

        def slot_uses(t, r):
            return (t - r) // 2

        @block.sync
        def _(sp):
            wt.load(sp)

            def body(t, r):
                sp.wait_ge(z_done, t + 1)
                alone(sp, w.sp_waited)
                for a, b in ((0, PA), (PA, PT)):
                    sp.dma_start(k.z[bass.ds(t * PT + a, b - a), :], z[a:b, r, :]).then_inc(z_out[r], 16)
            pairs(sp, body)
            for r in range(2):
                sp.wait_ge(z_out[r], 16 * T)

        @block.gpsimd
        def _(pool):
            def gather(t, r):
                need(pool, rows_done if l == 0 else split_lo, t - 1)
                alone(pool, w.pool_waited)
                pool.tensor_copy(index[:, r:r + 1], k.src[:, bass.ds(t, 1)]).then_inc(index_done, 1)
                pool.wait_ge(index_done, t + 1)
                alone(pool, w.pool_waited)
                pool.indirect_dma_start(out=got[:, r, :], out_offset=None, in_=h_in[:, :],
                                        in_offset=bass.IndirectOffsetOnAxis(ap=index[:, r:r + 1], axis=0)).then_inc(gathered[r], 16)

            def work(t, r):
                if l == 0:
                    pool.wait_ge(aggr, t + 1)
                    alone(pool, w.pool_waited)
                    pool.tensor_scalar(var[:, r:r + 1], mv[:, r, 1:2], LN_EPS, None, ALU.add).then_inc(var_done, 1)
                    pool.wait_ge(var_done, t + 1)
                    pool.tensor_tensor(rstd[:, r:r + 1], var[:, r:r + 1], k.minus_half[0:PT, 0:1], ALU.pow).then_inc(rstd_done, 1)
                pool.wait_ge(split_hi, t + 1)
                need(pool, sum_full, t - 1)
                pool.tensor_tensor(split[1][:, r, :], rows[:, r, :], split[0][:, r, :].bitcast(F32), ALU.subtract).then_inc(split_lo, 1)
            gather(0, 0)
            gather(1, 1)

            def body(t, r):
                work(t, r)
                if not (isinstance(t, int) and t >= T - 2):
                    gather(t + 2, r)
            pairs(pool, body)

        @block.scalar
        def _(act):
            def body(t, r):
                if l == 0:
                    act.wait_ge(rows_done, t + 1)
                else:
                    act.wait_ge(gathered[r], 16 * (slot_uses(t, r) + 1))
                need(act, sum_full, t - 1)
                act.activation(split[0][:, r, :], rows[:, r, :], ACT.Copy).then_inc(split_hi, 1)
                act.wait_ge(agg_done, C * (t + 1))
                need(act, z_full, t - 1)
                act.activation(aggs[0][:, r, :, :], agg[:, r, :, :], ACT.Copy).then_inc(agg_hi, 1)
            wt.split_hi(act, 0)
            pairs(act, body)

        @block.tensor
        def _(pe):
            def body(t, r):
                pe.wait_ge(same_done, t + 1)
                pe.wait_ge(split_lo, t + 1)
                need(pe, agg_done, C * (t - 1))
                for c in range(C):
                    for i in range(2):
                        mm = pe.matmul(pagg[r][:, c * PE1:(c + 1) * PE1], split[i][:, r, c * P:(c + 1) * P], same[:, r, :],
                                       start=(i == 0), stop=(i == 1))
                mm.then_inc(sum_full, 1)

            def product(t, r):
                pe.wait_ge(agg_lo, t + 1)
                need(pe, z_done, t - 1)
                for c in range(C):
                    mm = three(pe, pz[r][0:PT, :], aggs[0][:, r, c, 0:PT], aggs[1][:, r, c, 0:PT], wt.hi[0][:, c, :], wt.lo[0][:, c, :],
                               c == 0, c == C - 1)
                mm.then_inc(z_full, 1)

            def both(t, r):
                if not (isinstance(t, int) and t == T - 1):
                    body(t + 1, 1 - r)
                product(t, r)
            body(0, 0)
            wt.wait(pe, 0)
            pairs(pe, both)

        @block.vector
        def _(dve):
            def rows_and_masks(t, r):
                if l == 0:
                    dve.wait_ge(gathered[r], 16 * (slot_uses(t, r) + 1))
                    dve.bn_stats(stat[:, r, :], got[:, r, :]).then_inc(stats, 1)
                    dve.wait_ge(stats, t + 1)
                    alone(dve, w.dve_waited)
                    dve.bn_aggr(mv[:, r, :], stat[:, r, :]).then_inc(aggr, 1)
                need(dve, sum_full, t - 1)
                dve.tensor_scalar(same[:, r, :], k.drow[0:PT, bass.ds(t * PT, PE1)], k.dst[:, bass.ds(t, 1)], None, ALU.is_equal).then_inc(same_done, 1)
                dve.tensor_scalar(first_run[:, r, :], k.drow[:, bass.ds(t * PT, PE1)], k.drow[:, bass.ds(t * PT, 1)], None, ALU.is_equal).then_inc(first_done, 1)
                if l == 0:
                    dve.wait_ge(rstd_done, t + 1)
                    need(dve, split_lo, t - 1)
                    dve.tensor_scalar(rows[:, r, :], got[:, r, :], mv[:, r, 0:1], rstd[:, r:r + 1], ALU.subtract, ALU.mult).then_inc(rows_done, 1)

            def sums(t, r):
                dve.wait_ge(sum_full, t + 1)
                dve.wait_ge(first_done, t + 1)
                need(dve, agg_done, C * t)
                need(dve, agg_lo, t - 1)
                for c in range(C):
                    dve.scalar_tensor_tensor(agg[:, r, c, :], first_run[:, r, :], agg[:, 1 - r, c, PT:PE1], pagg[r][:, c * PE1:(c + 1) * PE1],
                                             ALU.mult, ALU.add).then_inc(agg_done, 1)
                dve.wait_ge(agg_hi, t + 1)
                dve.tensor_tensor(aggs[1][:, r, :, :], agg[:, r, :, :], aggs[0][:, r, :, :].bitcast(F32), ALU.subtract).then_inc(agg_lo, 1)

            def finish(t, r):
                dve.wait_ge(z_full, t + 1)
                need(dve, z_out[r], 32 * slot_uses(t, r))
                dve.scalar_tensor_tensor(z[:, r, :], pz[r][0:PT, :], k.rdeg[:, bass.ds(t, 1)], k.bias[0:PT, l, :], ALU.mult, ALU.add).then_inc(z_done, 1)

            def body(t, r):
                if not (isinstance(t, int) and t == T - 1):
                    rows_and_masks(t + 1, 1 - r)
                    sums(t + 1, 1 - r)
                finish(t, r)
            dve.memset(agg[:, 1, :, :], 0.0).then_inc(carry_zero, 1)
            dve.wait_ge(carry_zero, 1)
            rows_and_masks(0, 0)
            wt.split_lo(dve, 0)
            sums(0, 0)
            pairs(dve, body)


def build_layer(nc, k, arg, l, N, E):
    G = N // GT
    NT = G * J
    AHEAD = 3
    with Pass(nc, f"l{l}") as w:
        wt = Weights(w, [arg["L0_gnn_W_self"][l]])
        pin = w.sb("pin", [PT, J, D])
        zin, index = w.sb("zin", [PT, J, D]), w.sb("index", [PT, J], I32)
        junk = w.sb("junk", [PT, D])
        ss, floor, rnorm = w.sb("ss", [PT, J]), w.sb("floor", [PT, J]), w.sb("rnorm", [PT, J])
        h = w.sb("h", [PT, J, D])
        ht = [w.sb(f"ht{i}", [P, 2, C, PT], F32R) for i in "hl"]
        pout = w.sb("pout", [PT, J, D])
        pt = [w.ps(f"pt{i}") for i in range(2)]
        pp = [w.ps(f"pp{i}") for i in range(2)]
        p_in = [w.sem(f"p_in{i}") for i in range(2)]
        z_in = [w.sem(f"z_in{i}") for i in range(J)]
        h_out = [w.sem(f"h_out{i}") for i in range(2)]
        p_out = [w.sem(f"p_out{i}") for i in range(2)]
        prefilled, index_done, sum_done, ss_done, floor_done, rnorm_done, h_done = (w.sem(n) for n in (
            "prefilled", "index_done", "sum_done", "ss_done", "floor_done", "rnorm_done", "h_done"))
        t_full, t_hi, t_lo, p_full, p_done = (w.sem(n) for n in ("t_full", "t_hi", "t_lo", "p_full", "p_done"))
        block = w.block()

        def group(n, j):
            return (n - j) // J

        def ok(n):
            return not isinstance(n, int) or 0 <= n < NT

        def steps(eng, body):
            tile_steps(eng, body, -AHEAD - 1, NT, G)

        @block.sync
        def _(sp):
            wt.load(sp)

            def body(s, j):
                n, jn = s + AHEAD, (j + AHEAD) % J
                if ok(n) and jn % 2 == 1:
                    sp.wait_ge(h_done, n + 1)
                    alone(sp, w.sp_waited)
                    store_pair(sp, k.hs[l], h, group(n, jn), jn - 1, h_out[jn // 2])
                    if ok(n + J):
                        load_pair(sp, pin, k.ps[l - 1], group(n, jn) + 1, jn - 1, p_in[jn // 2])
                if ok(s) and j % 2 == 1:
                    sp.wait_ge(p_done, s + 1)
                    alone(sp, w.sp_waited)
                    store_pair(sp, k.ps[l], pout, group(s, j), j - 1, p_out[j // 2])
            for i in range(2):
                load_pair(sp, pin, k.ps[l - 1], 0, 2 * i, p_in[i])
            steps(sp, body)
            for i in range(2):
                sp.wait_ge(h_out[i], 32 * G)
                sp.wait_ge(p_out[i], 32 * G)

        @block.gpsimd
        def _(pool):
            def gather(n, j):
                need(pool, sum_done, n - J + 1)
                alone(pool, w.pool_waited)
                pool.tensor_copy(zin[:, j, :], k.bias[0:PT, l - 1, :]).then_inc(prefilled, 1)
                pool.tensor_copy(index[:, j:j + 1], k.slots[:, :, :].rearrange("p g j -> p (g j)")[:, bass.ds(n, 1)]).then_inc(index_done, 1)
                pool.wait_ge(prefilled, n + 1)
                pool.wait_ge(index_done, n + 1)
                alone(pool, w.pool_waited)
                pool.indirect_dma_start(out=zin[:, j, :], out_offset=None, in_=k.z[:, :],
                                        in_offset=bass.IndirectOffsetOnAxis(ap=index[:, j:j + 1], axis=0),
                                        bounds_check=E - 1, oob_is_err=False).then_inc(z_in[j], 16)

            def body(s, j):
                n, jn = s + AHEAD, (j + AHEAD) % J
                if ok(n):
                    pool.wait_ge(ss_done, n + 1)
                    alone(pool, w.pool_waited)
                    pool.tensor_scalar(floor[:, jn:jn + 1], ss[:, jn:jn + 1], NORM_EPS2, None, ALU.max).then_inc(floor_done, 1)
                    pool.wait_ge(floor_done, n + 1)
                    pool.tensor_tensor(rnorm[:, jn:jn + 1], floor[:, jn:jn + 1], k.minus_half[0:PT, 0:1], ALU.pow).then_inc(rnorm_done, 1)
                if ok(n + 3):
                    gather(n + 3, (jn + 3) % J)
            for j in range(2):
                gather(j, j)
            steps(pool, body)

        @block.vector
        def _(dve):
            def body(s, j):
                m = s + 1
                if ok(m):
                    r = (j + 1) % 2
                    dve.wait_ge(t_hi, m + 1)
                    dve.tensor_tensor(ht[1][:, r, :, :].rearrange("p c t -> p (c t)"), pt[r][:, 0:GT],
                                      ht[0][:, r, :, :].rearrange("p c t -> p (c t)").bitcast(F32), ALU.subtract).then_inc(t_lo, 1)
                n, jn = s + AHEAD, (j + AHEAD) % J
                if ok(n):
                    dve.wait_ge(p_in[jn // 2], 32 * (group(n, jn) + 1))
                    dve.wait_ge(z_in[jn], 16 * (group(n, jn) + 1))
                    dve.tensor_tensor(pin[:, jn, :], pin[:, jn, :], zin[:, jn, :], ALU.add).then_inc(sum_done, 1)
                    dve.wait_ge(sum_done, n + 1)
                    dve.scalar_tensor_tensor(junk[:, :], pin[:, jn, :], 0.0, pin[:, jn, :], ALU.max, ALU.mult,
                                             accum_out=ss[:, jn:jn + 1]).then_inc(ss_done, 1)
            wt.split_lo(dve, 0)
            steps(dve, body)

        @block.scalar
        def _(act):
            def body(s, j):
                m = s + 1
                if ok(m):
                    r = (j + 1) % 2
                    act.wait_ge(t_full, m + 1)
                    need(act, p_full, m - 1)
                    act.activation(ht[0][:, r, :, :].rearrange("p c t -> p (c t)"), pt[r][:, 0:GT], ACT.Copy).then_inc(t_hi, 1)
                n, jn = s + AHEAD, (j + AHEAD) % J
                if ok(n):
                    act.wait_ge(rnorm_done, n + 1)
                    need(act, t_full, n - J + 1)
                    need(act, h_out[jn // 2], 32 * group(n, jn))
                    act.activation(h[:, jn, :], pin[:, jn, :], ACT.Relu, scale=rnorm[:, jn:jn + 1]).then_inc(h_done, 1)
                if ok(s):
                    act.wait_ge(p_full, s + 1)
                    need(act, p_out[j // 2], 32 * group(s, j))
                    act.activation(pout[:, j, :], pp[j % 2][0:PT, :], ACT.Copy).then_inc(p_done, 1)
            wt.split_hi(act, 0)
            steps(act, body)

        @block.tensor
        def _(pe):
            def body(s, j):
                m = s + 1
                if ok(m):
                    r, jm = (j + 1) % 2, (j + 1) % J
                    pe.wait_ge(h_done, m + 1)
                    need(pe, t_lo, m - 1)
                    for c in range(C):
                        mm = pe.transpose(pt[r][:, c * PT:(c + 1) * PT], h[:, jm, c * P:(c + 1) * P], k.ident[0:PT, 0:PT])
                    mm.then_inc(t_full, 1)
                if ok(s):
                    r = j % 2
                    pe.wait_ge(t_lo, s + 1)
                    need(pe, p_done, s - 1)
                    for c in range(C):
                        mm = three(pe, pp[r][0:PT, :], ht[0][:, r, c, :], ht[1][:, r, c, :], wt.hi[0][:, c, :], wt.lo[0][:, c, :], c == 0, c == C - 1)
                    mm.then_inc(p_full, 1)
            wt.wait(pe, 0)
            steps(pe, body)



def build_attention_matrix(nc, k, arg, acc, m_hi, m_lo):
    with Pass(nc, "m") as w:
        wv, wp = w.sb("wv", [P, C, D]), w.sb("wp", [P, C, D])
        bv = w.sb("bv", [P, C])
        a, at = w.sb("a", [P, C, D]), w.sb("at", [P, C, D])
        ksum = w.sb("ksum", [P, D])
        outer = w.sb("outer", [P, C, P])
        kv = w.sb("kv", [P, C, P])
        mf = w.sb("mf", [P, C, D])
        bank = [w.ps(f"bank{i}") for i in range(4)]
        loaded, a_done, sum_full, sum_done, t_full, t_done, zeroed, kv_full, outer_done, kv_done, m_full, m_done, hi_done, lo_done = (w.sem(n) for n in (
            "loaded", "a_done", "sum_full", "sum_done", "t_full", "t_done", "zeroed", "kv_full", "outer_done", "kv_done", "m_full",
            "m_done", "hi_done", "lo_done"))
        block = w.block()

        @block.sync
        def _(sp):
            sp.dma_start(wv[:, :, :], arg["L0_mix_Wv"].rearrange("(c p) n -> p c n", p=P)).then_inc(loaded, 16)
            sp.dma_start(wp[:, :, :], arg["L0_mix_Wp"].rearrange("(c p) n -> p c n", p=P)).then_inc(loaded, 16)
            sp.dma_start(bv[:, :], arg["L0_mix_bv"].rearrange("(c p) -> p c", p=P)).then_inc(loaded, 16)

        @block.gpsimd
        def _(pool):
            pool.memset(kv[:, :, :], 0.0).then_inc(zeroed, 1)

        @block.scalar
        def _(act):
            for c in range(C):
                act.activation(a[:, c, :], acc[c][:, :], ACT.Copy).then_inc(a_done, 1)
            for c in range(C):
                act.wait_ge(m_full, c + 1)
                act.activation(mf[:, c, :], bank[c][:, :], ACT.Copy).then_inc(m_done, 1)
                act.wait_ge(m_done, c + 1)
                act.activation(m_hi[:, c, :], mf[:, c, :], ACT.Copy).then_inc(hi_done, 1)

        @block.tensor
        def _(pe):
            pe.matmul(bank[0][:, :], k.ones[0:PT, :], k.kacc[:, :], start=True, stop=True).then_inc(sum_full, 1)
            pe.wait_ge(a_done, C)
            pe.wait_ge(sum_done, 1)
            for f in range(C):
                for c in range(C):
                    mm = pe.transpose(bank[f][:, c * P:(c + 1) * P], a[:, c, f * P:(f + 1) * P], k.ident[:, :])
                mm.then_inc(t_full, 1)
            pe.wait_ge(loaded, 48)
            pe.wait_ge(t_done, C)
            for c in range(C):
                for f in range(C):
                    mm = pe.matmul(bank[c][:, 0:P], wv[:, f, c * P:(c + 1) * P], at[:, f, c * P:(c + 1) * P], start=f == 0, stop=f == C - 1)
                mm.then_inc(kv_full, 1)
            for c in range(C):
                pe.wait_ge(kv_done, 2 * C)
                pe.matmul(bank[c][:, :], kv[:, c, :], wp[:, c, :], start=True, stop=True).then_inc(m_full, 1)

        @block.vector
        def _(dve):
            dve.wait_ge(sum_full, 1)
            dve.tensor_copy(ksum[:, :], bank[0][:, :]).then_inc(sum_done, 1)
            dve.wait_ge(sum_done, 1)
            dve.tensor_copy(k.ksum[:, :], ksum[0:PT, :]).then_inc(sum_done, 1)
            for f in range(C):
                dve.wait_ge(t_full, f + 1)
                dve.tensor_copy(at[:, f, :], bank[f][:, :]).then_inc(t_done, 1)
            dve.wait_ge(loaded, 48)
            for c in range(C):
                dve.tensor_scalar(outer[:, c, :], ksum[:, c * P:(c + 1) * P], bv[:, c:c + 1], None, ALU.mult).then_inc(outer_done, 1)
            dve.wait_ge(outer_done, C)
            dve.wait_ge(zeroed, 1)
            for c in range(C):
                dve.wait_ge(kv_full, c + 1)
                for b in range(2):
                    one = slice(b * R, (b + 1) * R)
                    dve.tensor_tensor(kv[one, c, one], bank[c][one, one], outer[one, c, one], ALU.add).then_inc(kv_done, 1)
            for c in range(C):
                dve.wait_ge(hi_done, c + 1)
                dve.tensor_tensor(m_lo[:, c, :], mf[:, c, :], m_hi[:, c, :].bitcast(F32), ALU.subtract).then_inc(lo_done, 1)


def build_pass_d(nc, k, arg, out, m_hi, m_lo, N, E):
    G = N // GT
    NT = G * J
    HC = 3
    FH = HC * P
    with Pass(nc, "d") as w:
        w1_raw, w2_raw = w.sb("w1_raw", [P, C, FG]), w.sb("w2_raw", [P, HC, D])
        w1 = [w.sb(f"w1{i}", [P, C, FG], F32R) for i in "hl"]
        w2 = [w.sb(f"w2{i}", [P, HC, D], F32R) for i in "hl"]
        b1 = w.sb("b1", [P, FG])
        e_base, expert = w.sb("e_base", [P, NE]), w.sb("expert", [PT, NE])
        expert_i = w.sb("expert_i", [PT, NE], I32)
        pin, qin, xin = (w.sb(n, [PT, J, D]) for n in ("pin", "qin", "xin"))
        zin, index = w.sb("zin", [PT, J, D]), w.sb("index", [PT, J], I32)
        junk = w.sb("junk", [PT, D])
        weighted = w.sb("weighted", [PT, D])
        ss, floor, rnorm = w.sb("ss", [PT, J]), w.sb("floor", [PT, J]), w.sb("rnorm", [PT, J])
        den, den_eps, rden = w.sb("den", [PT, H]), w.sb("den_eps", [PT, H]), w.sb("rden", [PT, H])
        h = w.sb("h", [PT, 2, D])
        qn = w.sb("qn", [PT, 2, D])
        x2 = w.sb("x2", [PT, J, D])
        qt = [w.sb(f"qt{i}", [P, 2, C * PT], F32R) for i in "hl"]
        stat, mv, var, rstd = w.sb("stat", [PT, 6]), w.sb("mv", [PT, 2, 2]), w.sb("var", [PT, 1]), w.sb("rstd", [PT, 1])
        y = w.sb("y", [PT, 2, D])
        yt = [w.sb(f"yt{i}", [P, C * PT], F32R) for i in "hl"]
        hid = w.sb("hid", [PT, 2, FG])
        act_hid = w.sb("act_hid", [PT, FE])
        top, top_i, top_f = w.sb("top", [PT, 8]), w.sb("top_i", [PT, 8], U32), w.sb("top_f", [PT, 2])
        gap, ex = w.sb("gap", [PT, NE]), w.sb("ex", [PT, NE])
        is_first, chosen, ex_sum, top_ex, top_sum, weight, rweight = (w.sb(n, [PT, m]) for n, m in (
            ("is_first", NE), ("chosen", NE), ("ex_sum", 1), ("top_ex", NE), ("top_sum", 1), ("weight", 1), ("rweight", 1)))
        sh = w.sb("sh", [PT, 2, FH])
        st = [w.sb(f"st{i}", [P, HC * PT], F32R) for i in "hl"]
        res = w.sb("res", [PT, J, D])
        b_ty, b_tq, b_mix, b_ts, b_w1, b_w2 = (w.ps(n) for n in ("b_ty", "b_tq", "b_mix", "b_ts", "b_w1", "b_w2"))
        zeroed, expert_set, w_in, e_in, w_hi, w_lo, expert_done = (w.sem(n) for n in ("zeroed", "expert_set", "w_in", "e_in", "w_hi", "w_lo", "expert_done"))
        p_in, q_in, x_in, o_out = ([w.sem(f"{n}{i}") for i in range(2)] for n in ("p_in", "q_in", "x_in", "o_out"))
        z_in = [w.sem(f"z_in{i}") for i in range(J)]
        prefilled, index_done, sum_done, ss_done, floor_done, rnorm_done, h_done, xb_done, xh_done = (w.sem(n) for n in (
            "prefilled", "index_done", "sum_done", "ss_done", "floor_done", "rnorm_done", "h_done", "xb_done", "xh_done"))
        weighted_done, den_done, rden_done, qn_done = (w.sem(n) for n in ("weighted_done", "den_done", "rden_done", "qn_done"))
        tq_full, tq_hi, tq_lo, mix_full, x2_done, stat_done, aggr, var_done, rstd_done, y_done = (w.sem(n) for n in (
            "tq_full", "tq_hi", "tq_lo", "mix_full", "x2_done", "stat_done", "aggr", "var_done", "rstd_done", "y_done"))
        ty_full, ty_hi, ty_lo, hid_full, hid_done, gelu_done, gap_done, ex_done = (w.sem(n) for n in (
            "ty_full", "ty_hi", "ty_lo", "hid_full", "hid_done", "gelu_done", "gap_done", "ex_done"))
        weight_done, score_done = w.sem("weight_done"), w.sem("score_done")
        top_step, sh_done, ts_full, ts_hi, ts_lo, out_full, res_done = (w.sem(n) for n in (
            "top_step", "sh_done", "ts_full", "ts_hi", "ts_lo", "out_full", "res_done"))
        block = w.block()

        def group(n, j):
            return (n - j) // J

        def ok(n):
            return not isinstance(n, int) or 0 <= n < NT

        def steps(eng, body):
            tile_steps(eng, body, -6, NT + 2, G)

        @block.sync
        def _(sp):
            sp.wait_ge(zeroed, 3)
            sp.dma_start(w1_raw[:, :, FE:FG], arg["L0_ffn_Wg"].rearrange("(c p) e -> p c e", p=P)).then_inc(w_in, 16)
            for e in range(NE):
                sp.dma_start(w1_raw[:, :, e * HE:(e + 1) * HE], arg["L0_ffn_W1"][e].rearrange("(c p) f -> p c f", p=P)).then_inc(w_in, 16)
            w2_rows = arg["L0_ffn_W2"].rearrange("e f n -> (e f) n")
            sp.dma_start(w2_raw[:, 0:2, :], w2_rows.rearrange("(c p) n -> p c n", p=P)).then_inc(w_in, 16)
            sp.dma_start(w2_raw[0:NE, 2, :], arg["L0_ffn_b2"]).then_inc(w_in, 16)
            sp.dma_start(b1[:, 0:FE], arg["L0_ffn_b1"].rearrange("(o e) f -> o (e f)", o=1).partition_broadcast(P)).then_inc(w_in, 16)
            for i in range(2):
                load_pair(sp, pin, k.ps[2], 0, 2 * i, p_in[i])
                load_pair(sp, qin, k.phi_q, 0, 2 * i, q_in[i])
                load_pair(sp, xin, arg["x"], 0, 2 * i, x_in[i])

            def body(s, j):
                n, jn = s + 2, (j + 2) % J
                if ok(n) and jn % 2 == 1 and ok(n + J):
                    i = jn // 2
                    sp.wait_ge(h_done, n + 1)
                    alone(sp, w.sp_waited)
                    load_pair(sp, pin, k.ps[2], group(n, jn) + 1, jn - 1, p_in[i])
                    sp.wait_ge(qn_done, n + 1)
                    alone(sp, w.sp_waited)
                    load_pair(sp, qin, k.phi_q, group(n, jn) + 1, jn - 1, q_in[i])
                    sp.wait_ge(xb_done, n + 1)
                    alone(sp, w.sp_waited)
                    load_pair(sp, xin, arg["x"], group(n, jn) + 1, jn - 1, x_in[i])
                n, jn = s - 2, (j - 2) % J
                if ok(n) and jn % 2 == 1:
                    sp.wait_ge(res_done, n + 1)
                    alone(sp, w.sp_waited)
                    store_pair(sp, out, res, group(n, jn), jn - 1, o_out[jn // 2])
            steps(sp, body)
            for i in range(2):
                sp.wait_ge(o_out[i], 32 * G)

        @block.gpsimd
        def _(pool):
            pool.memset(w2_raw[:, 2, :], 0.0).then_inc(zeroed, 1)
            pool.memset(b1[:, :], 0.0).then_inc(zeroed, 1)
            pool.memset(sh[:, :, :], 0.0).then_inc(zeroed, 1)
            pool.memset(e_base[:, :], float(np.float32(np.e))).then_inc(expert_set, 1)
            pool.iota(expert_i[:, :], pattern=[[1, NE]], base=0, channel_multiplier=0).then_inc(expert_set, 1)
            pool.wait_ge(expert_set, 2)

            def gather(n, j):
                need(pool, sum_done, n - J + 1)
                alone(pool, w.pool_waited)
                pool.tensor_copy(zin[:, j, :], k.bias[0:PT, 2, :]).then_inc(prefilled, 1)
                pool.tensor_copy(index[:, j:j + 1], k.slots[:, :, :].rearrange("p g j -> p (g j)")[:, bass.ds(n, 1)]).then_inc(index_done, 1)
                pool.wait_ge(prefilled, n + 1)
                pool.wait_ge(index_done, n + 1)
                alone(pool, w.pool_waited)
                pool.indirect_dma_start(out=zin[:, j, :], out_offset=None, in_=k.z[:, :],
                                        in_offset=bass.IndirectOffsetOnAxis(ap=index[:, j:j + 1], axis=0),
                                        bounds_check=E - 1, oob_is_err=False).then_inc(z_in[j], 16)

            def body(s, j):
                if ok(s + 4):
                    gather(s + 4, j)
                if ok(s):
                    pool.wait_ge(aggr, s + 1)
                    alone(pool, w.pool_waited)
                    pool.tensor_scalar(var[:, :], mv[:, j % 2, 1:2], LN_EPS, None, ALU.add).then_inc(var_done, 1)
                    pool.wait_ge(var_done, s + 1)
                    pool.tensor_tensor(rstd[:, :], var[:, :], k.minus_half[0:PT, 0:1], ALU.pow).then_inc(rstd_done, 1)
                n = s - 1
                if ok(n):
                    pool.wait_ge(gap_done, n + 1)
                    pool.tensor_tensor(ex[:, :], e_base[0:PT, :], gap[:, :], ALU.pow).then_inc(ex_done, 1)
                n, jn = s + 2, (j + 2) % J
                if ok(n):
                    pool.wait_ge(ss_done, n + 1)
                    alone(pool, w.pool_waited)
                    pool.tensor_scalar(floor[:, jn:jn + 1], ss[:, jn:jn + 1], NORM_EPS2, None, ALU.max).then_inc(floor_done, 1)
                    pool.wait_ge(floor_done, n + 1)
                    pool.tensor_tensor(rnorm[:, jn:jn + 1], floor[:, jn:jn + 1], k.minus_half[0:PT, 0:1], ALU.pow).then_inc(rnorm_done, 1)
                    pool.wait_ge(x_in[jn // 2], 32 * (group(n, jn) + 1))
                    need(pool, res_done, n - J + 1)
                    pool.tensor_tensor(x2[:, jn, :], xin[:, jn, :], k.bp[0:PT, :], ALU.add).then_inc(xb_done, 1)
                    pool.wait_ge(xb_done, n + 1)
                    pool.wait_ge(h_done, n + 1)
                    pool.tensor_tensor(x2[:, jn, :], x2[:, jn, :], h[:, jn % 2, :], ALU.add).then_inc(xh_done, 1)
            steps(pool, body)

        @block.tensor
        def _(pe):
            pe.wait_ge(w_lo, 2)

            def body(s, j):
                n = s - 1
                if ok(n):
                    pe.wait_ge(y_done, n + 1)
                    need(pe, ty_lo, n)
                    for c in range(C):
                        mm = pe.transpose(b_ty[:, c * PT:(c + 1) * PT], y[:, (j - 1) % 2, c * P:(c + 1) * P], k.ident[0:PT, 0:PT])
                    mm.then_inc(ty_full, 1)
                n = s + 1
                if ok(n):
                    pe.wait_ge(qn_done, n + 1)
                    need(pe, tq_lo, n)
                    for c in range(C):
                        mm = pe.transpose(b_tq[:, c * PT:(c + 1) * PT], qn[:, (j + 1) % 2, c * P:(c + 1) * P], k.ident[0:PT, 0:PT])
                    mm.then_inc(tq_full, 1)
                if ok(s):
                    pe.wait_ge(tq_lo, s + 1)
                    need(pe, x2_done, s)
                    for c in range(C):
                        part = slice(c * PT, (c + 1) * PT)
                        mm = three(pe, b_mix[0:PT, :], qt[0][:, j % 2, part], qt[1][:, j % 2, part], m_hi[:, c, :], m_lo[:, c, :], c == 0, c == C - 1)
                    mm.then_inc(mix_full, 1)
                n = s - 2
                if ok(n):
                    pe.wait_ge(sh_done, n + 1)
                    need(pe, ts_lo, n)
                    for c in range(HC):
                        mm = pe.transpose(b_ts[:, c * PT:(c + 1) * PT], sh[:, j % 2, c * P:(c + 1) * P], k.ident[0:PT, 0:PT])
                    mm.then_inc(ts_full, 1)
                n = s - 1
                if ok(n):
                    pe.wait_ge(ty_lo, n + 1)
                    need(pe, hid_done, n)
                    for c in range(C):
                        part = slice(c * PT, (c + 1) * PT)
                        mm = three(pe, b_w1[0:PT, 0:FG], yt[0][:, part], yt[1][:, part], w1[0][:, c, :], w1[1][:, c, :], c == 0, c == C - 1)
                    mm.then_inc(hid_full, 1)
                n = s - 2
                if ok(n):
                    pe.wait_ge(ts_lo, n + 1)
                    need(pe, res_done, n)
                    for c in range(HC):
                        part = slice(c * PT, (c + 1) * PT)
                        mm = three(pe, b_w2[0:PT, :], st[0][:, part], st[1][:, part], w2[0][:, c, :], w2[1][:, c, :], c == 0, c == HC - 1)
                    mm.then_inc(out_full, 1)
            steps(pe, body)

        @block.scalar
        def _(act):
            act.wait_ge(zeroed, 3)
            act.wait_ge(w_in, 16 * (NE + 4))
            act.activation(w1[0][:, :, :], w1_raw[:, :, :], ACT.Copy).then_inc(w_hi, 1)
            act.activation(w2[0][:, :, :], w2_raw[:, :, :], ACT.Copy).then_inc(w_hi, 1)

            def body(s, j):
                n = s - 1
                if ok(n):
                    act.wait_ge(ty_full, n + 1)
                    need(act, hid_full, n)
                    act.activation(yt[0][:, :], b_ty[:, 0:C * PT], ACT.Copy).then_inc(ty_hi, 1)
                n = s + 1
                if ok(n):
                    act.wait_ge(tq_full, n + 1)
                    need(act, mix_full, n - 1)
                    act.activation(qt[0][:, (j + 1) % 2, :], b_tq[:, 0:C * PT], ACT.Copy).then_inc(tq_hi, 1)
                n = s - 2
                if ok(n):
                    act.wait_ge(ts_full, n + 1)
                    need(act, out_full, n)
                    act.activation(st[0][:, :], b_ts[:, 0:HC * PT], ACT.Copy).then_inc(ts_hi, 1)
                n, jn = s + 2, (j + 2) % J
                if ok(n):
                    act.wait_ge(rnorm_done, n + 1)
                    need(act, xh_done, n - 1)
                    act.activation(h[:, jn % 2, :], pin[:, jn, :], ACT.Relu, scale=rnorm[:, jn:jn + 1]).then_inc(h_done, 1)
                n = s - 1
                if ok(n):
                    act.wait_ge(hid_done, n + 1)
                    need(act, sh_done, n)
                    act.activation(act_hid[:, :], hid[:, (j - 1) % 2, 0:FE], ACT.Gelu).then_inc(gelu_done, 1)
            steps(act, body)

        @block.vector
        def _(dve):
            dve.wait_ge(w_hi, 2)
            dve.tensor_tensor(w1[1][:, :, :], w1_raw[:, :, :], w1[0][:, :, :].bitcast(F32), ALU.subtract).then_inc(w_lo, 1)
            dve.tensor_tensor(w2[1][:, :, :], w2_raw[:, :, :], w2[0][:, :, :].bitcast(F32), ALU.subtract).then_inc(w_lo, 1)
            dve.wait_ge(expert_set, 2)
            dve.tensor_copy(expert[:, :], expert_i[:, :]).then_inc(expert_done, 1)
            dve.wait_ge(expert_done, 1)
            TOP = 7

            def body(s, j):
                n = s - 1
                if ok(n):
                    dve.wait_ge(ty_hi, n + 1)
                    dve.tensor_tensor(yt[1][:, :], b_ty[:, 0:C * PT], yt[0][:, :].bitcast(F32), ALU.subtract).then_inc(ty_lo, 1)
                n = s + 1
                if ok(n):
                    dve.wait_ge(tq_hi, n + 1)
                    dve.tensor_tensor(qt[1][:, (j + 1) % 2, :], b_tq[:, 0:C * PT], qt[0][:, (j + 1) % 2, :].bitcast(F32), ALU.subtract).then_inc(tq_lo, 1)
                n, jn = s + 2, (j + 2) % J
                if ok(n):
                    g = group(n, jn)
                    dve.wait_ge(p_in[jn // 2], 32 * (g + 1))
                    dve.wait_ge(z_in[jn], 16 * (g + 1))
                    dve.tensor_tensor(pin[:, jn, :], pin[:, jn, :], zin[:, jn, :], ALU.add).then_inc(sum_done, 1)
                    dve.wait_ge(q_in[jn // 2], 32 * (g + 1))
                    dve.tensor_tensor(weighted[:, :], qin[:, jn, :], k.ksum[:, :], ALU.mult).then_inc(weighted_done, 1)
                    dve.wait_ge(sum_done, n + 1)
                    dve.scalar_tensor_tensor(junk[:, :], pin[:, jn, :], 0.0, pin[:, jn, :], ALU.max, ALU.mult,
                                             accum_out=ss[:, jn:jn + 1]).then_inc(ss_done, 1)
                    dve.wait_ge(weighted_done, n + 1)
                    dve.tensor_reduce(den[:, :], weighted[:, :].rearrange("p (h r) -> p h r", h=H), AX.X, ALU.add).then_inc(den_done, 1)
                    dve.wait_ge(den_done, 2 * n + 1)
                    dve.tensor_scalar(den_eps[:, :], den[:, :], DEN_EPS, None, ALU.add).then_inc(den_done, 1)
                    dve.wait_ge(den_done, 2 * n + 2)
                    dve.reciprocal(rden[:, :], den_eps[:, :]).then_inc(rden_done, 1)
                if ok(s):
                    dve.wait_ge(mix_full, s + 1)
                    dve.wait_ge(xh_done, s + 1)
                    dve.tensor_tensor(x2[:, j, :], b_mix[0:PT, :], x2[:, j, :], ALU.add).then_inc(x2_done, 1)
                if ok(n):
                    dve.wait_ge(rden_done, n + 1)
                    need(dve, tq_full, n - 1)
                    dve.tensor_tensor(qn[:, jn % 2, :].rearrange("p (h r) -> p h r", h=H), qin[:, jn, :].rearrange("p (h r) -> p h r", h=H),
                                      rden[:, :].unsqueeze(2).broadcast_to([PT, H, R]), ALU.mult).then_inc(qn_done, 1)
                if ok(s):
                    dve.wait_ge(x2_done, s + 1)
                    dve.bn_stats(stat[:, :], x2[:, j, :]).then_inc(stat_done, 1)
                    dve.wait_ge(stat_done, s + 1)
                    alone(dve, w.dve_waited)
                    dve.bn_aggr(mv[:, j % 2, :], stat[:, :]).then_inc(aggr, 1)
                n = s - 2
                if ok(n):
                    dve.wait_ge(ts_hi, n + 1)
                    dve.tensor_tensor(st[1][:, :], b_ts[:, 0:HC * PT], st[0][:, :].bitcast(F32), ALU.subtract).then_inc(ts_lo, 1)
                n, r = s - 1, (j - 1) % 2
                if ok(n):
                    dve.wait_ge(hid_full, n + 1)
                    need(dve, gelu_done, n - 1)
                    dve.tensor_tensor(hid[:, r, :], b_w1[0:PT, 0:FG], b1[0:PT, :], ALU.add).then_inc(hid_done, 1)
                    dve.wait_ge(hid_done, n + 1)
                    alone(dve, w.dve_waited)
                    dve.max(top[:, :], hid[:, r, FE:FG]).then_inc(top_step, 1)
                    dve.wait_ge(top_step, TOP * n + 1)
                    need(dve, ex_done, n)
                    dve.tensor_scalar(gap[:, :], hid[:, r, FE:FG], top[:, 0:1], None, ALU.subtract).then_inc(gap_done, 1)
                    alone(dve, w.dve_waited)
                    dve.max_index(top_i[:, :], top[:, :], hid[:, r, FE:FG]).then_inc(top_step, 1)
                if ok(s):
                    dve.wait_ge(rstd_done, s + 1)
                    need(dve, ty_full, s - 1)
                    dve.tensor_scalar(y[:, j % 2, :], x2[:, j, :], mv[:, j % 2, 0:1], rstd[:, :], ALU.subtract, ALU.mult).then_inc(y_done, 1)
                if ok(n):
                    dve.wait_ge(top_step, TOP * n + 2)
                    dve.tensor_copy(top_f[:, :], top_i[:, 0:2]).then_inc(top_step, 1)
                    dve.wait_ge(ex_done, n + 1)
                    dve.tensor_reduce(ex_sum[:, :], ex[:, :], AX.X, ALU.add).then_inc(top_step, 1)
                    dve.wait_ge(top_step, TOP * n + 4)
                    dve.tensor_scalar(is_first[:, :], expert[:, :], top_f[:, 0:1], None, ALU.is_equal).then_inc(top_step, 1)
                    dve.wait_ge(top_step, TOP * n + 5)
                    dve.scalar_tensor_tensor(chosen[:, :], expert[:, :], top_f[:, 1:2], is_first[:, :], ALU.is_equal, ALU.add).then_inc(top_step, 1)
                    dve.wait_ge(top_step, TOP * n + 6)
                    dve.scalar_tensor_tensor(top_ex[:, :], ex[:, :], 1.0, chosen[:, :], ALU.mult, ALU.mult, accum_out=top_sum[:, :]).then_inc(top_step, 1)
                    dve.wait_ge(top_step, TOP * n + 7)
                    dve.scalar_tensor_tensor(weight[:, :], ex_sum[:, :], 1e-6, top_sum[:, :], ALU.mult, ALU.add).then_inc(weight_done, 1)
                    dve.wait_ge(weight_done, 2 * n + 1)
                    dve.reciprocal(rweight[:, :], weight[:, :]).then_inc(weight_done, 1)
                    dve.wait_ge(weight_done, 2 * n + 2)
                    need(dve, ts_full, n - 1)
                    dve.tensor_scalar(sh[:, r, FE:FG], top_ex[:, :], rweight[:, :], None, ALU.mult).then_inc(score_done, 1)
                    dve.wait_ge(score_done, n + 1)
                    dve.wait_ge(gelu_done, n + 1)
                    dve.tensor_tensor(sh[:, r, 0:FE].rearrange("p (e f) -> p e f", e=NE), act_hid[:, :].rearrange("p (e f) -> p e f", e=NE),
                                      sh[:, r, FE:FG].unsqueeze(2).broadcast_to([PT, NE, HE]), ALU.mult).then_inc(sh_done, 1)
                n, jn = s - 2, (j - 2) % J
                if ok(n):
                    dve.wait_ge(out_full, n + 1)
                    need(dve, o_out[jn // 2], 32 * group(n, jn))
                    dve.tensor_tensor(res[:, jn, :], b_w2[0:PT, :], x2[:, jn, :], ALU.add).then_inc(res_done, 1)
            steps(dve, body)


_INS = ["x", "src", "dst", "L0_gnn_W_self", "L0_gnn_W_neigh", "L0_gnn_b", "L0_mix_Wq", "L0_mix_bq", "L0_mix_Wk",
        "L0_mix_bk", "L0_mix_Wv", "L0_mix_bv", "L0_mix_Wp", "L0_mix_bp", "L0_mix_gamma_q", "L0_mix_beta_q",
        "L0_mix_gamma_k", "L0_mix_beta_k", "L0_mix_qG1", "L0_mix_qG2", "L0_mix_kG1", "L0_mix_kG2", "L0_ffn_Wg",
        "L0_ffn_W1", "L0_ffn_b1", "L0_ffn_W2", "L0_ffn_b2"]


class Kept:
    pass


def build(nc, arg, out):
    N = arg["x"].shape[0]
    E = arg["src"].shape[0]
    T = E // PT
    G = N // GT
    assert arg["x"].shape[1] == D and N % GT == 0 and E % (2 * PT) == 0 and G >= 6
    k = Kept()

    def dram(name, shape, dt=F32):
        return nc.dram_tensor("kept_" + name, shape, dt, kind="Internal").ap()

    k.ps = [dram(f"p{l}", [N, D]) for l in range(3)]
    k.hs = [arg["x"]] + [dram(f"h{l}", [N, D]) for l in (1, 2)]
    k.phi_q = dram("phi_q", [N, D])
    k.z = dram("z", [E, D])
    k.edges_sorted, k.dst_sorted = dram("edges_sorted", [E, 4]), dram("dst_sorted", [E + 2, 1])
    k.slot_map = dram("slot_map", [N + E, 1], I32)
    with ExitStack() as ctx:
        def sb(name, shape, dt=F32):
            return ctx.enter_context(nc.sbuf_tensor(name, shape, dt))

        k.ident, k.ones, k.minus_half = sb("ident", [P, P]), sb("ones", [P, P]), sb("minus_half", [P, 8])
        k.bias, k.bp = sb("bias", [P, 3, D]), sb("bp", [P, D])
        k.kacc = sb("kacc", [PT, D])
        k.src, k.dst, k.rdeg = sb("src", [PT, T], I32), sb("dst", [PT, T]), sb("rdeg", [PT, T])
        k.drow = sb("drow", [P, E + 2])
        k.slots = sb("slots", [PT, G, J], I32)
        k.ksum = sb("ksum", [PT, D])
        build_constants(nc, k, arg, N, E)
        build_sort(nc, k, arg, N, E)
        build_slots(nc, k, arg, N, E)
        with ExitStack() as held:
            acc = [held.enter_context(nc.psum_tensor(f"acc{c}", [P, 512], F32)) for c in range(C)]
            build_pass_a(nc, k, arg, N, acc)
            m_hi, m_lo = sb("m_hi", [P, C, D], F32R), sb("m_lo", [P, C, D], F32R)
            build_attention_matrix(nc, k, arg, acc, m_hi, m_lo)
        build_neighbours(nc, k, arg, 0, arg["x"], E)
        build_layer(nc, k, arg, 1, N, E)
        build_neighbours(nc, k, arg, 1, k.hs[1], E)
        build_layer(nc, k, arg, 2, N, E)
        build_neighbours(nc, k, arg, 2, k.hs[2], E)
        build_pass_d(nc, k, arg, out, m_hi, m_lo, N, E)


def kernel(**inputs):
    import concourse.bacc as bacc
    from concourse.bass_utils import run_bass_kernel_spmd as run

    nc = bacc.Bacc("TRN2", target_bir_lowering=False, num_devices=1)
    arrays, arg = {}, {}
    for name in _INS:
        a = np.ascontiguousarray(inputs[name])
        arrays["in_" + name] = a
        arg[name] = nc.dram_tensor("in_" + name, a.shape, mybir.dt.from_np(a.dtype), kind="ExternalInput").ap()
    out = nc.dram_tensor("out", inputs["x"].shape, F32, kind="ExternalOutput").ap()
    build(nc, arg, out)
    return run(nc, [arrays], core_ids=[0]).results[0]["out"]
```

```python
from contextlib import ExitStack

import numpy as np

import concourse.bass as bass
from concourse import mybir

F32 = mybir.dt.float32
F32R = mybir.dt.float32r
I32 = mybir.dt.int32
U32 = mybir.dt.uint32
ACT = mybir.ActivationFunctionType
ALU = mybir.AluOpType
AX = mybir.AxisListType

P = 128
PT = 125
J = 4
GT = PT * J
PA = 112
D = 512
C = D // P
H = 8
R = 64
NE = 8
HE = 32
FE = NE * HE
FG = FE + NE
LN_EPS = 1e-5
NORM_EPS2 = 1e-24
DEN_EPS = 1e-6


def need(eng, sem, value):
    if isinstance(value, int) and value <= 0:
        return
    eng.wait_ge(sem, value)


def alone(eng, waited):
    eng.sem_inc(waited, 1)


def tile_steps(eng, body, first, end, groups, peeled=2):
    for s in range(first, peeled * J):
        body(s, s % J)
    with eng.Fori(peeled, groups - peeled) as g:
        for j in range(J):
            body(g * J + j, j)
    for s in range((groups - peeled) * J, end):
        body(s, s % J)


def slot2(j):
    return j % 2


def three(pe, out, a_hi, a_lo, b_hi, b_lo, first, last):
    pe.matmul(out, a_hi, b_hi, start=first, stop=False)
    pe.matmul(out, a_hi, b_lo, start=False, stop=False)
    return pe.matmul(out, a_lo, b_hi, start=False, stop=last)


def rows_of(dram, g, j0, j1):
    v = dram.rearrange("(q j) d -> q j d", j=J)
    for a, b in ((0, PA), (PA, PT)):
        yield slice(a, b), v[bass.ds(g * PT + a, b - a), j0:j1, :]


def load_group(eng, tile, dram, g, sem):
    for part, view in rows_of(dram, g, 0, J):
        eng.dma_start(tile[part, :, :], view).then_inc(sem, 16)


def load_pair(eng, tile, dram, g, j0, sem):
    for part, view in rows_of(dram, g, j0, j0 + 2):
        eng.dma_start(tile[part, j0:j0 + 2, :], view).then_inc(sem, 16)


def store_pair(eng, dram, tile, g, j0, sem):
    for part, view in rows_of(dram, g, j0, j0 + 2):
        eng.dma_start(view, tile[part, j0:j0 + 2, :]).then_inc(sem, 16)


class Pass:

    def __init__(self, nc, name):
        self.nc, self.name, self.ctx, self.sems = nc, name, ExitStack(), []

    def __enter__(self):
        self.ctx.__enter__()
        self.ctx.enter_context(self.nc.allow_non_contiguous_dma(reason="a few thousand words of indices and biases"))
        self.pool_waited, self.dve_waited, self.sp_waited = (self.sem(n) for n in ("pool_waited", "dve_waited", "sp_waited"))
        return self

    def __exit__(self, *a):
        self.ctx.__exit__(*a)
        self.nc.clear_and_free_semaphores(self.sems)
        self.nc.all_engine_barrier()

    def sb(self, name, shape, dt=F32):
        return self.ctx.enter_context(self.nc.sbuf_tensor(f"{self.name}_{name}", shape, dt))

    def ps(self, name, shape=(P, 512), dt=F32):
        return self.ctx.enter_context(self.nc.psum_tensor(f"{self.name}_{name}", list(shape), dt))

    def sem(self, name):
        self.sems.append(self.nc.alloc_semaphore(f"{self.name}_{name}"))
        return self.sems[-1]

    def block(self):
        return self.ctx.enter_context(self.nc.Block())


class Weights:

    def __init__(self, w, drams, scales=None, raw=None):
        self.drams, self.scales = drams, scales or [1.0] * len(drams)
        self.hi = [w.sb(f"w{i}_hi", [P, C, D], F32R) for i in range(len(drams))]
        self.lo = [w.sb(f"w{i}_lo", [P, C, D], F32R) for i in range(len(drams))]
        self.raw = [w.sb(f"w_raw{i}", [P, C, D]) for i in range(min(2, len(drams)))]
        self.loaded = [w.sem(f"w_loaded{i}") for i in range(len(self.raw))]
        self.hi_done, self.lo_done = w.sem("w_hi_done"), w.sem("w_lo_done")

    def load(self, sp):
        for i, dram in enumerate(self.drams):
            if i >= 2:
                sp.wait_ge(self.lo_done, i - 1)
            sp.dma_start(self.raw[i % 2][:, :, :], dram.rearrange("(c p) n -> p c n", p=P)).then_inc(self.loaded[i % 2], 16)

    def split_hi(self, act, i):
        act.wait_ge(self.loaded[i % 2], 16 * (i // 2 + 1))
        act.activation(self.hi[i][:, :, :], self.raw[i % 2][:, :, :], ACT.Identity, scale=self.scales[i]).then_inc(self.hi_done, 1)

    def split_lo(self, dve, i):
        dve.wait_ge(self.hi_done, i + 1)
        dve.scalar_tensor_tensor(self.lo[i][:, :, :], self.raw[i % 2][:, :, :], self.scales[i],
                                 self.hi[i][:, :, :].bitcast(F32), ALU.mult, ALU.subtract).then_inc(self.lo_done, 1)

    def wait(self, pe, i):
        pe.wait_ge(self.lo_done, i + 1)


def build_constants(nc, k, arg, N, E):
    with Pass(nc, "const") as w:
        ones_set, id_done, rows_in = w.sem("ones_set"), w.sem("id_done"), w.sem("rows_in")
        block = w.block()

        @block.sync
        def _(sp):
            for l in range(3):
                sp.dma_start(k.bias[:, l, :], arg["L0_gnn_b"][l:l + 1, :].partition_broadcast(P)).then_inc(rows_in, 16)
            sp.dma_start(k.bp[:, :], arg["L0_mix_bp"].rearrange("(o n) -> o n", o=1).partition_broadcast(P)).then_inc(rows_in, 16)
            sp.wait_ge(rows_in, 64)

        @block.gpsimd
        def _(pool):
            pool.memset(k.ident[:, :], 1.0).then_inc(ones_set, 1)
            pool.memset(k.ones[:, :], 1.0).then_inc(ones_set, 1)
            pool.memset(k.minus_half[:, :], -0.5).then_inc(ones_set, 1)
            pool.wait_ge(ones_set, 3)
            pool.affine_select(out=k.ident[:, :], in_=k.ident[:, :], compare_op=ALU.is_equal, fill=0.0, base=0,
                               pattern=[[1, P]], channel_multiplier=-1).then_inc(id_done, 1)
            pool.wait_ge(id_done, 1)


def build_sort(nc, k, arg, N, E):
    T = E // PT
    with Pass(nc, "sort") as w:
        row_i, row = w.sb("row_i", [PT, E], I32), w.sb("row", [PT, E])
        dcol_i, scol_i = w.sb("dcol_i", [PT, T], I32), w.sb("scol_i", [PT, T], I32)
        dcol = w.sb("dcol", [PT, T])
        junk = w.sb("junk", [PT, E])
        tri = w.sb("tri", [PT, PT])
        less, same, diag = w.sb("less", [PT, T]), w.sb("same", [PT, T]), w.sb("diag", [PT, T])
        before, rank = w.sb("before", [PT, T]), w.sb("rank", [PT, T])
        rank_i = w.sb("rank_i", [PT, T], I32)
        edge = w.sb("edge", [PT, T, 4])
        dsort = w.sb("dsort", [PT, T])
        absent = w.sb("absent", [PT, N // PT], I32)
        no_dst = w.sb("no_dst", [1, 2])
        inputs_in, tri_set, tri_done, cast = w.sem("inputs_in"), w.sem("tri_set"), w.sem("tri_done"), w.sem("cast")
        counted, counts_done, ranked = w.sem("counted"), w.sem("counts_done"), w.sem("ranked")
        scattered, filled, fills_out = w.sem("scattered"), w.sem("filled"), w.sem("fills_out")
        block = w.block()

        @block.sync
        def _(sp):
            sp.dma_start(row_i[:, :], arg["dst"].rearrange("(o e) -> o e", o=1).partition_broadcast(PT)).then_inc(inputs_in, 16)
            sp.dma_start(dcol_i[:, :], arg["dst"].rearrange("(t p) -> p t", p=PT)).then_inc(inputs_in, 16)
            sp.dma_start(scol_i[:, :], arg["src"].rearrange("(t p) -> p t", p=PT)).then_inc(inputs_in, 16)
            sp.wait_ge(filled, 2)
            sp.dma_start(k.slot_map[0:N, :].rearrange("(p q) o -> p (q o)", p=PT), absent[:, :]).then_inc(fills_out, 16)
            sp.dma_start(k.dst_sorted[E:E + 2, :].rearrange("(a e) o -> a (e o)", a=1), no_dst[:, :]).then_inc(fills_out, 16)
            sp.wait_ge(fills_out, 32)

        @block.gpsimd
        def _(pool):
            pool.memset(tri[:, :], 1.0).then_inc(tri_set, 1)
            pool.memset(absent[:, :], E).then_inc(filled, 1)
            pool.memset(no_dst[:, :], -1.0).then_inc(filled, 1)
            pool.wait_ge(tri_set, 1)
            pool.affine_select(out=tri[:, :], in_=tri[:, :], compare_op=ALU.is_gt, fill=0.0, base=0,
                               pattern=[[-1, PT]], channel_multiplier=1).then_inc(tri_done, 1)
            pool.wait_ge(ranked, 1)
            for t in range(T):
                at = bass.IndirectOffsetOnAxis(ap=rank_i[:, t:t + 1], axis=0)
                pool.indirect_dma_start(out=k.edges_sorted[:, :], out_offset=at, in_=edge[:, t, :], in_offset=None).then_inc(scattered, 16)
                pool.indirect_dma_start(out=k.dst_sorted[:, :], out_offset=at, in_=dsort[:, t:t + 1], in_offset=None).then_inc(scattered, 16)
            pool.wait_ge(scattered, 32 * T)

        @block.vector
        def _(dve):
            dve.wait_ge(inputs_in, 48)
            dve.tensor_copy(row[:, :], row_i[:, :]).then_inc(cast, 1)
            dve.tensor_copy(dcol[:, :], dcol_i[:, :]).then_inc(cast, 1)
            dve.tensor_copy(edge[:, :, 0], scol_i[:, :]).then_inc(cast, 1)
            dve.wait_ge(cast, 3)
            dve.tensor_copy(edge[:, :, 1], dcol[:, :]).then_inc(cast, 1)
            dve.tensor_copy(edge[:, :, 3], dcol[:, :]).then_inc(cast, 1)
            dve.tensor_copy(dsort[:, :], dcol[:, :]).then_inc(cast, 1)
            dve.memset(same[:, 0:1], 0.0).then_inc(counted, 1)
            dve.wait_ge(tri_done, 1)
            for t in range(T):
                if t:
                    dve.wait_ge(counted, 3 * t)
                dve.tensor_scalar(junk[:, :], row[:, :], dcol[:, t:t + 1], 0.0, ALU.is_lt, ALU.add,
                                  accum_out=less[:, t:t + 1]).then_inc(counted, 1)
                if t:
                    dve.wait_ge(counted, 3 * t + 1)
                    dve.tensor_scalar(junk[:, 0:t * PT], row[:, 0:t * PT], dcol[:, t:t + 1], 0.0, ALU.is_equal, ALU.add,
                                      accum_out=same[:, t:t + 1]).then_inc(counted, 1)
                dve.wait_ge(counted, 3 * t + 2)
                dve.scalar_tensor_tensor(junk[:, 0:PT], row[:, t * PT:(t + 1) * PT], dcol[:, t:t + 1], tri[:, :],
                                         ALU.is_equal, ALU.mult, accum_out=diag[:, t:t + 1]).then_inc(counted, 1)
            dve.wait_ge(counted, 3 * T)
            dve.tensor_tensor(before[:, :], same[:, :], diag[:, :], ALU.add).then_inc(counts_done, 1)
            dve.wait_ge(counts_done, 1)
            dve.tensor_tensor(rank[:, :], less[:, :], before[:, :], ALU.add).then_inc(counts_done, 1)
            dve.tensor_scalar(edge[:, :, 2], before[:, :], 1.0, None, ALU.add).then_inc(counts_done, 1)
            dve.wait_ge(counts_done, 3)
            dve.wait_ge(cast, 6)
            dve.tensor_copy(rank_i[:, :], rank[:, :]).then_inc(ranked, 1)


def build_slots(nc, k, arg, N, E):
    T = E // PT
    with Pass(nc, "slots") as w:
        cols = w.sb("cols", [PT, T, 4])
        after = w.sb("after", [PT, T])
        own = w.sb("own", [PT, T])
        own_i = w.sb("own_i", [PT, T], I32)
        is_last, inner, shift, target = w.sb("is_last", [PT, T]), w.sb("inner", [PT, T]), w.sb("shift", [PT, T]), w.sb("target", [PT, T])
        target_i = w.sb("target_i", [PT, T], I32)
        edges_in, own_done, step, target_ready = w.sem("edges_in"), w.sem("own_done"), w.sem("step"), w.sem("target_ready")
        scattered, slots_in = w.sem("scattered"), w.sem("slots_in")
        block = w.block()

        @block.sync
        def _(sp):
            sp.dma_start(cols[:, :, :], k.edges_sorted.rearrange("(t p) c -> p t c", p=PT)).then_inc(edges_in, 16)
            sp.dma_start(after[:, :], k.dst_sorted[1:E + 1, :].rearrange("(t p) o -> p (t o)", p=PT)).then_inc(edges_in, 16)
            sp.dma_start(k.drow[:, :], k.dst_sorted.rearrange("e o -> o e").partition_broadcast(P)).then_inc(edges_in, 16)
            sp.wait_ge(edges_in, 48)
            sp.wait_ge(scattered, 16 * T)
            sp.dma_start(k.slots[:, :, :], k.slot_map[0:N, :].rearrange("(g p j) o -> p g (j o)", p=PT, j=J)).then_inc(slots_in, 16)
            sp.wait_ge(slots_in, 16)

        @block.gpsimd
        def _(pool):
            pool.iota(own_i[:, :], pattern=[[PT, T]], base=0, channel_multiplier=1).then_inc(own_done, 1)
            pool.wait_ge(target_ready, 1)
            pool.wait_ge(own_done, 1)
            for t in range(T):
                pool.indirect_dma_start(out=k.slot_map[:, :], in_offset=None, in_=own_i[:, t:t + 1],
                                        out_offset=bass.IndirectOffsetOnAxis(ap=target_i[:, t:t + 1], axis=0)).then_inc(scattered, 16)
            pool.wait_ge(scattered, 16 * T)

        @block.vector
        def _(dve):
            dve.wait_ge(edges_in, 48)
            dve.wait_ge(own_done, 1)
            dve.tensor_copy(own[:, :], own_i[:, :]).then_inc(step, 1)
            dve.tensor_copy(k.src[:, :], cols[:, :, 0]).then_inc(step, 1)
            dve.tensor_copy(k.dst[:, :], cols[:, :, 1]).then_inc(step, 1)
            dve.reciprocal(k.rdeg[:, :], cols[:, :, 2]).then_inc(step, 1)
            dve.tensor_tensor(inner[:, :], cols[:, :, 1], after[:, :], ALU.is_equal).then_inc(step, 1)
            dve.wait_ge(step, 5)
            dve.tensor_scalar(is_last[:, :], inner[:, :], -1.0, 1.0, ALU.mult, ALU.add).then_inc(step, 1)
            dve.scalar_tensor_tensor(shift[:, :], k.dst[:, :], float(-N), own[:, :], ALU.add, ALU.subtract).then_inc(step, 1)
            dve.wait_ge(step, 7)
            dve.tensor_tensor(target[:, :], shift[:, :], is_last[:, :], ALU.mult).then_inc(step, 1)
            dve.wait_ge(step, 8)
            dve.scalar_tensor_tensor(shift[:, :], target[:, :], float(N), own[:, :], ALU.add, ALU.add).then_inc(step, 1)
            dve.wait_ge(step, 9)
            dve.tensor_copy(target_i[:, :], shift[:, :]).then_inc(target_ready, 1)


def build_pass_a(nc, k, arg, N, acc):
    G = N // GT
    with Pass(nc, "a") as w:
        gam = w.sb("gam", [P, 4])
        wt = Weights(w, [arg["L0_mix_Wk"], arg["L0_gnn_W_self"][0], arg["L0_mix_Wq"]],
                     [gam[:, 0:1], 1.0, gam[:, 2:3]])
        WK, WS, WQ = 0, 1, 2
        g_raw = w.sb("g_raw", [P, 2, 2 * P])
        g_hi, g_lo = w.sb("g_hi", [P, 2, 2 * P], F32R), w.sb("g_lo", [P, 2, 2 * P], F32R)
        x, xn = w.sb("x", [PT, J, D]), w.sb("xn", [PT, J, D])
        xs = [w.sb(f"xs{i}", [PT, J, D], F32R) for i in "hl"]
        xt = [w.sb(f"xt{i}", [P, C, GT], F32R) for i in "hl"]
        zt = [w.sb(f"zt{i}", [P, C, GT], F32R) for i in "hl"]
        ph = [w.sb(f"ph{i}", [PT, J, D], F32R) for i in "hl"]
        gz = w.sb("gz", [PT, 2, 2 * P])
        half = w.sb("half", [PT, 2, D])
        phk = w.sb("phk", [PT, 2, D])
        phq, pout = w.sb("phq", [PT, J, D]), w.sb("pout", [PT, J, D])
        stat, mv = w.sb("stat", [PT, J, 6]), w.sb("mv", [PT, J, 2])
        var, rstd = w.sb("var", [PT, J]), w.sb("rstd", [PT, J])
        zb_raw, zb = w.sb("zb_raw", [P, 2, C]), w.sb("zb", [P, 2, C])
        ring = [w.ps(f"ring{i}") for i in range(4)]
        k_full, p1_full, sk_full, q_full, t_full = (w.sem(n) for n in ("k_full", "p1_full", "sk_full", "q_full", "t_full"))
        small_in, g_zero, g_in, g_hi_done, g_lo_done = w.sem("small_in"), w.sem("g_zero"), w.sem("g_in"), w.sem("g_hi_done"), w.sem("g_lo_done")
        zb_done, kacc_zero = w.sem("zb_done"), w.sem("kacc_zero")
        x_in, stats, aggr, var_done, rstd_done, xn_done = (w.sem(n) for n in ("x_in", "stats", "aggr", "var_done", "rstd_done", "xn_done"))
        xs_hi, xs_lo, t_hi, t_done, k_hi, k_done, q_hi, q_done = (w.sem(n) for n in (
            "xs_hi", "xs_lo", "t_hi", "t_done", "k_hi", "k_done", "q_hi", "q_done"))
        gz_done, half_done, phi_done, ph_hi, ph_lo, kacc_done, acc_done, p1_done = (w.sem(n) for n in (
            "gz_done", "half_done", "phi_done", "ph_hi", "ph_lo", "kacc_done", "acc_done", "p1_done"))
        xn_out = w.sem("xn_out")
        p_out = [w.sem(f"p_out{i}") for i in range(2)]
        q_out = [w.sem(f"q_out{i}") for i in range(2)]
        JK, JP, JSK, JQ, JT, JSQ = 0, 4, 8, 16, 20, 24

        def wait_emptied(pe, g, job):
            if isinstance(g, int) and g == 0 and job < JP:
                pe.wait_ge(t_done, job + 1)
                return
            if job < JP:
                g, job = g - 1, job + JSQ + 8
            if isinstance(g, int) and g == G - 1 and JSQ <= job < JSQ + 4:
                job -= 4
            last = job - 4
            if last >= JSQ:
                pe.wait_ge(half_done, 4 * J * g + 2 * J + last - JSQ + 1)
            elif last >= JT:
                pe.wait_ge(t_done, J * (g + 1) + last - JT + 1)
            elif last >= JQ:
                pe.wait_ge(q_done, C * g + last - JQ + 1)
            elif last >= JSK:
                pe.wait_ge(half_done, 4 * J * g + last - JSK + 1)
            elif last >= JP:
                pe.wait_ge(p1_done, J * g + last - JP + 1)
            else:
                pe.wait_ge(k_done, C * g + last + 1)

        def groups(eng, body):
            body(0)
            with eng.Fori(1, G - 1) as g:
                body(g)
            body(G - 1)

        def is_last(g):
            return isinstance(g, int) and g == G - 1

        block = w.block()

        @block.sync
        def _(sp):
            for i, name in enumerate(("gamma_k", "beta_k", "gamma_q", "beta_q")):
                sp.dma_start(gam[:, i:i + 1], arg["L0_mix_" + name].rearrange("(o n) -> o n", o=1).partition_broadcast(P)).then_inc(small_in, 16)
            for i, name in enumerate(("bk", "bq")):
                sp.dma_start(zb_raw[:, i, :], arg["L0_mix_" + name].rearrange("(c p) -> p c", p=P)).then_inc(small_in, 16)
            load_group(sp, x, arg["x"], 0, x_in)
            sp.wait_ge(g_zero, 1)
            for i, z in enumerate("kq"):
                for m in range(2):
                    for d in range(2):
                        sp.dma_start(g_raw[d * R:(d + 1) * R, i, m * P + d * R:m * P + (d + 1) * R],
                                     arg[f"L0_mix_{z}G{m + 1}"]).then_inc(g_in, 16)
            wt.load(sp)

            def body(g):
                sp.wait_ge(xn_done, J * (g + 1))
                alone(sp, w.sp_waited)
                if not is_last(g):
                    load_group(sp, x, arg["x"], g + 1, x_in)
                for i in range(2):
                    store_pair(sp, k.hs[0], xn, g, 2 * i, xn_out)
                for i in range(2):
                    sp.wait_ge(p1_done, J * g + 2 * i + 2)
                    alone(sp, w.sp_waited)
                    store_pair(sp, k.ps[0], pout, g, 2 * i, p_out[i])
                for i in range(2):
                    sp.wait_ge(phi_done, 2 * J * g + J + 2 * i + 2)
                    alone(sp, w.sp_waited)
                    store_pair(sp, k.phi_q, phq, g, 2 * i, q_out[i])
            groups(sp, body)
            sp.wait_ge(xn_out, 64 * G)
            for i in range(2):
                sp.wait_ge(p_out[i], 32 * G)
                sp.wait_ge(q_out[i], 32 * G)

        @block.gpsimd
        def _(pool):
            pool.memset(g_raw[:, :, :], 0.0).then_inc(g_zero, 1)
            pool.memset(k.kacc[:, :], 0.0).then_inc(kacc_zero, 1)
            pool.wait_ge(kacc_zero, 1)
            def rstds(g):
                pool.wait_ge(aggr, J * (g + 1))
                alone(pool, w.pool_waited)
                pool.tensor_scalar(var[:, :], mv[:, :, 1], LN_EPS, None, ALU.add).then_inc(var_done, 1)
                pool.wait_ge(var_done, g + 1)
                pool.tensor_tensor(rstd[:, :], var[:, :], k.minus_half[0:PT, 0:J], ALU.pow).then_inc(rstd_done, 1)

            def body(g):
                for j in range(J):
                    pool.wait_ge(xn_done, J * g + j + 1)
                    need(pool, acc_done, J * (g - 1) + j + 1)
                    alone(pool, w.pool_waited)
                    pool.tensor_copy(xs[0][:, j, :], xn[:, j, :]).then_inc(xs_hi, 1)
                    pool.wait_ge(xs_hi, J * g + j + 1)
                    pool.tensor_tensor(xs[1][:, j, :], xn[:, j, :], xs[0][:, j, :].bitcast(F32), ALU.subtract).then_inc(xs_lo, 1)
                if not is_last(g):
                    rstds(g + 1)
                for j in range(J):
                    pool.wait_ge(phi_done, 2 * J * g + j + 1)
                    need(pool, acc_done, J * (g - 1) + j + 1)
                    alone(pool, w.pool_waited)
                    pool.tensor_copy(ph[0][:, j, :], phk[:, j % 2, :]).then_inc(ph_hi, 1)
                    pool.wait_ge(ph_hi, J * g + j + 1)
                    pool.tensor_tensor(ph[1][:, j, :], phk[:, j % 2, :], ph[0][:, j, :].bitcast(F32), ALU.subtract).then_inc(ph_lo, 1)
                    need(pool, kacc_done, J * g + j)
                    pool.tensor_tensor(k.kacc[:, :], k.kacc[:, :], phk[:, j % 2, :], ALU.add).then_inc(kacc_done, 1)
            rstds(0)
            groups(pool, body)

        @block.tensor
        def _(pe):
            def turn(g, at):
                for j in range(J):
                    if j == 0:
                        pe.wait_ge(xn_done, J * (g + 1))
                    if at is not None:
                        wait_emptied(pe, at, JT + j)
                    for c in range(C):
                        mm = pe.transpose(ring[j][:, c * PT:(c + 1) * PT], xn[:, j, c * P:(c + 1) * P], k.ident[0:PT, 0:PT])
                    mm.then_inc(t_full, 1)

            def project(g, job, i, filled):
                for m in range(C):
                    wait_emptied(pe, g, job + m)
                    for c in range(C):
                        mm = three(pe, ring[m][:, 0:GT], wt.hi[i][:, c, m * P:(m + 1) * P], wt.lo[i][:, c, m * P:(m + 1) * P],
                                   xt[0][:, c, :], xt[1][:, c, :], c == 0, c == C - 1)
                    mm.then_inc(filled, 1)

            def sketch(g, job, i):
                for j in range(J):
                    for b in range(2):
                        n = (2 * j + b) % 4
                        wait_emptied(pe, g, job + 2 * j + b)
                        for a in range(2):
                            c = 2 * b + a
                            mm = three(pe, ring[n][0:PT, a * 2 * P:(a + 1) * 2 * P], zt[0][:, c, j * PT:(j + 1) * PT],
                                       zt[1][:, c, j * PT:(j + 1) * PT], g_hi[:, i, :], g_lo[:, i, :], True, True)
                        mm.then_inc(sk_full, 1)

            def body(g):
                pe.wait_ge(t_done, J * (g + 1))
                if isinstance(g, int) and g == 0:
                    wt.wait(pe, WK)
                project(g, JK, WK, k_full)
                if isinstance(g, int) and g == 0:
                    wt.wait(pe, WS)
                for j in range(J):
                    wait_emptied(pe, g, JP + j)
                    for c in range(C):
                        mm = three(pe, ring[j][0:PT, :], xt[0][:, c, j * PT:(j + 1) * PT], xt[1][:, c, j * PT:(j + 1) * PT],
                                   wt.hi[WS][:, c, :], wt.lo[WS][:, c, :], c == 0, c == C - 1)
                    mm.then_inc(p1_full, 1)
                if isinstance(g, int) and g == 0:
                    pe.wait_ge(g_lo_done, 1)
                pe.wait_ge(k_done, C * (g + 1))
                sketch(g, JSK, 0)
                if isinstance(g, int) and g == 0:
                    wt.wait(pe, WQ)
                project(g, JQ, WQ, q_full)
                for j in range(J):
                    pe.wait_ge(ph_lo, J * g + j + 1)
                    pe.wait_ge(xs_lo, J * g + j + 1)
                    for c in range(C):
                        mm = three(pe, acc[c][:, :], ph[0][:, j, c * P:(c + 1) * P], ph[1][:, j, c * P:(c + 1) * P],
                                   xs[0][:, j, :], xs[1][:, j, :], isinstance(g, int) and g == 0 and j == 0,
                                   is_last(g) and j == J - 1)
                    mm.then_inc(acc_done, 1)
                if not is_last(g):
                    turn(g + 1, g)
                pe.wait_ge(q_done, C * (g + 1))
                sketch(g, JSQ, 1)
            turn(0, None)
            groups(pe, body)

        def sketch_at(g, q, j):
            return 2 * J * g + J * q + j

        @block.scalar
        def _(act):
            def turn(g):
                for j in range(J):
                    act.wait_ge(t_full, J * g + j + 1)
                    act.activation(xt[0][:, :, j * PT:(j + 1) * PT], ring[j][:, 0:GT].rearrange("p (c t) -> p c t", c=C),
                                   ACT.Copy).then_inc(t_hi, 1)

            def project(g, i, filled, done):
                for m in range(C):
                    act.wait_ge(filled, C * g + m + 1)
                    act.activation(zt[0][:, m, :], ring[m][:, 0:GT], ACT.Identity, bias=zb[:, i, m:m + 1]).then_inc(done, 1)

            def sketch(g, q):
                def square(j):
                    at = sketch_at(g, q, j)
                    act.wait_ge(half_done, 2 * at + 2)
                    if q:
                        if j % 2 == 0:
                            need(act, q_out[j // 2], 32 * g)
                        out = phq[:, j, :]
                    else:
                        need(act, kacc_done, J * g + j - 1)
                        out = phk[:, j % 2, :]
                    act.activation(out, half[:, j % 2, :], ACT.Square, scale=float(R) ** -0.5).then_inc(phi_done, 1)
                for j in range(J):
                    for b in range(2):
                        n = (2 * j + b) % 4
                        act.wait_ge(sk_full, 2 * sketch_at(g, q, j) + b + 1)
                        need(act, half_done, 2 * sketch_at(g, q, j) + b - 1)
                        act.activation(gz[:, b, :].rearrange("p (a r) -> p a r", a=2),
                                       ring[n][0:PT, :].rearrange("p (a m r) -> p a m r", a=2, m=2)[:, :, 0, :],
                                       ACT.Copy).then_inc(gz_done, 1)
                    if j:
                        square(j - 1)
                square(J - 1)

            def body(g):
                project(g, 0, k_full, k_hi)
                if isinstance(g, int) and g == 0:
                    wt.split_hi(act, WS)
                for j in range(J):
                    act.wait_ge(p1_full, J * g + j + 1)
                    if j % 2 == 0:
                        need(act, p_out[j // 2], 32 * g)
                    act.activation(pout[:, j, :], ring[j][0:PT, :], ACT.Copy).then_inc(p1_done, 1)
                if isinstance(g, int) and g == 0:
                    wt.split_hi(act, WQ)
                sketch(g, 0)
                project(g, 1, q_full, q_hi)
                if not is_last(g):
                    turn(g + 1)
                sketch(g, 1)
            act.wait_ge(small_in, 96)
            wt.split_hi(act, WK)
            act.wait_ge(g_in, 128)
            act.activation(g_hi[:, :, :], g_raw[:, :, :], ACT.Copy).then_inc(g_hi_done, 1)
            act.wait_ge(zb_done, 4)
            turn(0)
            groups(act, body)

        @block.vector
        def _(dve):
            def norm(g):
                dve.wait_ge(x_in, 32 * (g + 1))
                for j in range(J):
                    dve.bn_stats(stat[:, j, :], x[:, j, :]).then_inc(stats, 1)
                    if j:
                        dve.wait_ge(stats, J * g + j)
                        alone(dve, w.dve_waited)
                        dve.bn_aggr(mv[:, j - 1, :], stat[:, j - 1, :]).then_inc(aggr, 1)
                dve.wait_ge(stats, J * (g + 1))
                alone(dve, w.dve_waited)
                dve.bn_aggr(mv[:, J - 1, :], stat[:, J - 1, :]).then_inc(aggr, 1)
                dve.wait_ge(rstd_done, g + 1)
                need(dve, xn_out, 64 * g)
                need(dve, xs_lo, J * g)
                need(dve, t_hi, J * g)
                for j in range(J):
                    dve.tensor_scalar(xn[:, j, :], x[:, j, :], mv[:, j, 0:1], rstd[:, j:j + 1], ALU.subtract, ALU.mult).then_inc(xn_done, 1)

            def turn(g):
                for j in range(J):
                    dve.wait_ge(t_hi, J * g + j + 1)
                    dve.tensor_tensor(xt[1][:, :, j * PT:(j + 1) * PT], ring[j][:, 0:GT].rearrange("p (c t) -> p c t", c=C),
                                      xt[0][:, :, j * PT:(j + 1) * PT].bitcast(F32), ALU.subtract).then_inc(t_done, 1)

            def project(g, i, hi_done, done):
                for m in range(C):
                    dve.wait_ge(hi_done, C * g + m + 1)
                    dve.scalar_tensor_tensor(zt[1][:, m, :], ring[m][:, 0:GT], zb[:, i, m:m + 1], zt[0][:, m, :].bitcast(F32),
                                             ALU.add, ALU.subtract).then_inc(done, 1)

            def sketch(g, q):
                for j in range(J):
                    at = sketch_at(g, q, j)
                    for b in range(2):
                        n = (2 * j + b) % 4
                        dve.wait_ge(gz_done, 2 * at + b + 1)
                        if b == 0:
                            need(dve, phi_done, at - 1)
                        dve.tensor_tensor(half[:, j % 2, b * 2 * P:(b + 1) * 2 * P].rearrange("p (a r) -> p a r", a=2),
                                          ring[n][0:PT, :].rearrange("p (a m r) -> p a m r", a=2, m=2)[:, :, 1, :],
                                          gz[:, b, :].rearrange("p (a r) -> p a r", a=2), ALU.mult).then_inc(half_done, 1)

            def body(g):
                project(g, 0, k_hi, k_done)
                if isinstance(g, int) and g == 0:
                    wt.split_lo(dve, WS)
                if not is_last(g):
                    norm(g + 1)
                if isinstance(g, int) and g == 0:
                    wt.split_lo(dve, WQ)
                sketch(g, 0)
                project(g, 1, q_hi, q_done)
                if not is_last(g):
                    turn(g + 1)
                sketch(g, 1)
            dve.wait_ge(small_in, 96)
            for i in range(2):
                dve.tensor_scalar(zb[:, i, :], zb_raw[:, i, :], gam[:, 2 * i:2 * i + 1], gam[:, 2 * i + 1:2 * i + 2],
                                  ALU.mult, ALU.add).then_inc(zb_done, 2)
            wt.split_lo(dve, WK)
            dve.wait_ge(g_hi_done, 1)
            dve.tensor_tensor(g_lo[:, :, :], g_raw[:, :, :], g_hi[:, :, :].bitcast(F32), ALU.subtract).then_inc(g_lo_done, 1)
            norm(0)
            turn(0)
            groups(dve, body)


def build_neighbours(nc, k, arg, l, E):
    T = E // PT
    PE1 = PT + 1
    with Pass(nc, f"z{l}") as w:
        wt = Weights(w, [arg["L0_gnn_W_neigh"][l]])
        got, index = w.sb("got", [PT, J, D]), w.sb("index", [PT, J], I32)
        split = [w.sb(f"split{i}", [PT, 2, D], F32R) for i in "hl"]
        same = w.sb("same", [PT, 2, PE1], F32R)
        first_run = w.sb("first_run", [P, 2, PE1])
        agg = w.sb("agg", [P, 2, C, PE1])
        aggs = [w.sb(f"aggs{i}", [P, 2, C, PE1], F32R) for i in "hl"]
        z = w.sb("z", [PT, 2, D])
        pagg = [w.ps(f"pagg{i}") for i in range(2)]
        pz = [w.ps(f"pz{i}") for i in range(2)]
        index_done, gathered = w.sem("index_done"), [w.sem(f"gathered{i}") for i in range(J)]
        split_hi, split_lo, same_done, first_done, sum_full, carry_zero, agg_done, agg_hi, agg_lo, z_full, z_done = (w.sem(n) for n in (
            "split_hi", "split_lo", "same_done", "first_done", "sum_full", "carry_zero", "agg_done", "agg_hi", "agg_lo", "z_full", "z_done"))
        z_out = [w.sem(f"z_out{i}") for i in range(2)]
        block = w.block()

        def ok(n):
            return not isinstance(n, int) or 0 <= n < T

        def steps(eng, body):
            tile_steps(eng, body, -J, T, T // J, 1)

        @block.sync
        def _(sp):
            wt.load(sp)

            def body(s, j):
                if ok(s):
                    sp.wait_ge(z_done, s + 1)
                    alone(sp, w.sp_waited)
                    for a, b in ((0, PA), (PA, PT)):
                        sp.dma_start(k.z[bass.ds(s * PT + a, b - a), :], z[a:b, j % 2, :]).then_inc(z_out[j % 2], 16)
            steps(sp, body)
            for r in range(2):
                sp.wait_ge(z_out[r], 16 * T)

        @block.gpsimd
        def _(pool):
            def body(s, j):
                n, jn = s + 2, (j + 2) % J
                if ok(n):
                    pool.wait_ge(split_hi, n + 1)
                    need(pool, sum_full, n - 1)
                    pool.tensor_tensor(split[1][:, j % 2, :], got[:, jn, :], split[0][:, j % 2, :].bitcast(F32), ALU.subtract).then_inc(split_lo, 1)
                n = s + J
                if ok(n):
                    need(pool, split_lo, n - J + 1)
                    alone(pool, w.pool_waited)
                    pool.tensor_copy(index[:, j:j + 1], k.src[:, bass.ds(n, 1)]).then_inc(index_done, 1)
                    pool.wait_ge(index_done, n + 1)
                    alone(pool, w.pool_waited)
                    pool.indirect_dma_start(out=got[:, j, :], out_offset=None, in_=k.hs[l][:, :],
                                            in_offset=bass.IndirectOffsetOnAxis(ap=index[:, j:j + 1], axis=0)).then_inc(gathered[j], 16)
            steps(pool, body)

        @block.scalar
        def _(act):
            def body(s, j):
                n, jn = s + 2, (j + 2) % J
                if ok(n):
                    act.wait_ge(gathered[jn], 16 * ((n - jn) // J + 1))
                    need(act, sum_full, n - 1)
                    act.activation(split[0][:, j % 2, :], got[:, jn, :], ACT.Copy).then_inc(split_hi, 1)
                if isinstance(s, int) and s == -2:
                    wt.split_hi(act, 0)
                n, r = s + 1, slot2(j + 1)
                if ok(n):
                    act.wait_ge(agg_done, C * (n + 1))
                    need(act, z_full, n - 1)
                    act.activation(aggs[0][:, r, :, :], agg[:, r, :, :], ACT.Copy).then_inc(agg_hi, 1)
            steps(act, body)

        @block.tensor
        def _(pe):
            def body(s, j):
                n, r = s + 1, slot2(j + 1)
                if ok(n):
                    pe.wait_ge(same_done, n + 1)
                    pe.wait_ge(split_lo, n + 1)
                    need(pe, agg_done, C * (n - 1))
                    for c in range(C):
                        for i in range(2):
                            mm = pe.matmul(pagg[r][:, c * PE1:(c + 1) * PE1], split[i][:, r, c * P:(c + 1) * P], same[:, r, :],
                                           start=(i == 0), stop=(i == 1))
                    mm.then_inc(sum_full, 1)
                if isinstance(s, int) and s == 0:
                    wt.wait(pe, 0)
                r = j % 2
                if ok(s):
                    pe.wait_ge(agg_lo, s + 1)
                    need(pe, z_done, s - 1)
                    for c in range(C):
                        mm = three(pe, pz[r][0:PT, :], aggs[0][:, r, c, 0:PT], aggs[1][:, r, c, 0:PT], wt.hi[0][:, c, :], wt.lo[0][:, c, :],
                                   c == 0, c == C - 1)
                    mm.then_inc(z_full, 1)
            steps(pe, body)

        @block.vector
        def _(dve):
            def body(s, j):
                n, r = s + 1, slot2(j + 1)
                if ok(n):
                    dve.wait_ge(sum_full, n + 1)
                    dve.wait_ge(first_done, n + 1)
                    need(dve, agg_done, C * n)
                    need(dve, agg_lo, n - 1)
                    for c in range(C):
                        dve.scalar_tensor_tensor(agg[:, r, c, :], first_run[:, r, :], agg[:, 1 - r, c, PT:PE1], pagg[r][:, c * PE1:(c + 1) * PE1],
                                                 ALU.mult, ALU.add).then_inc(agg_done, 1)
                if isinstance(s, int) and s == -1:
                    wt.split_lo(dve, 0)
                m, q = s + 2, j % 2
                if ok(m):
                    need(dve, agg_done, C * (m - 1))
                    need(dve, sum_full, m - 1)
                    dve.tensor_scalar(same[:, q, :], k.drow[0:PT, bass.ds(m * PT, PE1)], k.dst[:, bass.ds(m, 1)], None, ALU.is_equal).then_inc(same_done, 1)
                    dve.tensor_scalar(first_run[:, q, :], k.drow[:, bass.ds(m * PT, PE1)], k.drow[:, bass.ds(m * PT, 1)], None, ALU.is_equal).then_inc(first_done, 1)
                if ok(n):
                    dve.wait_ge(agg_hi, n + 1)
                    dve.tensor_tensor(aggs[1][:, r, :, :], agg[:, r, :, :], aggs[0][:, r, :, :].bitcast(F32), ALU.subtract).then_inc(agg_lo, 1)
                if ok(s):
                    dve.wait_ge(z_full, s + 1)
                    need(dve, z_out[q], 32 * ((s - q) // 2))
                    dve.scalar_tensor_tensor(z[:, q, :], pz[q][0:PT, :], k.rdeg[:, bass.ds(s, 1)], k.bias[0:PT, l, :], ALU.mult, ALU.add).then_inc(z_done, 1)
            dve.memset(agg[:, 1, :, :], 0.0).then_inc(carry_zero, 1)
            dve.wait_ge(carry_zero, 1)
            steps(dve, body)


def build_layer(nc, k, arg, l, N, E):
    G = N // GT
    NT = G * J
    SUM, NORM = 3, 2
    with Pass(nc, f"l{l}") as w:
        wt = Weights(w, [arg["L0_gnn_W_self"][l]])
        pin, rows = w.sb("pin", [PT, J, D]), w.sb("rows", [PT, J, D])
        zin, index = w.sb("zin", [PT, J, D]), w.sb("index", [PT, J], I32)
        junk = w.sb("junk", [PT, D])
        ss, floor, rnorm = w.sb("ss", [PT, J]), w.sb("floor", [PT, J]), w.sb("rnorm", [PT, J])
        h = w.sb("h", [PT, J, D])
        ht = [w.sb(f"ht{i}", [P, 2, C, PT], F32R) for i in "hl"]
        pout = w.sb("pout", [PT, J, D])
        pt = [w.ps(f"pt{i}") for i in range(2)]
        pp = [w.ps(f"pp{i}") for i in range(2)]
        p_in = [w.sem(f"p_in{i}") for i in range(2)]
        z_in = [w.sem(f"z_in{i}") for i in range(J)]
        h_out = [w.sem(f"h_out{i}") for i in range(2)]
        p_out = [w.sem(f"p_out{i}") for i in range(2)]
        prefilled, index_done, sum_done, ss_done, floor_done, rnorm_done, h_done = (w.sem(n) for n in (
            "prefilled", "index_done", "sum_done", "ss_done", "floor_done", "rnorm_done", "h_done"))
        t_full, t_hi, t_lo, p_full, p_done = (w.sem(n) for n in ("t_full", "t_hi", "t_lo", "p_full", "p_done"))
        block = w.block()

        def group(n, j):
            return (n - j) // J

        def ok(n):
            return not isinstance(n, int) or 0 <= n < NT

        def steps(eng, body):
            tile_steps(eng, body, -SUM - 4, NT, G)

        @block.sync
        def _(sp):
            def body(s, j):
                n, jn = s + SUM, (j + SUM) % J
                if ok(n) and jn % 2 == 1 and ok(n + J):
                    sp.wait_ge(sum_done, n + 1)
                    alone(sp, w.sp_waited)
                    load_pair(sp, pin, k.ps[l - 1], group(n, jn) + 1, jn - 1, p_in[jn // 2])
                n, jn = s + NORM, (j + NORM) % J
                if ok(n) and jn % 2 == 1:
                    sp.wait_ge(h_done, n + 1)
                    alone(sp, w.sp_waited)
                    store_pair(sp, k.hs[l], h, group(n, jn), jn - 1, h_out[jn // 2])
                if ok(s) and j % 2 == 1:
                    sp.wait_ge(p_done, s + 1)
                    alone(sp, w.sp_waited)
                    store_pair(sp, k.ps[l], pout, group(s, j), j - 1, p_out[j // 2])
            for i in range(2):
                load_pair(sp, pin, k.ps[l - 1], 0, 2 * i, p_in[i])
            wt.load(sp)
            steps(sp, body)
            for i in range(2):
                sp.wait_ge(h_out[i], 32 * G)
                sp.wait_ge(p_out[i], 32 * G)

        @block.gpsimd
        def _(pool):
            def gather(n, j):
                need(pool, sum_done, n - J + 1)
                alone(pool, w.pool_waited)
                pool.tensor_copy(index[:, j:j + 1], k.slots[:, :, :].rearrange("p g j -> p (g j)")[:, bass.ds(n, 1)]).then_inc(index_done, 1)
                pool.wait_ge(prefilled, n + 1)
                pool.wait_ge(index_done, n + 1)
                alone(pool, w.pool_waited)
                pool.indirect_dma_start(out=zin[:, j, :], out_offset=None, in_=k.z[:, :],
                                        in_offset=bass.IndirectOffsetOnAxis(ap=index[:, j:j + 1], axis=0),
                                        bounds_check=E - 1, oob_is_err=False).then_inc(z_in[j], 16)

            def body(s, j):
                n, jn = s + NORM, (j + NORM) % J
                if ok(n):
                    pool.wait_ge(ss_done, n + 1)
                    alone(pool, w.pool_waited)
                    pool.tensor_scalar(floor[:, jn:jn + 1], ss[:, jn:jn + 1], NORM_EPS2, None, ALU.max).then_inc(floor_done, 1)
                    pool.wait_ge(floor_done, n + 1)
                    pool.tensor_tensor(rnorm[:, jn:jn + 1], floor[:, jn:jn + 1], k.minus_half[0:PT, 0:1], ALU.pow).then_inc(rnorm_done, 1)
                if ok(s + 6):
                    gather(s + 6, (j + 6) % J)
            steps(pool, body)

        @block.vector
        def _(dve):
            def body(s, j):
                n, jn = s + SUM, (j + SUM) % J
                if ok(n):
                    dve.wait_ge(p_in[jn // 2], 32 * (group(n, jn) + 1))
                    dve.wait_ge(z_in[jn], 16 * (group(n, jn) + 1))
                    need(dve, h_done, n - J + 1)
                    dve.tensor_tensor(rows[:, jn, :], pin[:, jn, :], zin[:, jn, :], ALU.add).then_inc(sum_done, 1)
                    dve.wait_ge(sum_done, n + 1)
                    dve.scalar_tensor_tensor(junk[:, :], rows[:, jn, :], 0.0, rows[:, jn, :], ALU.max, ALU.mult,
                                             accum_out=ss[:, jn:jn + 1]).then_inc(ss_done, 1)
                if isinstance(s, int) and s == -2:
                    wt.split_lo(dve, 0)
                m = s + 1
                if ok(m):
                    r = (j + 1) % 2
                    dve.wait_ge(t_hi, m + 1)
                    dve.tensor_tensor(ht[1][:, r, :, :].rearrange("p c t -> p (c t)"), pt[r][:, 0:GT],
                                      ht[0][:, r, :, :].rearrange("p c t -> p (c t)").bitcast(F32), ALU.subtract).then_inc(t_lo, 1)
            steps(dve, body)

        @block.scalar
        def _(act):
            def prefill(n, j):
                need(act, sum_done, n - J + 1)
                act.activation(zin[:, j, :], k.bias[0:PT, l - 1, :], ACT.Copy).then_inc(prefilled, 1)

            def body(s, j):
                if ok(s + 7):
                    prefill(s + 7, (j + 7) % J)
                n, jn = s + NORM, (j + NORM) % J
                if ok(n):
                    act.wait_ge(rnorm_done, n + 1)
                    need(act, t_full, n - J + 1)
                    need(act, h_out[jn // 2], 32 * group(n, jn))
                    act.activation(h[:, jn, :], rows[:, jn, :], ACT.Relu, scale=rnorm[:, jn:jn + 1]).then_inc(h_done, 1)
                if isinstance(s, int) and s == -2:
                    wt.split_hi(act, 0)
                m = s + 1
                if ok(m):
                    r = (j + 1) % 2
                    act.wait_ge(t_full, m + 1)
                    need(act, p_full, m - 1)
                    act.activation(ht[0][:, r, :, :].rearrange("p c t -> p (c t)"), pt[r][:, 0:GT], ACT.Copy).then_inc(t_hi, 1)
                if ok(s):
                    act.wait_ge(p_full, s + 1)
                    need(act, p_out[j // 2], 32 * group(s, j))
                    act.activation(pout[:, j, :], pp[j % 2][0:PT, :], ACT.Copy).then_inc(p_done, 1)
            steps(act, body)

        @block.tensor
        def _(pe):
            def body(s, j):
                m = s + 1
                if ok(m):
                    r, jm = (j + 1) % 2, (j + 1) % J
                    pe.wait_ge(h_done, m + 1)
                    need(pe, t_lo, m - 1)
                    for c in range(C):
                        mm = pe.transpose(pt[r][:, c * PT:(c + 1) * PT], h[:, jm, c * P:(c + 1) * P], k.ident[0:PT, 0:PT])
                    mm.then_inc(t_full, 1)
                if isinstance(s, int) and s == 0:
                    wt.wait(pe, 0)
                if ok(s):
                    r = j % 2
                    pe.wait_ge(t_lo, s + 1)
                    need(pe, p_done, s - 1)
                    for c in range(C):
                        mm = three(pe, pp[r][0:PT, :], ht[0][:, r, c, :], ht[1][:, r, c, :], wt.hi[0][:, c, :], wt.lo[0][:, c, :], c == 0, c == C - 1)
                    mm.then_inc(p_full, 1)
            steps(pe, body)



def build_attention_matrix(nc, k, arg, acc, m_hi, m_lo):
    with Pass(nc, "m") as w:
        wv, wp = w.sb("wv", [P, C, D]), w.sb("wp", [P, C, D])
        bv = w.sb("bv", [P, C])
        a, at = w.sb("a", [P, C, D]), w.sb("at", [P, C, D])
        ksum = w.sb("ksum", [P, D])
        outer = w.sb("outer", [P, C, P])
        kv = w.sb("kv", [P, C, P])
        mf = w.sb("mf", [P, C, D])
        bank = [w.ps(f"bank{i}") for i in range(4)]
        loaded, a_done, sum_full, sum_done, t_full, t_done, zeroed, kv_full, outer_done, kv_done, m_full, m_done, hi_done, lo_done = (w.sem(n) for n in (
            "loaded", "a_done", "sum_full", "sum_done", "t_full", "t_done", "zeroed", "kv_full", "outer_done", "kv_done", "m_full",
            "m_done", "hi_done", "lo_done"))
        block = w.block()

        @block.sync
        def _(sp):
            sp.dma_start(wv[:, :, :], arg["L0_mix_Wv"].rearrange("(c p) n -> p c n", p=P)).then_inc(loaded, 16)
            sp.dma_start(wp[:, :, :], arg["L0_mix_Wp"].rearrange("(c p) n -> p c n", p=P)).then_inc(loaded, 16)
            sp.dma_start(bv[:, :], arg["L0_mix_bv"].rearrange("(c p) -> p c", p=P)).then_inc(loaded, 16)

        @block.gpsimd
        def _(pool):
            pool.memset(kv[:, :, :], 0.0).then_inc(zeroed, 1)

        @block.scalar
        def _(act):
            for c in range(C):
                act.activation(a[:, c, :], acc[c][:, :], ACT.Copy).then_inc(a_done, 1)
            for c in range(C):
                act.wait_ge(m_full, c + 1)
                act.activation(mf[:, c, :], bank[c][:, :], ACT.Copy).then_inc(m_done, 1)
                act.wait_ge(m_done, c + 1)
                act.activation(m_hi[:, c, :], mf[:, c, :], ACT.Copy).then_inc(hi_done, 1)

        @block.tensor
        def _(pe):
            pe.matmul(bank[0][:, :], k.ones[0:PT, :], k.kacc[:, :], start=True, stop=True).then_inc(sum_full, 1)
            pe.wait_ge(a_done, C)
            pe.wait_ge(sum_done, 1)
            for f in range(C):
                for c in range(C):
                    mm = pe.transpose(bank[f][:, c * P:(c + 1) * P], a[:, c, f * P:(f + 1) * P], k.ident[:, :])
                mm.then_inc(t_full, 1)
            pe.wait_ge(loaded, 48)
            pe.wait_ge(t_done, C)
            for c in range(C):
                for f in range(C):
                    mm = pe.matmul(bank[c][:, 0:P], wv[:, f, c * P:(c + 1) * P], at[:, f, c * P:(c + 1) * P], start=f == 0, stop=f == C - 1)
                mm.then_inc(kv_full, 1)
            for c in range(C):
                pe.wait_ge(kv_done, 2 * C)
                pe.matmul(bank[c][:, :], kv[:, c, :], wp[:, c, :], start=True, stop=True).then_inc(m_full, 1)

        @block.vector
        def _(dve):
            dve.wait_ge(sum_full, 1)
            dve.tensor_copy(ksum[:, :], bank[0][:, :]).then_inc(sum_done, 1)
            dve.wait_ge(sum_done, 1)
            dve.tensor_copy(k.ksum[:, :], ksum[0:PT, :]).then_inc(sum_done, 1)
            for f in range(C):
                dve.wait_ge(t_full, f + 1)
                dve.tensor_copy(at[:, f, :], bank[f][:, :]).then_inc(t_done, 1)
            dve.wait_ge(loaded, 48)
            for c in range(C):
                dve.tensor_scalar(outer[:, c, :], ksum[:, c * P:(c + 1) * P], bv[:, c:c + 1], None, ALU.mult).then_inc(outer_done, 1)
            dve.wait_ge(outer_done, C)
            dve.wait_ge(zeroed, 1)
            for c in range(C):
                dve.wait_ge(kv_full, c + 1)
                for b in range(2):
                    one = slice(b * R, (b + 1) * R)
                    dve.tensor_tensor(kv[one, c, one], bank[c][one, one], outer[one, c, one], ALU.add).then_inc(kv_done, 1)
            for c in range(C):
                dve.wait_ge(hi_done, c + 1)
                dve.tensor_tensor(m_lo[:, c, :], mf[:, c, :], m_hi[:, c, :].bitcast(F32), ALU.subtract).then_inc(lo_done, 1)


def build_pass_d(nc, k, arg, out, m_hi, m_lo, N, E):
    G = N // GT
    NT = G * J
    HC = 3
    FH = HC * P
    with Pass(nc, "d") as w:
        w1_raw, w2_raw = w.sb("w1_raw", [P, C, FG]), w.sb("w2_raw", [P, HC, D])
        w1 = [w.sb(f"w1{i}", [P, C, FG], F32R) for i in "hl"]
        w2 = [w.sb(f"w2{i}", [P, HC, D], F32R) for i in "hl"]
        b1_raw = w.sb("b1_raw", [1, FG])
        b1 = [w.sb(f"b1{i}", [1, FG], F32R) for i in "hl"]
        bp = [w.sb(f"bp{i}", [1, D], F32R) for i in "hl"]
        one = w.sb("one", [1, PT], F32R)
        expert = w.sb("expert", [PT, NE])
        expert_i = w.sb("expert_i", [PT, NE], I32)
        pin, qin, xin = (w.sb(n, [PT, J, D]) for n in ("pin", "qin", "xin"))
        zin, index = w.sb("zin", [PT, J, D]), w.sb("index", [PT, J], I32)
        pos = w.sb("pos", [PT, D])
        ss, floor, rnorm = w.sb("ss", [PT, J]), w.sb("floor", [PT, J]), w.sb("rnorm", [PT, J])
        weighted = w.sb("weighted", [PT, 2, D])
        den, den_eps, rden = w.sb("den", [PT, H]), w.sb("den_eps", [PT, H]), w.sb("rden", [PT, H])
        h = w.sb("h", [PT, 2, D])
        xh = w.sb("xh", [PT, 2, D])
        qn = w.sb("qn", [PT, 2, D])
        x2 = w.sb("x2", [PT, J, D])
        qt = [w.sb(f"qt{i}", [P, 2, C * PT], F32R) for i in "hl"]
        stat, mv, var, rstd = w.sb("stat", [PT, 6]), w.sb("mv", [PT, 2, 2]), w.sb("var", [PT, 1]), w.sb("rstd", [PT, 2])
        shift = w.sb("shift", [PT, 2])
        y = w.sb("y", [PT, 2, D])
        yt = [w.sb(f"yt{i}", [P, 2, C * PT], F32R) for i in "hl"]
        act_hid = w.sb("act_hid", [PT, FE])
        top, top_i, top_f = w.sb("top", [PT, 8]), w.sb("top_i", [PT, 8], U32), w.sb("top_f", [PT, 2])
        gap, th, gap_low, gap_inv, ex = (w.sb(n, [PT, NE]) for n in ("gap", "th", "gap_low", "gap_inv", "ex"))
        is_first, chosen, ex_sum, top_sum, weight, rweight = (w.sb(n, [PT, m]) for n, m in (
            ("is_first", NE), ("chosen", NE), ("ex_sum", 1), ("top_sum", 1), ("weight", 1), ("rweight", 2)))
        sh = w.sb("sh", [PT, 2, FH])
        st = [w.sb(f"st{i}", [P, HC * PT], F32R) for i in "hl"]
        res = w.sb("res", [PT, J, D])
        b_ty, b_tq, b_mix, b_ts, b_w1, b_w2 = (w.ps(n) for n in ("b_ty", "b_tq", "b_mix", "b_ts", "b_w1", "b_w2"))
        zeroed, expert_set, w_in, w_hi, w_lo, expert_done = (w.sem(n) for n in ("zeroed", "expert_set", "w_in", "w_hi", "w_lo", "expert_done"))
        p_in, q_in, x_in, o_out = ([w.sem(f"{n}{i}") for i in range(2)] for n in ("p_in", "q_in", "x_in", "o_out"))
        z_in = [w.sem(f"z_in{i}") for i in range(J)]
        prefilled, index_done, sum_done, relu_done, ss_done, floor_done, rnorm_done, h_done, xh_done = (w.sem(n) for n in (
            "prefilled", "index_done", "sum_done", "relu_done", "ss_done", "floor_done", "rnorm_done", "h_done", "xh_done"))
        weighted_done, den_done, rden_done, qn_done = (w.sem(n) for n in ("weighted_done", "den_done", "rden_done", "qn_done"))
        tq_full, tq_hi, tq_lo, mix_full, x2_done, stat_done, aggr, var_done, rstd_done, shift_done, y_done = (w.sem(n) for n in (
            "tq_full", "tq_hi", "tq_lo", "mix_full", "x2_done", "stat_done", "aggr", "var_done", "rstd_done", "shift_done", "y_done"))
        ty_full, ty_hi, ty_lo, hid_full, top_done, gap_done, index_found, tanh_done, gelu_done = (w.sem(n) for n in (
            "ty_full", "ty_hi", "ty_lo", "hid_full", "top_done", "gap_done", "index_found", "tanh_done", "gelu_done"))
        score_step, sh_done, ts_full, ts_hi, ts_lo, out_full, res_done = (w.sem(n) for n in (
            "score_step", "sh_done", "ts_full", "ts_hi", "ts_lo", "out_full", "res_done"))
        block = w.block()

        def group(n, j):
            return (n - j) // J

        def ok(n):
            return not isinstance(n, int) or 0 <= n < NT

        def steps(eng, body):
            tile_steps(eng, body, -6, NT + 4, G)

        @block.sync
        def _(sp):
            for i in range(2):
                load_pair(sp, pin, k.ps[2], 0, 2 * i, p_in[i])
                load_pair(sp, qin, k.phi_q, 0, 2 * i, q_in[i])
                load_pair(sp, xin, arg["x"], 0, 2 * i, x_in[i])
            sp.wait_ge(zeroed, 3)
            sp.dma_start(w1_raw[:, :, FE:FG], arg["L0_ffn_Wg"].rearrange("(c p) e -> p c e", p=P)).then_inc(w_in, 16)
            for e in range(NE):
                sp.dma_start(w1_raw[:, :, e * HE:(e + 1) * HE], arg["L0_ffn_W1"][e].rearrange("(c p) f -> p c f", p=P)).then_inc(w_in, 16)
            w2_rows = arg["L0_ffn_W2"].rearrange("e f n -> (e f) n")
            sp.dma_start(w2_raw[:, 0:2, :], w2_rows.rearrange("(c p) n -> p c n", p=P)).then_inc(w_in, 16)
            sp.dma_start(w2_raw[0:NE, 2, :], arg["L0_ffn_b2"]).then_inc(w_in, 16)
            sp.dma_start(b1_raw[:, 0:FE], arg["L0_ffn_b1"].rearrange("(o e) f -> o (e f)", o=1)).then_inc(w_in, 16)

            def body(s, j):
                n, jn = s + 1, (j + 1) % J
                if ok(n) and jn % 2 == 1 and ok(n + J):
                    sp.wait_ge(xh_done, n + 1)
                    alone(sp, w.sp_waited)
                    load_pair(sp, xin, arg["x"], group(n, jn) + 1, jn - 1, x_in[jn // 2])
                n, jn = s + 2, (j + 2) % J
                if ok(n) and jn % 2 == 1 and ok(n + J):
                    sp.wait_ge(qn_done, n + 1)
                    alone(sp, w.sp_waited)
                    load_pair(sp, qin, k.phi_q, group(n, jn) + 1, jn - 1, q_in[jn // 2])
                    sp.wait_ge(h_done, n + 1)
                    alone(sp, w.sp_waited)
                    load_pair(sp, pin, k.ps[2], group(n, jn) + 1, jn - 1, p_in[jn // 2])
                n = s - 4
                if ok(n) and j % 2 == 1:
                    sp.wait_ge(res_done, n + 1)
                    alone(sp, w.sp_waited)
                    store_pair(sp, out, res, group(n, j), j - 1, o_out[j // 2])
            steps(sp, body)
            for i in range(2):
                sp.wait_ge(o_out[i], 32 * G)

        @block.gpsimd
        def _(pool):
            pool.memset(w2_raw[:, 2, :], 0.0).then_inc(zeroed, 1)
            pool.memset(b1_raw[:, :], 0.0).then_inc(zeroed, 1)
            pool.memset(sh[:, :, :], 0.0).then_inc(zeroed, 1)
            pool.iota(expert_i[:, :], pattern=[[1, NE]], base=0, channel_multiplier=0).then_inc(expert_set, 1)

            def body(s, j):
                n, r = s - 1, slot2(j - 1)
                if ok(n):
                    pool.wait_ge(aggr, n + 1)
                    alone(pool, w.pool_waited)
                    pool.tensor_scalar(var[:, :], mv[:, r, 1:2], LN_EPS, None, ALU.add).then_inc(var_done, 1)
                    pool.wait_ge(var_done, n + 1)
                    need(pool, y_done, n - 1)
                    pool.tensor_tensor(rstd[:, r:r + 1], var[:, :], k.minus_half[0:PT, 0:1], ALU.pow).then_inc(rstd_done, 1)
                n, jn = s + 2, (j + 2) % J
                if ok(n):
                    pool.wait_ge(ss_done, n + 1)
                    alone(pool, w.pool_waited)
                    pool.tensor_scalar(floor[:, jn:jn + 1], ss[:, jn:jn + 1], NORM_EPS2, None, ALU.max).then_inc(floor_done, 1)
                    pool.wait_ge(floor_done, n + 1)
                    pool.tensor_tensor(rnorm[:, jn:jn + 1], floor[:, jn:jn + 1], k.minus_half[0:PT, 0:1], ALU.pow).then_inc(rnorm_done, 1)
                n, jn = s + 3, (j + 3) % J
                if ok(n):
                    pool.wait_ge(p_in[jn // 2], 32 * (group(n, jn) + 1))
                    pool.wait_ge(z_in[jn], 16 * (group(n, jn) + 1))
                    pool.tensor_tensor(pin[:, jn, :], pin[:, jn, :], zin[:, jn, :], ALU.add).then_inc(sum_done, 1)
                n, jn = s + 1, (j + 1) % J
                if ok(n):
                    pool.wait_ge(x_in[jn // 2], 32 * (group(n, jn) + 1))
                    pool.wait_ge(h_done, n + 1)
                    need(pool, x2_done, n - 1)
                    pool.tensor_tensor(xh[:, jn % 2, :], xin[:, jn, :], h[:, jn % 2, :], ALU.add).then_inc(xh_done, 1)
                n = s + 4
                if ok(n):
                    pool.wait_ge(q_in[j // 2], 32 * (group(n, j) + 1))
                    need(pool, den_done, 2 * (n - 2) + 1)
                    pool.tensor_tensor(weighted[:, j % 2, :], qin[:, j, :], k.ksum[:, :], ALU.mult).then_inc(weighted_done, 1)
                n, jn = s + 5, (j + 5) % J
                if ok(n):
                    need(pool, sum_done, n - J + 1)
                    alone(pool, w.pool_waited)
                    pool.tensor_copy(index[:, jn:jn + 1], k.slots[:, :, :].rearrange("p g j -> p (g j)")[:, bass.ds(n, 1)]).then_inc(index_done, 1)
                    pool.wait_ge(prefilled, n + 1)
                    pool.wait_ge(index_done, n + 1)
                    alone(pool, w.pool_waited)
                    pool.indirect_dma_start(out=zin[:, jn, :], out_offset=None, in_=k.z[:, :],
                                            in_offset=bass.IndirectOffsetOnAxis(ap=index[:, jn:jn + 1], axis=0),
                                            bounds_check=E - 1, oob_is_err=False).then_inc(z_in[jn], 16)
            steps(pool, body)

        @block.tensor
        def _(pe):
            pe.wait_ge(w_lo, 4)

            def body(s, j):
                n = s + 1
                if ok(n):
                    pe.wait_ge(qn_done, n + 1)
                    need(pe, tq_lo, n)
                    for c in range(C):
                        mm = pe.transpose(b_tq[:, c * PT:(c + 1) * PT], qn[:, slot2(j + 1), c * P:(c + 1) * P], k.ident[0:PT, 0:PT])
                    mm.then_inc(tq_full, 1)
                n = s - 4
                if ok(n):
                    pe.wait_ge(ts_lo, n + 1)
                    need(pe, res_done, n)
                    for c in range(HC):
                        part = slice(c * PT, (c + 1) * PT)
                        mm = three(pe, b_w2[0:PT, :], st[0][:, part], st[1][:, part], w2[0][:, c, :], w2[1][:, c, :], c == 0, c == HC - 1)
                    mm.then_inc(out_full, 1)
                if ok(s):
                    pe.wait_ge(tq_lo, s + 1)
                    need(pe, x2_done, s)
                    for i in range(2):
                        pe.matmul(b_mix[0:PT, :], one[:, :], bp[i][:, :], start=i == 0, stop=False)
                    for c in range(C):
                        part = slice(c * PT, (c + 1) * PT)
                        mm = three(pe, b_mix[0:PT, :], qt[0][:, j % 2, part], qt[1][:, j % 2, part], m_hi[:, c, :], m_lo[:, c, :], False, c == C - 1)
                    mm.then_inc(mix_full, 1)
                n = s - 1
                if ok(n):
                    pe.wait_ge(y_done, n + 1)
                    need(pe, ty_lo, n)
                    for c in range(C):
                        mm = pe.transpose(b_ty[:, c * PT:(c + 1) * PT], y[:, slot2(j - 1), c * P:(c + 1) * P], k.ident[0:PT, 0:PT])
                    mm.then_inc(ty_full, 1)
                n = s - 3
                if ok(n):
                    pe.wait_ge(sh_done, n + 1)
                    need(pe, ts_lo, n)
                    for c in range(HC):
                        mm = pe.transpose(b_ts[:, c * PT:(c + 1) * PT], sh[:, slot2(j - 3), c * P:(c + 1) * P], k.ident[0:PT, 0:PT])
                    mm.then_inc(ts_full, 1)
                n = s - 2
                if ok(n):
                    pe.wait_ge(ty_lo, n + 1)
                    need(pe, gelu_done, n)
                    for i in range(2):
                        pe.matmul(b_w1[0:PT, 0:FG], one[:, :], b1[i][:, :], start=i == 0, stop=False)
                    for c in range(C):
                        part = slice(c * PT, (c + 1) * PT)
                        mm = three(pe, b_w1[0:PT, 0:FG], yt[0][:, j % 2, part], yt[1][:, j % 2, part], w1[0][:, c, :], w1[1][:, c, :], False, c == C - 1)
                    mm.then_inc(hid_full, 1)
            steps(pe, body)

        @block.scalar
        def _(act):
            act.activation(one[:, :], k.ones[0:1, 0:PT], ACT.Copy).then_inc(w_hi, 1)
            act.activation(bp[0][:, :], k.bp[0:1, :], ACT.Copy).then_inc(w_hi, 1)

            def weights():
                act.wait_ge(zeroed, 3)
                act.wait_ge(w_in, 16 * (NE + 4))
                act.activation(b1[0][:, :], b1_raw[:, :], ACT.Copy).then_inc(w_hi, 1)
                act.activation(w1[0][:, :, :], w1_raw[:, :, :], ACT.Copy).then_inc(w_hi, 1)
                act.activation(w2[0][:, :, :], w2_raw[:, :, :], ACT.Copy).then_inc(w_hi, 1)

            def body(s, j):
                n = s - 3
                if ok(n):
                    need(act, sh_done, n)
                    act.wait_ge(gap_done, n + 1)
                    act.activation(th[:, :], gap[:, :], ACT.Tanh, scale=0.5).then_inc(tanh_done, 1)
                    act.wait_ge(index_found, n + 1)
                    act.activation(act_hid[:, :], b_w1[0:PT, 0:FE], ACT.Gelu).then_inc(gelu_done, 1)
                n = s + 1
                if ok(n):
                    act.wait_ge(tq_full, n + 1)
                    need(act, mix_full, n - 1)
                    act.activation(qt[0][:, slot2(j + 1), :], b_tq[:, 0:C * PT], ACT.Copy).then_inc(tq_hi, 1)
                n, jn = s + 6, (j + 6) % J
                if ok(n):
                    need(act, sum_done, n - J + 1)
                    act.activation(zin[:, jn, :], k.bias[0:PT, 2, :], ACT.Copy).then_inc(prefilled, 1)
                if isinstance(s, int) and s == -3:
                    weights()
                n, jn = s + 2, (j + 2) % J
                if ok(n):
                    act.wait_ge(rnorm_done, n + 1)
                    need(act, xh_done, n - 1)
                    act.activation(h[:, jn % 2, :], pin[:, jn, :], ACT.Relu, scale=rnorm[:, jn:jn + 1]).then_inc(h_done, 1)
                n, jn = s - 1, (j - 1) % J
                if ok(n):
                    act.wait_ge(shift_done, n + 1)
                    need(act, ty_full, n - 1)
                    act.activation(y[:, jn % 2, :], x2[:, jn, :], ACT.Identity, bias=shift[:, jn % 2:jn % 2 + 1],
                                   scale=rstd[:, jn % 2:jn % 2 + 1]).then_inc(y_done, 1)
                n, jn = s + 3, (j + 3) % J
                if ok(n):
                    act.wait_ge(sum_done, n + 1)
                    need(act, ss_done, n)
                    act.activation(pos[:, :], pin[:, jn, :], ACT.Relu).then_inc(relu_done, 1)
                    act.wait_ge(relu_done, n + 1)
                    act.activation(pos[:, :], pos[:, :], ACT.Square, accum_out=ss[:, jn:jn + 1]).then_inc(ss_done, 1)
                n = s - 1
                if ok(n):
                    act.wait_ge(ty_full, n + 1)
                    need(act, hid_full, n - 1)
                    act.activation(yt[0][:, slot2(j - 1), :], b_ty[:, 0:C * PT], ACT.Copy).then_inc(ty_hi, 1)
                n = s - 3
                if ok(n):
                    act.wait_ge(ts_full, n + 1)
                    need(act, out_full, n)
                    act.activation(st[0][:, :], b_ts[:, 0:HC * PT], ACT.Copy).then_inc(ts_hi, 1)
            steps(act, body)

        @block.vector
        def _(dve):
            dve.wait_ge(w_hi, 2)
            dve.tensor_tensor(bp[1][:, :], k.bp[0:1, :], bp[0][:, :].bitcast(F32), ALU.subtract).then_inc(w_lo, 1)
            dve.wait_ge(expert_set, 1)
            dve.tensor_copy(expert[:, :], expert_i[:, :]).then_inc(expert_done, 1)
            dve.wait_ge(expert_done, 1)

            def weights():
                dve.wait_ge(w_hi, 5)
                dve.tensor_tensor(b1[1][:, :], b1_raw[:, :], b1[0][:, :].bitcast(F32), ALU.subtract).then_inc(w_lo, 1)
                dve.tensor_tensor(w1[1][:, :, :], w1_raw[:, :, :], w1[0][:, :, :].bitcast(F32), ALU.subtract).then_inc(w_lo, 1)
                dve.tensor_tensor(w2[1][:, :, :], w2_raw[:, :, :], w2[0][:, :, :].bitcast(F32), ALU.subtract).then_inc(w_lo, 1)
            SCORE = 9

            def body(s, j):
                if isinstance(s, int) and s == -3:
                    weights()
                n, r = s - 3, slot2(j - 3)
                gate, done = ok(n), SCORE * n
                if gate:
                    dve.wait_ge(hid_full, n + 1)
                    alone(dve, w.dve_waited)
                    dve.max(top[:, :], b_w1[0:PT, FE:FG]).then_inc(top_done, 1)
                    dve.wait_ge(top_done, n + 1)
                    need(dve, tanh_done, n)
                    dve.tensor_scalar(gap[:, :], b_w1[0:PT, FE:FG], top[:, 0:1], None, ALU.subtract).then_inc(gap_done, 1)
                    alone(dve, w.dve_waited)
                    dve.max_index(top_i[:, :], top[:, :], b_w1[0:PT, FE:FG]).then_inc(index_found, 1)
                m = s - 2
                if ok(m):
                    dve.wait_ge(ty_hi, m + 1)
                    dve.tensor_tensor(yt[1][:, slot2(j), :], b_ty[:, 0:C * PT], yt[0][:, slot2(j), :].bitcast(F32), ALU.subtract).then_inc(ty_lo, 1)
                if gate:
                    dve.wait_ge(index_found, n + 1)
                    dve.tensor_copy(top_f[:, :], top_i[:, 0:2]).then_inc(score_step, 1)
                    dve.wait_ge(tanh_done, n + 1)
                    dve.tensor_scalar(gap_low[:, :], th[:, :], -1.0, 1.0, ALU.mult, ALU.add).then_inc(score_step, 1)
                m, jm = s + 2, (j + 2) % J
                if ok(m):
                    dve.wait_ge(rden_done, m + 1)
                    need(dve, tq_full, m - 1)
                    dve.tensor_tensor(qn[:, jm % 2, :].rearrange("p (h r) -> p h r", h=H), qin[:, jm, :].rearrange("p (h r) -> p h r", h=H),
                                      rden[:, :].unsqueeze(2).broadcast_to([PT, H, R]), ALU.mult).then_inc(qn_done, 1)
                if gate:
                    dve.wait_ge(score_step, done + 1)
                    dve.tensor_scalar(is_first[:, :], expert[:, :], top_f[:, 0:1], None, ALU.is_equal).then_inc(score_step, 1)
                    dve.wait_ge(score_step, done + 2)
                    dve.reciprocal(gap_inv[:, :], gap_low[:, :]).then_inc(score_step, 1)
                m, rm = s - 1, slot2(j - 1)
                if ok(m):
                    dve.wait_ge(rstd_done, m + 1)
                    need(dve, y_done, m - 1)
                    dve.scalar_tensor_tensor(shift[:, rm:rm + 1], mv[:, rm, 0:1], -1.0, rstd[:, rm:rm + 1],
                                             ALU.mult, ALU.mult).then_inc(shift_done, 1)
                t, jt = s + 3, (j + 3) % J
                if ok(t):
                    dve.wait_ge(weighted_done, t + 1)
                    dve.tensor_reduce(den[:, :], weighted[:, jt % 2, :].rearrange("p (h r) -> p h r", h=H), AX.X, ALU.add).then_inc(den_done, 1)
                if gate:
                    dve.wait_ge(score_step, done + 3)
                    dve.scalar_tensor_tensor(chosen[:, :], expert[:, :], top_f[:, 1:2], is_first[:, :], ALU.is_equal, ALU.add).then_inc(score_step, 1)
                    dve.wait_ge(score_step, done + 4)
                    dve.scalar_tensor_tensor(ex[:, :], th[:, :], 1.0, gap_inv[:, :], ALU.add, ALU.mult,
                                             accum_out=ex_sum[:, :]).then_inc(score_step, 1)
                m = s + 1
                if ok(m):
                    dve.wait_ge(tq_hi, m + 1)
                    dve.tensor_tensor(qt[1][:, slot2(j + 1), :], b_tq[:, 0:C * PT], qt[0][:, slot2(j + 1), :].bitcast(F32), ALU.subtract).then_inc(tq_lo, 1)
                if gate:
                    dve.wait_ge(score_step, done + 6)
                    need(dve, ts_full, n - 1)
                    dve.scalar_tensor_tensor(sh[:, r, FE:FG], ex[:, :], 1.0, chosen[:, :], ALU.mult, ALU.mult, accum_out=top_sum[:, :]).then_inc(score_step, 1)
                m = s - 4
                if ok(m):
                    dve.wait_ge(out_full, m + 1)
                    dve.wait_ge(score_step, SCORE * (m + 1))
                    need(dve, o_out[j // 2], 32 * group(m, j))
                    dve.scalar_tensor_tensor(res[:, j, :], b_w2[0:PT, :], rweight[:, slot2(j):slot2(j) + 1], x2[:, j, :], ALU.mult, ALU.add).then_inc(res_done, 1)
                if gate:
                    dve.wait_ge(score_step, done + 7)
                    dve.wait_ge(gelu_done, n + 1)
                    dve.tensor_tensor(sh[:, r, 0:FE].rearrange("p (e f) -> p e f", e=NE), act_hid[:, :].rearrange("p (e f) -> p e f", e=NE),
                                      sh[:, r, FE:FG].unsqueeze(2).broadcast_to([PT, NE, HE]), ALU.mult).then_inc(sh_done, 1)
                    dve.scalar_tensor_tensor(weight[:, :], ex_sum[:, :], 1e-6, top_sum[:, :], ALU.mult, ALU.add).then_inc(score_step, 1)
                if ok(t):
                    dve.wait_ge(den_done, 2 * t + 1)
                    dve.tensor_scalar(den_eps[:, :], den[:, :], DEN_EPS, None, ALU.add).then_inc(den_done, 1)
                if gate:
                    dve.wait_ge(score_step, done + 8)
                    need(dve, res_done, n - 1)
                    dve.reciprocal(rweight[:, r:r + 1], weight[:, :]).then_inc(score_step, 1)
                if ok(t):
                    dve.wait_ge(den_done, 2 * t + 2)
                    need(dve, qn_done, t)
                    dve.reciprocal(rden[:, :], den_eps[:, :]).then_inc(rden_done, 1)
                if ok(s):
                    dve.wait_ge(mix_full, s + 1)
                    dve.wait_ge(xh_done, s + 1)
                    need(dve, res_done, s - J + 1)
                    dve.tensor_tensor(x2[:, j, :], b_mix[0:PT, :], xh[:, j % 2, :], ALU.add).then_inc(x2_done, 1)
                    dve.wait_ge(x2_done, s + 1)
                    dve.bn_stats(stat[:, :], x2[:, j, :]).then_inc(stat_done, 1)
                if ok(n):
                    dve.wait_ge(ts_hi, n + 1)
                    dve.tensor_tensor(st[1][:, :], b_ts[:, 0:HC * PT], st[0][:, :].bitcast(F32), ALU.subtract).then_inc(ts_lo, 1)
                if ok(s):
                    dve.wait_ge(stat_done, s + 1)
                    alone(dve, w.dve_waited)
                    dve.bn_aggr(mv[:, j % 2, :], stat[:, :]).then_inc(aggr, 1)
            steps(dve, body)


_INS = ["x", "src", "dst", "L0_gnn_W_self", "L0_gnn_W_neigh", "L0_gnn_b", "L0_mix_Wq", "L0_mix_bq", "L0_mix_Wk",
        "L0_mix_bk", "L0_mix_Wv", "L0_mix_bv", "L0_mix_Wp", "L0_mix_bp", "L0_mix_gamma_q", "L0_mix_beta_q",
        "L0_mix_gamma_k", "L0_mix_beta_k", "L0_mix_qG1", "L0_mix_qG2", "L0_mix_kG1", "L0_mix_kG2", "L0_ffn_Wg",
        "L0_ffn_W1", "L0_ffn_b1", "L0_ffn_W2", "L0_ffn_b2"]


class Kept:
    pass


def build(nc, arg, out):
    N = arg["x"].shape[0]
    E = arg["src"].shape[0]
    T = E // PT
    G = N // GT
    assert arg["x"].shape[1] == D and N % GT == 0 and T % J == 0 and T > 2 * J and G >= 6
    k = Kept()

    def dram(name, shape, dt=F32):
        return nc.dram_tensor("kept_" + name, shape, dt, kind="Internal").ap()

    k.ps = [dram(f"p{l}", [N, D]) for l in range(3)]
    k.hs = [dram(f"h{l}", [N, D]) for l in range(3)]
    k.phi_q = dram("phi_q", [N, D])
    k.z = dram("z", [E, D])
    k.edges_sorted, k.dst_sorted = dram("edges_sorted", [E, 4]), dram("dst_sorted", [E + 2, 1])
    k.slot_map = dram("slot_map", [N + E, 1], I32)
    with ExitStack() as ctx:
        def sb(name, shape, dt=F32):
            return ctx.enter_context(nc.sbuf_tensor(name, shape, dt))

        k.ident, k.ones, k.minus_half = sb("ident", [P, P]), sb("ones", [P, P]), sb("minus_half", [P, 8])
        k.bias, k.bp = sb("bias", [P, 3, D]), sb("bp", [P, D])
        k.kacc = sb("kacc", [PT, D])
        k.src, k.dst, k.rdeg = sb("src", [PT, T], I32), sb("dst", [PT, T]), sb("rdeg", [PT, T])
        k.drow = sb("drow", [P, E + 2])
        k.slots = sb("slots", [PT, G, J], I32)
        k.ksum = sb("ksum", [PT, D])
        build_constants(nc, k, arg, N, E)
        build_sort(nc, k, arg, N, E)
        build_slots(nc, k, arg, N, E)
        with ExitStack() as held:
            acc = [held.enter_context(nc.psum_tensor(f"acc{c}", [P, 512], F32)) for c in range(C)]
            build_pass_a(nc, k, arg, N, acc)
            m_hi, m_lo = sb("m_hi", [P, C, D], F32R), sb("m_lo", [P, C, D], F32R)
            build_attention_matrix(nc, k, arg, acc, m_hi, m_lo)
        build_neighbours(nc, k, arg, 0, E)
        build_layer(nc, k, arg, 1, N, E)
        build_neighbours(nc, k, arg, 1, E)
        build_layer(nc, k, arg, 2, N, E)
        build_neighbours(nc, k, arg, 2, E)
        build_pass_d(nc, k, arg, out, m_hi, m_lo, N, E)


def kernel(**inputs):
    import concourse.bacc as bacc
    from concourse.bass_utils import run_bass_kernel_spmd as run

    nc = bacc.Bacc("TRN2", target_bir_lowering=False, num_devices=1)
    arrays, arg = {}, {}
    for name in _INS:
        a = np.ascontiguousarray(inputs[name])
        arrays["in_" + name] = a
        arg[name] = nc.dram_tensor("in_" + name, a.shape, mybir.dt.from_np(a.dtype), kind="ExternalInput").ap()
    out = nc.dram_tensor("out", inputs["x"].shape, F32, kind="ExternalOutput").ap()
    build(nc, arg, out)
    return run(nc, [arrays], core_ids=[0]).results[0]["out"]
```

```python
from contextlib import ExitStack

import numpy as np

import concourse.bass as bass
from concourse import mybir

F32 = mybir.dt.float32
F32R = mybir.dt.float32r
I32 = mybir.dt.int32
U32 = mybir.dt.uint32
ACT = mybir.ActivationFunctionType
ALU = mybir.AluOpType
AX = mybir.AxisListType

P = 128
PT = 125
J = 4
GT = PT * J
PA = 112
D = 512
C = D // P
H = 8
R = 64
NE = 8
HE = 32
FE = NE * HE
FG = FE + NE
LN_EPS = 1e-5
NORM_EPS2 = 1e-24
DEN_EPS = 1e-6


def need(eng, sem, value):
    if isinstance(value, int) and value <= 0:
        return
    eng.wait_ge(sem, value)


def alone(eng, waited):
    eng.sem_inc(waited, 1)


def tile_steps(eng, body, first, end, groups, peeled=2):
    for s in range(first, peeled * J):
        body(s, s % J)
    with eng.Fori(peeled, groups - peeled) as g:
        for j in range(J):
            body(g * J + j, j)
    for s in range((groups - peeled) * J, end):
        body(s, s % J)


def slot2(j):
    return j % 2


def three(pe, out, a_hi, a_lo, b_hi, b_lo, first, last):
    pe.matmul(out, a_hi, b_hi, start=first, stop=False)
    pe.matmul(out, a_hi, b_lo, start=False, stop=False)
    return pe.matmul(out, a_lo, b_hi, start=False, stop=last)


def rows_of(dram, g, j0, j1):
    v = dram.rearrange("(q j) d -> q j d", j=J)
    for a, b in ((0, PA), (PA, PT)):
        yield slice(a, b), v[bass.ds(g * PT + a, b - a), j0:j1, :]


def load_group(eng, tile, dram, g, sem):
    for part, view in rows_of(dram, g, 0, J):
        eng.dma_start(tile[part, :, :], view).then_inc(sem, 16)


def load_pair(eng, tile, dram, g, j0, sem):
    for part, view in rows_of(dram, g, j0, j0 + 2):
        eng.dma_start(tile[part, j0:j0 + 2, :], view).then_inc(sem, 16)


def store_pair(eng, dram, tile, g, j0, sem):
    for part, view in rows_of(dram, g, j0, j0 + 2):
        eng.dma_start(view, tile[part, j0:j0 + 2, :]).then_inc(sem, 16)


class Pass:

    def __init__(self, nc, name):
        self.nc, self.name, self.ctx, self.sems = nc, name, ExitStack(), []

    def __enter__(self):
        self.ctx.__enter__()
        self.ctx.enter_context(self.nc.allow_non_contiguous_dma(reason="a few thousand words of indices and biases"))
        self.pool_waited, self.dve_waited, self.sp_waited = (self.sem(n) for n in ("pool_waited", "dve_waited", "sp_waited"))
        return self

    def __exit__(self, *a):
        self.ctx.__exit__(*a)
        self.nc.clear_and_free_semaphores(self.sems)
        self.nc.all_engine_barrier()

    def sb(self, name, shape, dt=F32):
        return self.ctx.enter_context(self.nc.sbuf_tensor(f"{self.name}_{name}", shape, dt))

    def ps(self, name, shape=(P, 512), dt=F32):
        return self.ctx.enter_context(self.nc.psum_tensor(f"{self.name}_{name}", list(shape), dt))

    def sem(self, name):
        self.sems.append(self.nc.alloc_semaphore(f"{self.name}_{name}"))
        return self.sems[-1]

    def block(self):
        return self.ctx.enter_context(self.nc.Block())


class Weights:

    def __init__(self, w, drams, scales=None, kept=None):
        self.drams, self.scales = drams, scales or [1.0] * len(drams)
        self.hi = [kept[0]] if kept else [w.sb(f"w{i}_hi", [P, C, D], F32R) for i in range(len(drams))]
        self.lo = [kept[1]] if kept else [w.sb(f"w{i}_lo", [P, C, D], F32R) for i in range(len(drams))]
        self.raw = [w.sb(f"w_raw{i}", [P, C, D]) for i in range(min(2, len(drams)))]
        self.loaded = [w.sem(f"w_loaded{i}") for i in range(len(self.raw))]
        self.hi_done, self.lo_done = w.sem("w_hi_done"), w.sem("w_lo_done")

    def load(self, sp, first=0, end=None):
        for i, dram in list(enumerate(self.drams))[first:end]:
            if i >= 2:
                sp.wait_ge(self.lo_done, i - 1)
            sp.dma_start(self.raw[i % 2][:, :, :], dram.rearrange("(c p) n -> p c n", p=P)).then_inc(self.loaded[i % 2], 16)

    def split_hi(self, act, i):
        act.wait_ge(self.loaded[i % 2], 16 * (i // 2 + 1))
        act.activation(self.hi[i][:, :, :], self.raw[i % 2][:, :, :], ACT.Identity, scale=self.scales[i]).then_inc(self.hi_done, 1)

    def split_lo(self, dve, i):
        dve.wait_ge(self.hi_done, i + 1)
        dve.scalar_tensor_tensor(self.lo[i][:, :, :], self.raw[i % 2][:, :, :], self.scales[i],
                                 self.hi[i][:, :, :].bitcast(F32), ALU.mult, ALU.subtract).then_inc(self.lo_done, 1)

    def split_chunk_hi(self, act, c):
        act.wait_ge(self.loaded[0], 16)
        act.activation(self.hi[0][:, c, :], self.raw[0][:, c, :], ACT.Copy).then_inc(self.hi_done, 1)

    def split_chunk_lo(self, dve, c):
        dve.wait_ge(self.hi_done, c + 1)
        dve.tensor_tensor(self.lo[0][:, c, :], self.raw[0][:, c, :], self.hi[0][:, c, :].bitcast(F32), ALU.subtract).then_inc(self.lo_done, 1)

    def wait(self, pe, i):
        pe.wait_ge(self.lo_done, i + 1)


def build_constants(nc, k):
    with Pass(nc, "const") as w:
        set_done, masked = w.sem("set_done"), w.sem("masked")
        block = w.block()

        @block.gpsimd
        def _(pool):
            pool.memset(k.edge[:, :], 0.0).then_inc(set_done, 1)
            pool.memset(k.ident[:, :], 1.0).then_inc(set_done, 1)
            pool.memset(k.ones[:, :], 1.0).then_inc(set_done, 1)
            pool.memset(k.earlier[:, :], 1.0).then_inc(set_done, 1)
            pool.memset(k.minus_half[:, :], -0.5).then_inc(set_done, 1)
            pool.wait_ge(set_done, 5)
            pool.affine_select(out=k.ident[:, :], in_=k.ident[:, :], compare_op=ALU.is_equal, fill=0.0, base=0,
                               pattern=[[1, P]], channel_multiplier=-1).then_inc(masked, 1)
            pool.affine_select(out=k.earlier[:, :], in_=k.earlier[:, :], compare_op=ALU.is_gt, fill=0.0, base=0,
                               pattern=[[-1, PT]], channel_multiplier=1).then_inc(masked, 1)
            pool.wait_ge(masked, 2)


def build_pass_a(nc, k, arg, N, E, acc):
    G = N // GT
    assert E // PT == G
    with Pass(nc, "a") as w:
        gam = w.sb("gam", [P, 4])
        wt = Weights(w, [arg["L0_mix_Wk"], arg["L0_gnn_W_self"][0], arg["L0_mix_Wq"]],
                     [gam[:, 0:1], 1.0, gam[:, 2:3]])
        WK, WS, WQ = 0, 1, 2
        g_raw = w.sb("g_raw", [P, 2, 2 * P])
        g_hi, g_lo = w.sb("g_hi", [P, 2, 2 * P], F32R), w.sb("g_lo", [P, 2, 2 * P], F32R)
        x, xn = w.sb("x", [PT, J, D]), w.sb("xn", [PT, J, D])
        xs = [w.sb(f"xs{i}", [PT, J, D], F32R) for i in "hl"]
        xt = [w.sb(f"xt{i}", [P, C, GT], F32R) for i in "hl"]
        zt = [w.sb(f"zt{i}", [P, C, GT], F32R) for i in "hl"]
        ph = [w.sb(f"ph{i}", [PT, J, D], F32R) for i in "hl"]
        gz = w.sb("gz", [PT, 2, 2 * P])
        half = w.sb("half", [PT, 2, D])
        phk = w.sb("phk", [PT, 2, D])
        phq, pout = w.sb("phq", [PT, J, D]), w.sb("pout", [PT, J, D])
        stat, mv = w.sb("stat", [PT, J, 6]), w.sb("mv", [PT, J, 2])
        var, rstd = w.sb("var", [PT, J]), w.sb("rstd", [PT, J])
        zb_raw, zb = w.sb("zb_raw", [P, 2, C]), w.sb("zb", [P, 2, C])
        hit = w.sb("hit", [PT, E // 2])
        count = w.sb("count", [PT, 5])
        rank, below, rank_i = w.sb("rank", [PT, 1]), w.sb("below", [PT, 1]), w.sb("rank_i", [PT, 1], I32)
        absent, no_dst = w.sb("absent", [PT, N // PT], I32), w.sb("no_dst", [1, 2])
        edges_in, cast, filled, fills_out, rows_in = (w.sem(n) for n in ("edges_in", "cast", "filled", "fills_out", "rows_in"))
        counted, edge_step, edge_ready, scattered = (w.sem(n) for n in ("counted", "edge_step", "edge_ready", "scattered"))
        ring = [w.ps(f"ring{i}") for i in range(4)]
        k_full, p1_full, sk_full, q_full, t_full = (w.sem(n) for n in ("k_full", "p1_full", "sk_full", "q_full", "t_full"))
        small_in, g_zero, g_in, g_hi_done, g_lo_done = w.sem("small_in"), w.sem("g_zero"), w.sem("g_in"), w.sem("g_hi_done"), w.sem("g_lo_done")
        zb_done, kacc_zero = w.sem("zb_done"), w.sem("kacc_zero")
        x_in, stats, aggr, var_done, rstd_done, xn_done = (w.sem(n) for n in ("x_in", "stats", "aggr", "var_done", "rstd_done", "xn_done"))
        xs_hi, xs_lo, t_hi, t_done, k_hi, k_done, q_hi, q_done = (w.sem(n) for n in (
            "xs_hi", "xs_lo", "t_hi", "t_done", "k_hi", "k_done", "q_hi", "q_done"))
        gz_done, half_done, phi_done, ph_hi, ph_lo, kacc_done, acc_done, p1_done = (w.sem(n) for n in (
            "gz_done", "half_done", "phi_done", "ph_hi", "ph_lo", "kacc_done", "acc_done", "p1_done"))
        xn_out = w.sem("xn_out")
        p_out = [w.sem(f"p_out{i}") for i in range(2)]
        q_out = [w.sem(f"q_out{i}") for i in range(2)]
        JK, JP, JSK, JQ, JT, JSQ = 0, 4, 8, 16, 20, 24

        def wait_emptied(pe, g, job):
            if isinstance(g, int) and g == 0 and job < JP:
                pe.wait_ge(t_done, job + 1)
                return
            if job < JP:
                g, job = g - 1, job + JSQ + 8
            if isinstance(g, int) and g == G - 1 and JSQ <= job < JSQ + 4:
                job -= 4
            last = job - 4
            if last >= JSQ:
                pe.wait_ge(half_done, 4 * J * g + 2 * J + last - JSQ + 1)
            elif last >= JT:
                pe.wait_ge(t_done, J * (g + 1) + last - JT + 1)
            elif last >= JQ:
                pe.wait_ge(q_done, C * g + last - JQ + 1)
            elif last >= JSK:
                pe.wait_ge(half_done, 4 * J * g + last - JSK + 1)
            elif last >= JP:
                pe.wait_ge(p1_done, J * g + last - JP + 1)
            else:
                pe.wait_ge(k_done, C * g + last + 1)

        def groups(eng, body):
            body(0)
            with eng.Fori(1, G - 1) as g:
                body(g)
            body(G - 1)

        def is_last(g):
            return isinstance(g, int) and g == G - 1

        block = w.block()

        @block.sync
        def _(sp):
            load_group(sp, x, arg["x"], 0, x_in)
            wt.load(sp, 0, 1)
            for i, name in enumerate(("gamma_k", "beta_k", "gamma_q", "beta_q")):
                sp.dma_start(gam[:, i:i + 1], arg["L0_mix_" + name].rearrange("(o n) -> o n", o=1).partition_broadcast(P)).then_inc(small_in, 16)
            for i, name in enumerate(("bk", "bq")):
                sp.dma_start(zb_raw[:, i, :], arg["L0_mix_" + name].rearrange("(c p) -> p c", p=P)).then_inc(small_in, 16)
            wt.load(sp, 1, 2)
            sp.wait_ge(g_zero, 1)
            for i, z in enumerate("kq"):
                for m in range(2):
                    for d in range(2):
                        sp.dma_start(g_raw[d * R:(d + 1) * R, i, m * P + d * R:m * P + (d + 1) * R],
                                     arg[f"L0_mix_{z}G{m + 1}"]).then_inc(g_in, 16)
            sp.dma_start(k.drow[0:PT, 0:E].bitcast(I32), arg["dst"].rearrange("(o e) -> o e", o=1).partition_broadcast(PT)).then_inc(edges_in, 16)
            sp.dma_start(k.edge_dst[:, :].bitcast(I32), arg["dst"].rearrange("(t p) -> p t", p=PT)).then_inc(edges_in, 16)
            sp.dma_start(k.edge_src[:, :].bitcast(I32), arg["src"].rearrange("(t p) -> p t", p=PT)).then_inc(edges_in, 16)
            sp.wait_ge(filled, 2)
            sp.dma_start(k.slot_map[0:N, :].rearrange("(p q) o -> p (q o)", p=PT), absent[:, :]).then_inc(fills_out, 16)
            sp.dma_start(k.dst_sorted[E:E + 2, :].rearrange("(a e) o -> a (e o)", a=1), no_dst[:, :]).then_inc(fills_out, 16)
            wt.load(sp, 2)
            for l in range(3):
                sp.dma_start(k.bias[:, l, :], arg["L0_gnn_b"][l:l + 1, :].partition_broadcast(P)).then_inc(rows_in, 16)
            sp.dma_start(k.bp[:, :], arg["L0_mix_bp"].rearrange("(o n) -> o n", o=1).partition_broadcast(P)).then_inc(rows_in, 16)

            def body(g):
                sp.wait_ge(xn_done, J * (g + 1))
                alone(sp, w.sp_waited)
                if not is_last(g):
                    load_group(sp, x, arg["x"], g + 1, x_in)
                for i in range(2):
                    store_pair(sp, k.hs[0], xn, g, 2 * i, xn_out)
                for i in range(2):
                    sp.wait_ge(p1_done, J * g + 2 * i + 2)
                    alone(sp, w.sp_waited)
                    store_pair(sp, k.ps[0], pout, g, 2 * i, p_out[i])
                for i in range(2):
                    sp.wait_ge(phi_done, 2 * J * g + J + 2 * i + 2)
                    alone(sp, w.sp_waited)
                    store_pair(sp, k.phi_q, phq, g, 2 * i, q_out[i])
            groups(sp, body)
            sp.wait_ge(fills_out, 32)
            sp.wait_ge(rows_in, 64)
            sp.wait_ge(xn_out, 64 * G)
            for i in range(2):
                sp.wait_ge(p_out[i], 32 * G)
                sp.wait_ge(q_out[i], 32 * G)

        @block.gpsimd
        def _(pool):
            pool.memset(g_raw[:, :, :], 0.0).then_inc(g_zero, 1)
            pool.memset(absent[:, :], E).then_inc(filled, 1)
            pool.memset(no_dst[:, :], -1.0).then_inc(filled, 1)
            pool.memset(k.kacc[:, :], 0.0).then_inc(kacc_zero, 1)
            pool.wait_ge(kacc_zero, 1)
            def rstds(g):
                pool.wait_ge(aggr, J * (g + 1))
                alone(pool, w.pool_waited)
                pool.tensor_scalar(var[:, :], mv[:, :, 1], LN_EPS, None, ALU.add).then_inc(var_done, 1)
                pool.wait_ge(var_done, g + 1)
                pool.tensor_tensor(rstd[:, :], var[:, :], k.minus_half[0:PT, 0:J], ALU.pow).then_inc(rstd_done, 1)

            def body(g):
                for j in range(J):
                    pool.wait_ge(xn_done, J * g + j + 1)
                    need(pool, acc_done, J * (g - 1) + j + 1)
                    alone(pool, w.pool_waited)
                    pool.tensor_copy(xs[0][:, j, :], xn[:, j, :]).then_inc(xs_hi, 1)
                    pool.wait_ge(xs_hi, J * g + j + 1)
                    pool.tensor_tensor(xs[1][:, j, :], xn[:, j, :], xs[0][:, j, :].bitcast(F32), ALU.subtract).then_inc(xs_lo, 1)
                if not is_last(g):
                    rstds(g + 1)
                for j in range(J):
                    pool.wait_ge(phi_done, 2 * J * g + j + 1)
                    need(pool, acc_done, J * (g - 1) + j + 1)
                    alone(pool, w.pool_waited)
                    pool.tensor_copy(ph[0][:, j, :], phk[:, j % 2, :]).then_inc(ph_hi, 1)
                    pool.wait_ge(ph_hi, J * g + j + 1)
                    pool.tensor_tensor(ph[1][:, j, :], phk[:, j % 2, :], ph[0][:, j, :].bitcast(F32), ALU.subtract).then_inc(ph_lo, 1)
                    need(pool, kacc_done, J * g + j)
                    pool.tensor_tensor(k.kacc[:, :], k.kacc[:, :], phk[:, j % 2, :], ALU.add).then_inc(kacc_done, 1)
                pool.wait_ge(edge_ready, 4 * (g + 1))
                alone(pool, w.pool_waited)
                at = bass.IndirectOffsetOnAxis(ap=rank_i[:, :], axis=0)
                pool.indirect_dma_start(out=k.edges_sorted[:, :], out_offset=at, in_=k.edge[:, :], in_offset=None).then_inc(scattered, 16)
                pool.indirect_dma_start(out=k.dst_sorted[:, :], out_offset=at, in_=k.edge[:, 1:2], in_offset=None).then_inc(scattered, 16)
            rstds(0)
            groups(pool, body)
            pool.wait_ge(scattered, 32 * G)

        @block.tensor
        def _(pe):
            def turn(g, at):
                for j in range(J):
                    if j == 0:
                        pe.wait_ge(xn_done, J * (g + 1))
                    if at is not None:
                        wait_emptied(pe, at, JT + j)
                    for c in range(C):
                        mm = pe.transpose(ring[j][:, c * PT:(c + 1) * PT], xn[:, j, c * P:(c + 1) * P], k.ident[0:PT, 0:PT])
                    mm.then_inc(t_full, 1)

            def project(g, job, i, filled):
                for m in range(C):
                    wait_emptied(pe, g, job + m)
                    for c in range(C):
                        mm = three(pe, ring[m][:, 0:GT], wt.hi[i][:, c, m * P:(m + 1) * P], wt.lo[i][:, c, m * P:(m + 1) * P],
                                   xt[0][:, c, :], xt[1][:, c, :], c == 0, c == C - 1)
                    mm.then_inc(filled, 1)

            def sketch(g, job, i):
                for j in range(J):
                    for b in range(2):
                        n = (2 * j + b) % 4
                        wait_emptied(pe, g, job + 2 * j + b)
                        for a in range(2):
                            c = 2 * b + a
                            mm = three(pe, ring[n][0:PT, a * 2 * P:(a + 1) * 2 * P], zt[0][:, c, j * PT:(j + 1) * PT],
                                       zt[1][:, c, j * PT:(j + 1) * PT], g_hi[:, i, :], g_lo[:, i, :], True, True)
                        mm.then_inc(sk_full, 1)

            def body(g):
                pe.wait_ge(t_done, J * (g + 1))
                if isinstance(g, int) and g == 0:
                    wt.wait(pe, WK)
                project(g, JK, WK, k_full)
                if isinstance(g, int) and g == 0:
                    wt.wait(pe, WS)
                for j in range(J):
                    wait_emptied(pe, g, JP + j)
                    for c in range(C):
                        mm = three(pe, ring[j][0:PT, :], xt[0][:, c, j * PT:(j + 1) * PT], xt[1][:, c, j * PT:(j + 1) * PT],
                                   wt.hi[WS][:, c, :], wt.lo[WS][:, c, :], c == 0, c == C - 1)
                    mm.then_inc(p1_full, 1)
                if isinstance(g, int) and g == 0:
                    pe.wait_ge(g_lo_done, 1)
                pe.wait_ge(k_done, C * (g + 1))
                sketch(g, JSK, 0)
                if isinstance(g, int) and g == 0:
                    wt.wait(pe, WQ)
                project(g, JQ, WQ, q_full)
                for j in range(J):
                    pe.wait_ge(ph_lo, J * g + j + 1)
                    pe.wait_ge(xs_lo, J * g + j + 1)
                    for c in range(C):
                        mm = three(pe, acc[c][:, :], ph[0][:, j, c * P:(c + 1) * P], ph[1][:, j, c * P:(c + 1) * P],
                                   xs[0][:, j, :], xs[1][:, j, :], isinstance(g, int) and g == 0 and j == 0,
                                   is_last(g) and j == J - 1)
                    mm.then_inc(acc_done, 1)
                if not is_last(g):
                    turn(g + 1, g)
                pe.wait_ge(q_done, C * (g + 1))
                sketch(g, JSQ, 1)
            turn(0, None)
            groups(pe, body)

        def sketch_at(g, q, j):
            return 2 * J * g + J * q + j

        @block.scalar
        def _(act):
            def turn(g):
                for j in range(J):
                    act.wait_ge(t_full, J * g + j + 1)
                    act.activation(xt[0][:, :, j * PT:(j + 1) * PT], ring[j][:, 0:GT].rearrange("p (c t) -> p c t", c=C),
                                   ACT.Copy).then_inc(t_hi, 1)

            def project(g, i, filled, done):
                for m in range(C):
                    act.wait_ge(filled, C * g + m + 1)
                    act.activation(zt[0][:, m, :], ring[m][:, 0:GT], ACT.Identity, bias=zb[:, i, m:m + 1]).then_inc(done, 1)

            def sketch(g, q):
                def square(j):
                    at = sketch_at(g, q, j)
                    act.wait_ge(half_done, 2 * at + 2)
                    if q:
                        if j % 2 == 0:
                            need(act, q_out[j // 2], 32 * g)
                        out = phq[:, j, :]
                    else:
                        need(act, kacc_done, J * g + j - 1)
                        out = phk[:, j % 2, :]
                    act.activation(out, half[:, j % 2, :], ACT.Square, scale=float(R) ** -0.5).then_inc(phi_done, 1)
                for j in range(J):
                    for b in range(2):
                        n = (2 * j + b) % 4
                        act.wait_ge(sk_full, 2 * sketch_at(g, q, j) + b + 1)
                        need(act, half_done, 2 * sketch_at(g, q, j) + b - 1)
                        act.activation(gz[:, b, :].rearrange("p (a r) -> p a r", a=2),
                                       ring[n][0:PT, :].rearrange("p (a m r) -> p a m r", a=2, m=2)[:, :, 0, :],
                                       ACT.Copy).then_inc(gz_done, 1)
                    if j:
                        square(j - 1)
                square(J - 1)

            def body(g):
                if isinstance(g, int) and g == 0:
                    wt.split_hi(act, WS)
                project(g, 0, k_full, k_hi)
                if isinstance(g, int) and g == 0:
                    act.wait_ge(g_in, 128)
                    act.activation(g_hi[:, :, :], g_raw[:, :, :], ACT.Copy).then_inc(g_hi_done, 1)
                    wt.split_hi(act, WQ)
                for j in range(J):
                    act.wait_ge(p1_full, J * g + j + 1)
                    if j % 2 == 0:
                        need(act, p_out[j // 2], 32 * g)
                    act.activation(pout[:, j, :], ring[j][0:PT, :], ACT.Copy).then_inc(p1_done, 1)
                sketch(g, 0)
                project(g, 1, q_full, q_hi)
                if not is_last(g):
                    turn(g + 1)
                sketch(g, 1)
            act.wait_ge(small_in, 96)
            wt.split_hi(act, WK)
            act.wait_ge(zb_done, 4)
            turn(0)
            groups(act, body)

        @block.vector
        def _(dve):
            def norm(g):
                dve.wait_ge(x_in, 32 * (g + 1))
                for j in range(J):
                    dve.bn_stats(stat[:, j, :], x[:, j, :]).then_inc(stats, 1)
                    if j:
                        dve.wait_ge(stats, J * g + j)
                        alone(dve, w.dve_waited)
                        dve.bn_aggr(mv[:, j - 1, :], stat[:, j - 1, :]).then_inc(aggr, 1)
                dve.wait_ge(stats, J * (g + 1))
                alone(dve, w.dve_waited)
                dve.bn_aggr(mv[:, J - 1, :], stat[:, J - 1, :]).then_inc(aggr, 1)
                dve.wait_ge(rstd_done, g + 1)
                need(dve, xn_out, 64 * g)
                need(dve, xs_lo, J * g)
                need(dve, t_hi, J * g)
                for j in range(J):
                    dve.tensor_scalar(xn[:, j, :], x[:, j, :], mv[:, j, 0:1], rstd[:, j:j + 1], ALU.subtract, ALU.mult).then_inc(xn_done, 1)

            def turn(g):
                for j in range(J):
                    dve.wait_ge(t_hi, J * g + j + 1)
                    dve.tensor_tensor(xt[1][:, :, j * PT:(j + 1) * PT], ring[j][:, 0:GT].rearrange("p (c t) -> p c t", c=C),
                                      xt[0][:, :, j * PT:(j + 1) * PT].bitcast(F32), ALU.subtract).then_inc(t_done, 1)

            def project(g, i, hi_done, done):
                for m in range(C):
                    dve.wait_ge(hi_done, C * g + m + 1)
                    dve.scalar_tensor_tensor(zt[1][:, m, :], ring[m][:, 0:GT], zb[:, i, m:m + 1], zt[0][:, m, :].bitcast(F32),
                                             ALU.add, ALU.subtract).then_inc(done, 1)

            def sketch(g, q):
                for j in range(J):
                    at = sketch_at(g, q, j)
                    for b in range(2):
                        n = (2 * j + b) % 4
                        dve.wait_ge(gz_done, 2 * at + b + 1)
                        if b == 0:
                            need(dve, phi_done, at - 1)
                        dve.tensor_tensor(half[:, j % 2, b * 2 * P:(b + 1) * 2 * P].rearrange("p (a r) -> p a r", a=2),
                                          ring[n][0:PT, :].rearrange("p (a m r) -> p a m r", a=2, m=2)[:, :, 1, :],
                                          gz[:, b, :].rearrange("p (a r) -> p a r", a=2), ALU.mult).then_inc(half_done, 1)

            def rank_edges(g):
                d, low, half_row = k.edge_dst[:, bass.ds(g, 1)], k.edge_low[:, bass.ds(g, 1)], E // 2
                done = 6 * g
                for i in range(4):
                    need(dve, counted, done + i)
                    dve.tensor_scalar(hit[:, :], k.drow[0:PT, (i % 2) * half_row:(i % 2 + 1) * half_row], (d, low)[i // 2], 0.0,
                                      ALU.is_lt, ALU.add, accum_out=count[:, i:i + 1]).then_inc(counted, 1)
                own = k.drow[0:PT, bass.ds(g * PT, PT)]
                dve.wait_ge(counted, done + 4)
                dve.scalar_tensor_tensor(hit[:, 0:PT], own, d, k.earlier[:, :], ALU.is_equal, ALU.mult,
                                         accum_out=count[:, 4:5]).then_inc(counted, 1)
                dve.wait_ge(counted, done + 5)
                dve.tensor_scalar(own, own, -0.5, None, ALU.add).then_inc(counted, 1)
                need(dve, scattered, 32 * g)
                dve.scalar_tensor_tensor(rank[:, :], count[:, 0:1], count[:, 1:2], count[:, 4:5], ALU.add, ALU.add).then_inc(edge_step, 1)
                dve.scalar_tensor_tensor(below[:, :], count[:, 2:3], -1.0, count[:, 3:4], ALU.add, ALU.add).then_inc(edge_step, 1)
                dve.tensor_copy(k.edge[:, 0:1], k.edge_src[:, bass.ds(g, 1)]).then_inc(edge_ready, 1)
                dve.tensor_copy(k.edge[:, 1:2], d).then_inc(edge_ready, 1)
                dve.wait_ge(edge_step, 2 * g + 2)
                dve.tensor_tensor(k.edge[:, 2:3], rank[:, :], below[:, :], ALU.subtract).then_inc(edge_ready, 1)
                dve.tensor_copy(rank_i[:, :], rank[:, :]).then_inc(edge_ready, 1)

            def body(g):
                if isinstance(g, int) and g == 0:
                    wt.split_lo(dve, WS)
                project(g, 0, k_hi, k_done)
                if isinstance(g, int) and g == 0:
                    dve.wait_ge(g_hi_done, 1)
                    dve.tensor_tensor(g_lo[:, :, :], g_raw[:, :, :], g_hi[:, :, :].bitcast(F32), ALU.subtract).then_inc(g_lo_done, 1)
                    wt.split_lo(dve, WQ)
                if not is_last(g):
                    norm(g + 1)
                sketch(g, 0)
                project(g, 1, q_hi, q_done)
                if isinstance(g, int) and g == 0:
                    dve.wait_ge(edges_in, 48)
                    dve.tensor_copy(k.drow[0:PT, 0:E], k.drow[0:PT, 0:E].bitcast(I32)).then_inc(cast, 1)
                    dve.tensor_copy(k.edge_dst[:, :], k.edge_dst[:, :].bitcast(I32)).then_inc(cast, 1)
                    dve.tensor_copy(k.edge_src[:, :], k.edge_src[:, :].bitcast(I32)).then_inc(cast, 1)
                    dve.wait_ge(cast, 3)
                    dve.tensor_scalar(k.edge_low[:, :], k.edge_dst[:, :], -0.75, None, ALU.add).then_inc(cast, 1)
                    dve.wait_ge(cast, 4)
                rank_edges(g)
                if not is_last(g):
                    turn(g + 1)
                sketch(g, 1)
            norm(0)
            dve.wait_ge(small_in, 96)
            for i in range(2):
                dve.tensor_scalar(zb[:, i, :], zb_raw[:, i, :], gam[:, 2 * i:2 * i + 1], gam[:, 2 * i + 1:2 * i + 2],
                                  ALU.mult, ALU.add).then_inc(zb_done, 2)
            turn(0)
            wt.split_lo(dve, WK)
            groups(dve, body)


def build_neighbours(nc, k, arg, l, N, E):
    T = E // PT
    PE1 = PT + 1
    with Pass(nc, f"z{l}") as w:
        ahead = Weights(w, [arg["L0_gnn_W_self"][l + 1]], kept=k.w_self) if l < 2 else None
        got, index = w.sb("got", [PT, J, D]), w.sb("index", [PT, J], I32)
        split = [w.sb(f"split{i}", [PT, 2, D], F32R) for i in "hl"]
        same = w.sb("same", [PT, 2, PE1], F32R)
        first_run = w.sb("first_run", [P, 2, PE1])
        agg = w.sb("agg", [P, 2, C, PE1])
        aggs = [w.sb(f"aggs{i}", [P, 2, C, PE1], F32R) for i in "hl"]
        z = w.sb("z", [PT, 2, D])
        pagg = [w.ps(f"pagg{i}") for i in range(2)]
        pz = [w.ps(f"pz{i}") for i in range(2)]
        index_done, gathered = w.sem("index_done"), [w.sem(f"gathered{i}") for i in range(J)]
        split_hi, split_lo, same_done, first_done, sum_full, carry_zero, agg_done, agg_hi, agg_lo, z_full, z_done = (w.sem(n) for n in (
            "split_hi", "split_lo", "same_done", "first_done", "sum_full", "carry_zero", "agg_done", "agg_hi", "agg_lo", "z_full", "z_done"))
        slot = w.sb("slot", [PT, 2], I32)
        slot_done, slot_out, slots_in = w.sem("slot_done"), w.sem("slot_out"), w.sem("slots_in")
        z_out = [w.sem(f"z_out{i}") for i in range(2)]
        block = w.block()

        def ok(n):
            return not isinstance(n, int) or 0 <= n < T

        def steps(eng, body):
            tile_steps(eng, body, -J, T, T // J, 1)

        @block.sync
        def _(sp):
            def body(s, j):
                if ahead and isinstance(s, int) and s == 1:
                    ahead.load(sp)
                if l == 0 and isinstance(s, int) and s == T - 1:
                    sp.wait_ge(slot_out, 16 * T)
                    sp.dma_start(k.slots[:, :, :], k.slot_map[0:N, :].rearrange("(g p j) o -> p g (j o)", p=PT, j=J)).then_inc(slots_in, 16)
                if ok(s):
                    sp.wait_ge(z_done, s + 1)
                    alone(sp, w.sp_waited)
                    for a, b in ((0, PA), (PA, PT)):
                        sp.dma_start(k.z[bass.ds(s * PT + a, b - a), :], z[a:b, j % 2, :]).then_inc(z_out[j % 2], 16)
            steps(sp, body)
            for r in range(2):
                sp.wait_ge(z_out[r], 16 * T)
            if l == 0:
                sp.wait_ge(slots_in, 16)

        @block.gpsimd
        def _(pool):
            def body(s, j):
                n, jn = s + 2, (j + 2) % J
                if ok(n):
                    pool.wait_ge(split_hi, n + 1)
                    need(pool, sum_full, n - 1)
                    pool.tensor_tensor(split[1][:, j % 2, :], got[:, jn, :], split[0][:, j % 2, :].bitcast(F32), ALU.subtract).then_inc(split_lo, 1)
                n = s + J
                if ok(n):
                    need(pool, split_lo, n - J + 1)
                    alone(pool, w.pool_waited)
                    pool.tensor_copy(index[:, j:j + 1], k.src[:, bass.ds(n, 1)]).then_inc(index_done, 1)
                    pool.wait_ge(index_done, n + 1)
                    alone(pool, w.pool_waited)
                    pool.indirect_dma_start(out=got[:, j, :], out_offset=None, in_=k.hs[l][:, :],
                                            in_offset=bass.IndirectOffsetOnAxis(ap=index[:, j:j + 1], axis=0)).then_inc(gathered[j], 16)
                n = s + 3
                if l == 0 and ok(n):
                    need(pool, slot_out, 16 * n)
                    alone(pool, w.pool_waited)
                    pool.tensor_copy(slot[:, :], k.slot_rows[:, bass.ds(n, 1), :].rearrange("p t c -> p (t c)")).then_inc(slot_done, 1)
                    pool.wait_ge(slot_done, n + 1)
                    alone(pool, w.pool_waited)
                    pool.indirect_dma_start(out=k.slot_map[:, :], in_offset=None, in_=slot[:, 1:2],
                                            out_offset=bass.IndirectOffsetOnAxis(ap=slot[:, 0:1], axis=0)).then_inc(slot_out, 16)
            steps(pool, body)

        @block.scalar
        def _(act):
            def body(s, j):
                n, jn = s + 2, (j + 2) % J
                if ok(n):
                    act.wait_ge(gathered[jn], 16 * ((n - jn) // J + 1))
                    need(act, sum_full, n - 1)
                    act.activation(split[0][:, j % 2, :], got[:, jn, :], ACT.Copy).then_inc(split_hi, 1)
                if ahead and isinstance(s, int) and s >= T - C:
                    ahead.split_chunk_hi(act, s - (T - C))
                n, r = s + 1, slot2(j + 1)
                if ok(n):
                    act.wait_ge(agg_done, C * (n + 1))
                    need(act, z_full, n - 1)
                    act.activation(aggs[0][:, r, :, :], agg[:, r, :, :], ACT.Copy).then_inc(agg_hi, 1)
            steps(act, body)

        @block.tensor
        def _(pe):
            def body(s, j):
                n, r = s + 1, slot2(j + 1)
                if ok(n):
                    pe.wait_ge(same_done, n + 1)
                    pe.wait_ge(split_lo, n + 1)
                    need(pe, agg_done, C * (n - 1))
                    for c in range(C):
                        for i in range(2):
                            mm = pe.matmul(pagg[r][:, c * PE1:(c + 1) * PE1], split[i][:, r, c * P:(c + 1) * P], same[:, r, :],
                                           start=(i == 0), stop=(i == 1))
                    mm.then_inc(sum_full, 1)
                r = j % 2
                if ok(s):
                    pe.wait_ge(agg_lo, s + 1)
                    need(pe, z_done, s - 1)
                    for c in range(C):
                        mm = three(pe, pz[r][0:PT, :], aggs[0][:, r, c, 0:PT], aggs[1][:, r, c, 0:PT], k.w_neigh[0][:, c, :], k.w_neigh[1][:, c, :],
                                   c == 0, c == C - 1)
                    mm.then_inc(z_full, 1)
            steps(pe, body)

        @block.vector
        def _(dve):
            def body(s, j):
                n, r = s + 1, slot2(j + 1)
                if ok(n):
                    dve.wait_ge(sum_full, n + 1)
                    dve.wait_ge(first_done, n + 1)
                    need(dve, agg_done, C * n)
                    need(dve, agg_lo, n - 1)
                    for c in range(C):
                        dve.scalar_tensor_tensor(agg[:, r, c, :], first_run[:, r, :], agg[:, 1 - r, c, PT:PE1], pagg[r][:, c * PE1:(c + 1) * PE1],
                                                 ALU.mult, ALU.add).then_inc(agg_done, 1)
                if ahead and isinstance(s, int) and s >= T - C:
                    ahead.split_chunk_lo(dve, s - (T - C))
                m, q = s + 2, j % 2
                if ok(m):
                    need(dve, agg_done, C * (m - 1))
                    need(dve, sum_full, m - 1)
                    dve.tensor_scalar(same[:, q, :], k.drow[0:PT, bass.ds(m * PT, PE1)], k.dst[:, bass.ds(m, 1)], None, ALU.is_equal).then_inc(same_done, 1)
                    dve.tensor_scalar(first_run[:, q, :], k.drow[:, bass.ds(m * PT, PE1)], k.drow[:, bass.ds(m * PT, 1)], None, ALU.is_equal).then_inc(first_done, 1)
                if ok(n):
                    dve.wait_ge(agg_hi, n + 1)
                    dve.tensor_tensor(aggs[1][:, r, :, :], agg[:, r, :, :], aggs[0][:, r, :, :].bitcast(F32), ALU.subtract).then_inc(agg_lo, 1)
                if ok(s):
                    dve.wait_ge(z_full, s + 1)
                    need(dve, z_out[q], 32 * ((s - q) // 2))
                    dve.scalar_tensor_tensor(z[:, q, :], pz[q][0:PT, :], k.rdeg[:, bass.ds(s, 1)], k.bias[0:PT, l, :], ALU.mult, ALU.add).then_inc(z_done, 1)
            dve.memset(agg[:, 1, :, :], 0.0).then_inc(carry_zero, 1)
            dve.wait_ge(carry_zero, 1)
            steps(dve, body)


def build_layer(nc, k, arg, l, N, E):
    G = N // GT
    NT = G * J
    SUM, NORM = 3, 2
    with Pass(nc, f"l{l}") as w:
        ahead = Weights(w, [arg["L0_gnn_W_neigh"][l]], kept=k.w_neigh)
        pin, rows = w.sb("pin", [PT, J, D]), w.sb("rows", [PT, J, D])
        zin, index = w.sb("zin", [PT, J, D]), w.sb("index", [PT, J], I32)
        junk = w.sb("junk", [PT, D])
        ss, floor, rnorm = w.sb("ss", [PT, J]), w.sb("floor", [PT, J]), w.sb("rnorm", [PT, J])
        h = w.sb("h", [PT, J, D])
        ht = [w.sb(f"ht{i}", [P, 2, C, PT], F32R) for i in "hl"]
        pout = w.sb("pout", [PT, J, D])
        pt = [w.ps(f"pt{i}") for i in range(2)]
        pp = [w.ps(f"pp{i}") for i in range(2)]
        p_in = [w.sem(f"p_in{i}") for i in range(2)]
        z_in = [w.sem(f"z_in{i}") for i in range(J)]
        h_out = [w.sem(f"h_out{i}") for i in range(2)]
        p_out = [w.sem(f"p_out{i}") for i in range(2)]
        prefilled, index_done, sum_done, ss_done, floor_done, rnorm_done, h_done = (w.sem(n) for n in (
            "prefilled", "index_done", "sum_done", "ss_done", "floor_done", "rnorm_done", "h_done"))
        t_full, t_hi, t_lo, p_full, p_done = (w.sem(n) for n in ("t_full", "t_hi", "t_lo", "p_full", "p_done"))
        block = w.block()

        def group(n, j):
            return (n - j) // J

        def ok(n):
            return not isinstance(n, int) or 0 <= n < NT

        def steps(eng, body):
            tile_steps(eng, body, -SUM - 4, NT, G)

        @block.sync
        def _(sp):
            def body(s, j):
                if isinstance(s, int) and s == 0:
                    ahead.load(sp)
                n, jn = s + SUM, (j + SUM) % J
                if ok(n) and jn % 2 == 1 and ok(n + J):
                    sp.wait_ge(sum_done, n + 1)
                    alone(sp, w.sp_waited)
                    load_pair(sp, pin, k.ps[l - 1], group(n, jn) + 1, jn - 1, p_in[jn // 2])
                n, jn = s + NORM, (j + NORM) % J
                if ok(n) and jn % 2 == 1:
                    sp.wait_ge(h_done, n + 1)
                    alone(sp, w.sp_waited)
                    store_pair(sp, k.hs[l], h, group(n, jn), jn - 1, h_out[jn // 2])
                if ok(s) and j % 2 == 1:
                    sp.wait_ge(p_done, s + 1)
                    alone(sp, w.sp_waited)
                    store_pair(sp, k.ps[l], pout, group(s, j), j - 1, p_out[j // 2])
            for i in range(2):
                load_pair(sp, pin, k.ps[l - 1], 0, 2 * i, p_in[i])
            steps(sp, body)
            for i in range(2):
                sp.wait_ge(h_out[i], 32 * G)
                sp.wait_ge(p_out[i], 32 * G)

        @block.gpsimd
        def _(pool):
            def gather(n, j):
                need(pool, sum_done, n - J + 1)
                alone(pool, w.pool_waited)
                pool.tensor_copy(index[:, j:j + 1], k.slots[:, :, :].rearrange("p g j -> p (g j)")[:, bass.ds(n, 1)]).then_inc(index_done, 1)
                pool.wait_ge(prefilled, n + 1)
                pool.wait_ge(index_done, n + 1)
                alone(pool, w.pool_waited)
                pool.indirect_dma_start(out=zin[:, j, :], out_offset=None, in_=k.z[:, :],
                                        in_offset=bass.IndirectOffsetOnAxis(ap=index[:, j:j + 1], axis=0),
                                        bounds_check=E - 1, oob_is_err=False).then_inc(z_in[j], 16)

            def body(s, j):
                n, jn = s + NORM, (j + NORM) % J
                if ok(n):
                    pool.wait_ge(ss_done, n + 1)
                    alone(pool, w.pool_waited)
                    pool.tensor_scalar(floor[:, jn:jn + 1], ss[:, jn:jn + 1], NORM_EPS2, None, ALU.max).then_inc(floor_done, 1)
                    pool.wait_ge(floor_done, n + 1)
                    pool.tensor_tensor(rnorm[:, jn:jn + 1], floor[:, jn:jn + 1], k.minus_half[0:PT, 0:1], ALU.pow).then_inc(rnorm_done, 1)
                if ok(s + 6) and not (isinstance(s, int) and s + 6 < J):
                    gather(s + 6, (j + 6) % J)
            for j in range(J):
                gather(j, j)
            steps(pool, body)

        @block.vector
        def _(dve):
            def body(s, j):
                n, jn = s + SUM, (j + SUM) % J
                if ok(n):
                    dve.wait_ge(p_in[jn // 2], 32 * (group(n, jn) + 1))
                    dve.wait_ge(z_in[jn], 16 * (group(n, jn) + 1))
                    need(dve, h_done, n - J + 1)
                    dve.tensor_tensor(rows[:, jn, :], pin[:, jn, :], zin[:, jn, :], ALU.add).then_inc(sum_done, 1)
                    dve.wait_ge(sum_done, n + 1)
                    dve.scalar_tensor_tensor(junk[:, :], rows[:, jn, :], 0.0, rows[:, jn, :], ALU.max, ALU.mult,
                                             accum_out=ss[:, jn:jn + 1]).then_inc(ss_done, 1)
                if isinstance(s, int) and 0 <= s - (NT - 2 * J) < C:
                    ahead.split_chunk_lo(dve, s - (NT - 2 * J))
                m = s + 1
                if ok(m):
                    r = (j + 1) % 2
                    dve.wait_ge(t_hi, m + 1)
                    dve.tensor_tensor(ht[1][:, r, :, :].rearrange("p c t -> p (c t)"), pt[r][:, 0:GT],
                                      ht[0][:, r, :, :].rearrange("p c t -> p (c t)").bitcast(F32), ALU.subtract).then_inc(t_lo, 1)
            steps(dve, body)

        @block.scalar
        def _(act):
            def prefill(n, j):
                need(act, sum_done, n - J + 1)
                act.activation(zin[:, j, :], k.bias[0:PT, l - 1, :], ACT.Copy).then_inc(prefilled, 1)

            def body(s, j):
                if ok(s + 7) and not (isinstance(s, int) and s + 7 < J):
                    prefill(s + 7, (j + 7) % J)
                n, jn = s + NORM, (j + NORM) % J
                if ok(n):
                    act.wait_ge(rnorm_done, n + 1)
                    need(act, t_full, n - J + 1)
                    need(act, h_out[jn // 2], 32 * group(n, jn))
                    act.activation(h[:, jn, :], rows[:, jn, :], ACT.Relu, scale=rnorm[:, jn:jn + 1]).then_inc(h_done, 1)
                if isinstance(s, int) and 0 <= s - (NT - 2 * J) < C:
                    ahead.split_chunk_hi(act, s - (NT - 2 * J))
                m = s + 1
                if ok(m):
                    r = (j + 1) % 2
                    act.wait_ge(t_full, m + 1)
                    need(act, p_full, m - 1)
                    act.activation(ht[0][:, r, :, :].rearrange("p c t -> p (c t)"), pt[r][:, 0:GT], ACT.Copy).then_inc(t_hi, 1)
                if ok(s):
                    act.wait_ge(p_full, s + 1)
                    need(act, p_out[j // 2], 32 * group(s, j))
                    act.activation(pout[:, j, :], pp[j % 2][0:PT, :], ACT.Copy).then_inc(p_done, 1)
            for j in range(J):
                prefill(j, j)
            steps(act, body)

        @block.tensor
        def _(pe):
            def body(s, j):
                m = s + 1
                if ok(m):
                    r, jm = (j + 1) % 2, (j + 1) % J
                    pe.wait_ge(h_done, m + 1)
                    need(pe, t_lo, m - 1)
                    for c in range(C):
                        mm = pe.transpose(pt[r][:, c * PT:(c + 1) * PT], h[:, jm, c * P:(c + 1) * P], k.ident[0:PT, 0:PT])
                    mm.then_inc(t_full, 1)
                if ok(s):
                    r = j % 2
                    pe.wait_ge(t_lo, s + 1)
                    need(pe, p_done, s - 1)
                    for c in range(C):
                        mm = three(pe, pp[r][0:PT, :], ht[0][:, r, c, :], ht[1][:, r, c, :], k.w_self[0][:, c, :], k.w_self[1][:, c, :], c == 0, c == C - 1)
                    mm.then_inc(p_full, 1)
            steps(pe, body)


def build_attention_matrix(nc, k, arg, acc, m_hi, m_lo, N, E):
    T = E // PT
    with Pass(nc, "m") as w:
        wv, wp = w.sb("wv", [P, C, D]), w.sb("wp", [P, C, D])
        bv = w.sb("bv", [P, C])
        a, at = w.sb("a", [P, C, D]), w.sb("at", [P, C, D])
        ksum = w.sb("ksum", [P, D])
        outer = w.sb("outer", [P, C, P])
        kv = w.sb("kv", [P, C, P])
        mf = w.sb("mf", [P, C, D])
        bank = [w.ps(f"bank{i}") for i in range(4)]
        loaded, a_done, sum_full, sum_done, t_full, t_done, zeroed, kv_full, outer_done, kv_done, m_full, m_done, hi_done, lo_done = (w.sem(n) for n in (
            "loaded", "a_done", "sum_full", "sum_done", "t_full", "t_done", "zeroed", "kv_full", "outer_done", "kv_done", "m_full",
            "m_done", "hi_done", "lo_done"))
        ahead = Weights(w, [arg["L0_gnn_W_neigh"][0]], kept=k.w_neigh)
        cols = w.sb("cols", [PT, T, 4])
        after = w.sb("after", [PT, T])
        own, is_last, inner, shift, target, row = (w.sb(n, [PT, T]) for n in ("own", "is_last", "inner", "shift", "target", "row"))
        own_i = w.sb("own_i", [PT, T], I32)
        edges_in, row_in, own_done, edge_step, target_done = (w.sem(n) for n in ("edges_in", "row_in", "own_done", "edge_step", "target_done"))
        block = w.block()

        @block.sync
        def _(sp):
            sp.dma_start(cols[:, :, :], k.edges_sorted.rearrange("(t p) c -> p t c", p=PT)).then_inc(edges_in, 16)
            sp.dma_start(after[:, :], k.dst_sorted[1:E + 1, :].rearrange("(t p) o -> p (t o)", p=PT)).then_inc(edges_in, 16)
            sp.dma_start(wv[:, :, :], arg["L0_mix_Wv"].rearrange("(c p) n -> p c n", p=P)).then_inc(loaded, 16)
            sp.dma_start(wp[:, :, :], arg["L0_mix_Wp"].rearrange("(c p) n -> p c n", p=P)).then_inc(loaded, 16)
            sp.dma_start(bv[:, :], arg["L0_mix_bv"].rearrange("(c p) -> p c", p=P)).then_inc(loaded, 16)
            sp.dma_start(k.drow[:, :], k.dst_sorted.rearrange("e o -> o e").partition_broadcast(P)).then_inc(row_in, 16)
            ahead.load(sp)
            sp.wait_ge(row_in, 16)

        @block.gpsimd
        def _(pool):
            pool.memset(kv[:, :, :], 0.0).then_inc(zeroed, 1)
            pool.iota(own_i[:, :], pattern=[[PT, T]], base=0, channel_multiplier=1).then_inc(own_done, 1)

        @block.scalar
        def _(act):
            for c in range(C):
                act.activation(a[:, c, :], acc[c][:, :], ACT.Copy).then_inc(a_done, 1)
            ahead.split_hi(act, 0)
            for c in range(C):
                act.wait_ge(m_full, c + 1)
                act.activation(mf[:, c, :], bank[c][:, :], ACT.Copy).then_inc(m_done, 1)
                act.wait_ge(m_done, c + 1)
                act.activation(m_hi[:, c, :], mf[:, c, :], ACT.Copy).then_inc(hi_done, 1)

        @block.tensor
        def _(pe):
            pe.matmul(bank[0][:, :], k.ones[0:PT, :], k.kacc[:, :], start=True, stop=True).then_inc(sum_full, 1)
            pe.wait_ge(a_done, C)
            pe.wait_ge(sum_done, 1)
            for f in range(C):
                for c in range(C):
                    mm = pe.transpose(bank[f][:, c * P:(c + 1) * P], a[:, c, f * P:(f + 1) * P], k.ident[:, :])
                mm.then_inc(t_full, 1)
            pe.wait_ge(loaded, 48)
            pe.wait_ge(t_done, C)
            for c in range(C):
                for f in range(C):
                    mm = pe.matmul(bank[c][:, 0:P], wv[:, f, c * P:(c + 1) * P], at[:, f, c * P:(c + 1) * P], start=f == 0, stop=f == C - 1)
                mm.then_inc(kv_full, 1)
            for c in range(C):
                pe.wait_ge(kv_done, 2 * C)
                pe.matmul(bank[c][:, :], kv[:, c, :], wp[:, c, :], start=True, stop=True).then_inc(m_full, 1)

        @block.vector
        def _(dve):
            dve.wait_ge(sum_full, 1)
            dve.tensor_copy(ksum[:, :], bank[0][:, :]).then_inc(sum_done, 1)
            dve.wait_ge(sum_done, 1)
            dve.tensor_copy(k.ksum[:, :], ksum[0:PT, :]).then_inc(sum_done, 1)
            for f in range(C):
                dve.wait_ge(t_full, f + 1)
                dve.tensor_copy(at[:, f, :], bank[f][:, :]).then_inc(t_done, 1)
            dve.wait_ge(edges_in, 32)
            dve.wait_ge(own_done, 1)
            dve.tensor_copy(own[:, :], own_i[:, :]).then_inc(edge_step, 1)
            dve.tensor_copy(k.src[:, :], cols[:, :, 0]).then_inc(edge_step, 1)
            dve.tensor_copy(k.dst[:, :], cols[:, :, 1]).then_inc(edge_step, 1)
            dve.reciprocal(k.rdeg[:, :], cols[:, :, 2]).then_inc(edge_step, 1)
            dve.tensor_tensor(inner[:, :], cols[:, :, 1], after[:, :], ALU.is_equal).then_inc(edge_step, 1)
            dve.tensor_copy(k.slot_rows[:, :, 1], own_i[:, :]).then_inc(edge_step, 1)
            dve.wait_ge(loaded, 48)
            for c in range(C):
                dve.tensor_scalar(outer[:, c, :], ksum[:, c * P:(c + 1) * P], bv[:, c:c + 1], None, ALU.mult).then_inc(outer_done, 1)
            dve.wait_ge(edge_step, 6)
            dve.tensor_scalar(is_last[:, :], inner[:, :], -1.0, 1.0, ALU.mult, ALU.add).then_inc(edge_step, 1)
            dve.scalar_tensor_tensor(shift[:, :], k.dst[:, :], float(-N), own[:, :], ALU.add, ALU.subtract).then_inc(edge_step, 1)
            dve.wait_ge(edge_step, 8)
            dve.tensor_tensor(target[:, :], shift[:, :], is_last[:, :], ALU.mult).then_inc(target_done, 1)
            dve.wait_ge(target_done, 1)
            dve.scalar_tensor_tensor(row[:, :], target[:, :], float(N), own[:, :], ALU.add, ALU.add).then_inc(edge_step, 1)
            dve.wait_ge(outer_done, C)
            dve.wait_ge(zeroed, 1)
            for c in range(C):
                dve.wait_ge(kv_full, c + 1)
                for b in range(2):
                    one = slice(b * R, (b + 1) * R)
                    dve.tensor_tensor(kv[one, c, one], bank[c][one, one], outer[one, c, one], ALU.add).then_inc(kv_done, 1)
            ahead.split_lo(dve, 0)
            for c in range(C):
                dve.wait_ge(hi_done, c + 1)
                dve.tensor_tensor(m_lo[:, c, :], mf[:, c, :], m_hi[:, c, :].bitcast(F32), ALU.subtract).then_inc(lo_done, 1)
            dve.wait_ge(edge_step, 9)
            dve.tensor_copy(k.slot_rows[:, :, 0], row[:, :]).then_inc(edge_step, 1)


def build_pass_d(nc, k, arg, out, m_hi, m_lo, N, E):
    G = N // GT
    NT = G * J
    HC = FE // P
    S = 32
    FH = FE + P
    with Pass(nc, "d") as w:
        w1_raw, w2_raw = w.sb("w1_raw", [P, C, FG]), w.sb("w2_raw", [P, HC + 1, D])
        w1 = [w.sb(f"w1{i}", [P, C, FG], F32R) for i in "hl"]
        w2, w2_lo = w.sb("w2", [P, HC + 1, D], F32R), w.sb("w2_lo", [P, HC, D], F32R)
        b1_raw, b1 = w.sb("b1_raw", [2 * S, FG]), w.sb("b1", [2 * S, FG], F32R)
        bp = w.sb("bp", [2 * S, D], F32R)
        one_raw, one = w.sb("one_raw", [2 * S, PT]), w.sb("one", [2 * S, PT], F32R)
        expert = w.sb("expert", [PT, NE])
        expert_i = w.sb("expert_i", [PT, NE], I32)
        pin, qin, xin = (w.sb(n, [PT, J, D]) for n in ("pin", "qin", "xin"))
        zin, index = w.sb("zin", [PT, J, D]), w.sb("index", [PT, J], I32)
        pos = w.sb("pos", [PT, D])
        ss, floor, rnorm = w.sb("ss", [PT, J]), w.sb("floor", [PT, J]), w.sb("rnorm", [PT, J])
        weighted = w.sb("weighted", [PT, 2, D])
        den, den_eps, rden = w.sb("den", [PT, H]), w.sb("den_eps", [PT, H]), w.sb("rden", [PT, H])
        h = w.sb("h", [PT, 2, D])
        xh = w.sb("xh", [PT, 2, D])
        qn = w.sb("qn", [PT, 2, D])
        x2 = w.sb("x2", [PT, J, D])
        qt = [w.sb(f"qt{i}", [P, 2, C * PT], F32R) for i in "hl"]
        stat, mv, var, rstd = w.sb("stat", [PT, 6]), w.sb("mv", [PT, 2, 2]), w.sb("var", [PT, 1]), w.sb("rstd", [PT, 2])
        shift = w.sb("shift", [PT, 2])
        y = w.sb("y", [PT, 2, D])
        yt = [w.sb(f"yt{i}", [P, 2, C * PT], F32R) for i in "hl"]
        act_hid = w.sb("act_hid", [PT, FE])
        top, top_i, top_f = w.sb("top", [PT, 8]), w.sb("top_i", [PT, 8], U32), w.sb("top_f", [PT, 2])
        gap, th, gap_low, gap_inv, ex = (w.sb(n, [PT, NE]) for n in ("gap", "th", "gap_low", "gap_inv", "ex"))
        is_first, chosen, ex_sum, top_sum, weight, rweight = (w.sb(n, [PT, m]) for n, m in (
            ("is_first", NE), ("chosen", NE), ("ex_sum", 1), ("top_sum", 1), ("weight", 1), ("rweight", 2)))
        sh = w.sb("sh", [PT, 2, FH])
        st, st_lo = w.sb("st", [P, (HC + 1) * PT], F32R), w.sb("st_lo", [P, HC * PT], F32R)
        res = w.sb("res", [PT, J, D])
        b_ty, b_tq, b_mix, b_ts, b_w1, b_w2 = (w.ps(n) for n in ("b_ty", "b_tq", "b_mix", "b_ts", "b_w1", "b_w2"))
        one_set, w2_in = w.sem("one_set"), w.sem("w2_in")
        zeroed, expert_set, w_in, w_hi, w_lo, expert_done = (w.sem(n) for n in ("zeroed", "expert_set", "w_in", "w_hi", "w_lo", "expert_done"))
        p_in, q_in, x_in, o_out = ([w.sem(f"{n}{i}") for i in range(2)] for n in ("p_in", "q_in", "x_in", "o_out"))
        z_in = [w.sem(f"z_in{i}") for i in range(J)]
        prefilled, index_done, sum_done, relu_done, ss_done, floor_done, rnorm_done, h_done, xh_done = (w.sem(n) for n in (
            "prefilled", "index_done", "sum_done", "relu_done", "ss_done", "floor_done", "rnorm_done", "h_done", "xh_done"))
        weighted_done, den_done, rden_done, qn_done = (w.sem(n) for n in ("weighted_done", "den_done", "rden_done", "qn_done"))
        tq_full, tq_hi, tq_lo, mix_full, x2_done, stat_done, aggr, var_done, rstd_done, shift_done, y_done = (w.sem(n) for n in (
            "tq_full", "tq_hi", "tq_lo", "mix_full", "x2_done", "stat_done", "aggr", "var_done", "rstd_done", "shift_done", "y_done"))
        ty_full, ty_hi, ty_lo, hid_full, top_done, gap_done, index_found, tanh_done, gelu_done = (w.sem(n) for n in (
            "ty_full", "ty_hi", "ty_lo", "hid_full", "top_done", "gap_done", "index_found", "tanh_done", "gelu_done"))
        score_step, sh_done, ts_full, ts_hi, ts_lo, out_full, res_done = (w.sem(n) for n in (
            "score_step", "sh_done", "ts_full", "ts_hi", "ts_lo", "out_full", "res_done"))
        block = w.block()

        def group(n, j):
            return (n - j) // J

        def ok(n):
            return not isinstance(n, int) or 0 <= n < NT

        def steps(eng, body):
            tile_steps(eng, body, -6, NT + 4, G)

        @block.sync
        def _(sp):
            for i in range(2):
                load_pair(sp, pin, k.ps[2], 0, 2 * i, p_in[i])
                load_pair(sp, qin, k.phi_q, 0, 2 * i, q_in[i])
                load_pair(sp, xin, arg["x"], 0, 2 * i, x_in[i])
            sp.wait_ge(zeroed, 4)
            sp.dma_start(w1_raw[:, :, FE:FG], arg["L0_ffn_Wg"].rearrange("(c p) e -> p c e", p=P)).then_inc(w_in, 16)
            for e in range(NE):
                sp.dma_start(w1_raw[:, :, e * HE:(e + 1) * HE], arg["L0_ffn_W1"][e].rearrange("(c p) f -> p c f", p=P)).then_inc(w_in, 16)
            sp.dma_start(b1_raw[:, 0:FE], arg["L0_ffn_b1"].rearrange("(o e) f -> o (e f)", o=1).partition_broadcast(2 * S)).then_inc(w_in, 16)
            w2_rows = arg["L0_ffn_W2"].rearrange("e f n -> (e f) n")
            sp.dma_start(w2_raw[:, 0:2, :], w2_rows.rearrange("(c p) n -> p c n", p=P)).then_inc(w2_in, 16)
            for i in range(3):
                sp.dma_start(w2_raw[i * S:i * S + NE, HC, :], arg["L0_ffn_b2"]).then_inc(w2_in, 16)

            def body(s, j):
                n, jn = s + 1, (j + 1) % J
                if ok(n) and jn % 2 == 1 and ok(n + J):
                    sp.wait_ge(xh_done, n + 1)
                    alone(sp, w.sp_waited)
                    load_pair(sp, xin, arg["x"], group(n, jn) + 1, jn - 1, x_in[jn // 2])
                n, jn = s + 2, (j + 2) % J
                if ok(n) and jn % 2 == 1 and ok(n + J):
                    sp.wait_ge(qn_done, n + 1)
                    alone(sp, w.sp_waited)
                    load_pair(sp, qin, k.phi_q, group(n, jn) + 1, jn - 1, q_in[jn // 2])
                    sp.wait_ge(h_done, n + 1)
                    alone(sp, w.sp_waited)
                    load_pair(sp, pin, k.ps[2], group(n, jn) + 1, jn - 1, p_in[jn // 2])
                n = s - 4
                if ok(n) and j % 2 == 1:
                    sp.wait_ge(res_done, n + 1)
                    alone(sp, w.sp_waited)
                    store_pair(sp, out, res, group(n, j), j - 1, o_out[j // 2])
            steps(sp, body)
            for i in range(2):
                sp.wait_ge(o_out[i], 32 * G)

        @block.gpsimd
        def _(pool):
            pool.memset(one_raw[:, :], 0.0).then_inc(zeroed, 1)
            pool.memset(w2_raw[:, HC, :], 0.0).then_inc(zeroed, 1)
            pool.memset(b1_raw[:, :], 0.0).then_inc(zeroed, 1)
            pool.memset(sh[:, :, :], 0.0).then_inc(zeroed, 1)
            pool.iota(expert_i[:, :], pattern=[[1, NE]], base=0, channel_multiplier=0).then_inc(expert_set, 1)
            pool.wait_ge(zeroed, 4)
            pool.wait_ge(expert_set, 1)
            for i in range(2):
                pool.memset(one_raw[i * S:i * S + 1, :], 1.0).then_inc(one_set, 1)
            pool.wait_ge(one_set, 2)

            def gather(n, j):
                need(pool, sum_done, n - J + 1)
                alone(pool, w.pool_waited)
                pool.tensor_copy(index[:, j:j + 1], k.slots[:, :, :].rearrange("p g j -> p (g j)")[:, bass.ds(n, 1)]).then_inc(index_done, 1)
                pool.wait_ge(prefilled, n + 1)
                pool.wait_ge(index_done, n + 1)
                alone(pool, w.pool_waited)
                pool.indirect_dma_start(out=zin[:, j, :], out_offset=None, in_=k.z[:, :],
                                        in_offset=bass.IndirectOffsetOnAxis(ap=index[:, j:j + 1], axis=0),
                                        bounds_check=E - 1, oob_is_err=False).then_inc(z_in[j], 16)

            def body(s, j):
                n, r = s - 1, slot2(j - 1)
                if ok(n):
                    pool.wait_ge(aggr, n + 1)
                    alone(pool, w.pool_waited)
                    pool.tensor_scalar(var[:, :], mv[:, r, 1:2], LN_EPS, None, ALU.add).then_inc(var_done, 1)
                    pool.wait_ge(var_done, n + 1)
                    need(pool, y_done, n - 1)
                    pool.tensor_tensor(rstd[:, r:r + 1], var[:, :], k.minus_half[0:PT, 0:1], ALU.pow).then_inc(rstd_done, 1)
                n, jn = s + 2, (j + 2) % J
                if ok(n):
                    pool.wait_ge(ss_done, n + 1)
                    alone(pool, w.pool_waited)
                    pool.tensor_scalar(floor[:, jn:jn + 1], ss[:, jn:jn + 1], NORM_EPS2, None, ALU.max).then_inc(floor_done, 1)
                    pool.wait_ge(floor_done, n + 1)
                    pool.tensor_tensor(rnorm[:, jn:jn + 1], floor[:, jn:jn + 1], k.minus_half[0:PT, 0:1], ALU.pow).then_inc(rnorm_done, 1)
                n, jn = s + 3, (j + 3) % J
                if ok(n):
                    pool.wait_ge(p_in[jn // 2], 32 * (group(n, jn) + 1))
                    pool.wait_ge(z_in[jn], 16 * (group(n, jn) + 1))
                    pool.tensor_tensor(pin[:, jn, :], pin[:, jn, :], zin[:, jn, :], ALU.add).then_inc(sum_done, 1)
                n, jn = s + 1, (j + 1) % J
                if ok(n):
                    pool.wait_ge(x_in[jn // 2], 32 * (group(n, jn) + 1))
                    pool.wait_ge(h_done, n + 1)
                    need(pool, x2_done, n - 1)
                    pool.tensor_tensor(xh[:, jn % 2, :], xin[:, jn, :], h[:, jn % 2, :], ALU.add).then_inc(xh_done, 1)
                n = s + 4
                if ok(n):
                    pool.wait_ge(q_in[j // 2], 32 * (group(n, j) + 1))
                    need(pool, den_done, 2 * (n - 2) + 1)
                    pool.tensor_tensor(weighted[:, j % 2, :], qin[:, j, :], k.ksum[:, :], ALU.mult).then_inc(weighted_done, 1)
                if ok(s + 5) and not (isinstance(s, int) and s + 5 < J):
                    gather(s + 5, (j + 5) % J)
            for j in range(J):
                gather(j, j)
            steps(pool, body)

        @block.tensor
        def _(pe):
            def body(s, j):
                n = s + 1
                if ok(n):
                    pe.wait_ge(qn_done, n + 1)
                    need(pe, tq_lo, n)
                    for c in range(C):
                        mm = pe.transpose(b_tq[:, c * PT:(c + 1) * PT], qn[:, slot2(j + 1), c * P:(c + 1) * P], k.ident[0:PT, 0:PT])
                    mm.then_inc(tq_full, 1)
                n = s - 4
                if ok(n):
                    if isinstance(s, int) and s == 4:
                        pe.wait_ge(w_lo, 5)
                    pe.wait_ge(ts_lo, 2 * (n + 1))
                    need(pe, res_done, n)
                    for c in range(HC):
                        part = slice(c * PT, (c + 1) * PT)
                        three(pe, b_w2[0:PT, :], st[:, part], st_lo[:, part], w2[:, c, :], w2_lo[:, c, :], c == 0, False)
                    mm = pe.matmul(b_w2[0:PT, :], st[0:3 * S, HC * PT:(HC + 1) * PT], w2[0:3 * S, HC, :], start=False, stop=True)
                    mm.then_inc(out_full, 1)
                if isinstance(s, int) and s == 0:
                    pe.wait_ge(w_lo, 1)
                if ok(s):
                    pe.wait_ge(tq_lo, s + 1)
                    need(pe, x2_done, s)
                    pe.matmul(b_mix[0:PT, :], one[:, :], bp[:, :], start=True, stop=False)
                    for c in range(C):
                        part = slice(c * PT, (c + 1) * PT)
                        mm = three(pe, b_mix[0:PT, :], qt[0][:, j % 2, part], qt[1][:, j % 2, part], m_hi[:, c, :], m_lo[:, c, :], False, c == C - 1)
                    mm.then_inc(mix_full, 1)
                n = s - 1
                if ok(n):
                    pe.wait_ge(y_done, n + 1)
                    need(pe, ty_lo, n)
                    for c in range(C):
                        mm = pe.transpose(b_ty[:, c * PT:(c + 1) * PT], y[:, slot2(j - 1), c * P:(c + 1) * P], k.ident[0:PT, 0:PT])
                    mm.then_inc(ty_full, 1)
                n = s - 3
                if ok(n):
                    pe.wait_ge(sh_done, 2 * (n + 1))
                    need(pe, ts_lo, 2 * n)
                    for c in range(HC + 1):
                        mm = pe.transpose(b_ts[:, c * PT:(c + 1) * PT], sh[:, slot2(j - 3), c * P:(c + 1) * P], k.ident[0:PT, 0:PT])
                    mm.then_inc(ts_full, 1)
                if isinstance(s, int) and s == 2:
                    pe.wait_ge(w_lo, 3)
                n = s - 2
                if ok(n):
                    pe.wait_ge(ty_lo, n + 1)
                    need(pe, gelu_done, n)
                    pe.matmul(b_w1[0:PT, 0:FG], one[:, :], b1[:, :], start=True, stop=False)
                    for c in range(C):
                        part = slice(c * PT, (c + 1) * PT)
                        mm = three(pe, b_w1[0:PT, 0:FG], yt[0][:, j % 2, part], yt[1][:, j % 2, part], w1[0][:, c, :], w1[1][:, c, :], False, c == C - 1)
                    mm.then_inc(hid_full, 1)
            steps(pe, body)

        @block.scalar
        def _(act):
            def prefill(n, j):
                need(act, sum_done, n - J + 1)
                act.activation(zin[:, j, :], k.bias[0:PT, 2, :], ACT.Copy).then_inc(prefilled, 1)
            for j in range(J):
                prefill(j, j)
            act.activation(bp[:, :], k.bp[0:2 * S, :], ACT.Copy).then_inc(w_hi, 1)
            act.wait_ge(one_set, 2)
            act.activation(one[:, :], one_raw[:, :], ACT.Copy).then_inc(w_hi, 1)

            def hidden_weights():
                act.wait_ge(w_in, 16 * (NE + 2))
                act.activation(b1[:, :], b1_raw[:, :], ACT.Copy).then_inc(w_hi, 1)
                act.activation(w1[0][:, :, :], w1_raw[:, :, :], ACT.Copy).then_inc(w_hi, 1)

            def output_weights():
                act.wait_ge(w2_in, 64)
                act.activation(w2[:, :, :], w2_raw[:, :, :], ACT.Copy).then_inc(w_hi, 1)

            def body(s, j):
                n = s - 3
                if ok(n):
                    need(act, sh_done, 2 * n)
                    act.wait_ge(gap_done, n + 1)
                    act.activation(th[:, :], gap[:, :], ACT.Tanh, scale=0.5).then_inc(tanh_done, 1)
                    act.wait_ge(index_found, n + 1)
                    act.activation(act_hid[:, :], b_w1[0:PT, 0:FE], ACT.Gelu).then_inc(gelu_done, 1)
                n = s + 1
                if ok(n):
                    act.wait_ge(tq_full, n + 1)
                    need(act, mix_full, n - 1)
                    act.activation(qt[0][:, slot2(j + 1), :], b_tq[:, 0:C * PT], ACT.Copy).then_inc(tq_hi, 1)
                if ok(s + 6) and not (isinstance(s, int) and s + 6 < J):
                    prefill(s + 6, (j + 6) % J)
                n, jn = s + 2, (j + 2) % J
                if ok(n):
                    act.wait_ge(rnorm_done, n + 1)
                    need(act, xh_done, n - 1)
                    act.activation(h[:, jn % 2, :], pin[:, jn, :], ACT.Relu, scale=rnorm[:, jn:jn + 1]).then_inc(h_done, 1)
                n, jn = s - 1, (j - 1) % J
                if ok(n):
                    act.wait_ge(shift_done, n + 1)
                    need(act, ty_full, n - 1)
                    act.activation(y[:, jn % 2, :], x2[:, jn, :], ACT.Identity, bias=shift[:, jn % 2:jn % 2 + 1],
                                   scale=rstd[:, jn % 2:jn % 2 + 1]).then_inc(y_done, 1)
                n, jn = s + 3, (j + 3) % J
                if ok(n):
                    act.wait_ge(sum_done, n + 1)
                    need(act, ss_done, n)
                    act.activation(pos[:, :], pin[:, jn, :], ACT.Relu).then_inc(relu_done, 1)
                    act.wait_ge(relu_done, n + 1)
                    act.activation(pos[:, :], pos[:, :], ACT.Square, accum_out=ss[:, jn:jn + 1]).then_inc(ss_done, 1)
                n = s - 1
                if ok(n):
                    act.wait_ge(ty_full, n + 1)
                    need(act, hid_full, n - 1)
                    act.activation(yt[0][:, slot2(j - 1), :], b_ty[:, 0:C * PT], ACT.Copy).then_inc(ty_hi, 1)
                n = s - 3
                if ok(n):
                    act.wait_ge(ts_full, n + 1)
                    need(act, out_full, n)
                    act.activation(st[:, :], b_ts[:, 0:(HC + 1) * PT], ACT.Copy).then_inc(ts_hi, 1)
                if isinstance(s, int) and s == 0:
                    hidden_weights()
                if isinstance(s, int) and s == 2:
                    output_weights()
            steps(act, body)

        @block.vector
        def _(dve):
            dve.wait_ge(w_hi, 2)
            dve.tensor_tensor(bp[S:2 * S, :], k.bp[S:2 * S, :], bp[S:2 * S, :].bitcast(F32), ALU.subtract).then_inc(w_lo, 1)
            dve.wait_ge(expert_set, 1)
            dve.tensor_copy(expert[:, :], expert_i[:, :]).then_inc(expert_done, 1)
            dve.wait_ge(expert_done, 1)

            def hidden_weights():
                dve.wait_ge(w_hi, 4)
                dve.tensor_tensor(b1[S:2 * S, :], b1_raw[S:2 * S, :], b1[S:2 * S, :].bitcast(F32), ALU.subtract).then_inc(w_lo, 1)
                dve.tensor_tensor(w1[1][:, :, :], w1_raw[:, :, :], w1[0][:, :, :].bitcast(F32), ALU.subtract).then_inc(w_lo, 1)

            def output_weights():
                dve.wait_ge(w_hi, 5)
                dve.tensor_tensor(w2_lo[:, :, :], w2_raw[:, 0:HC, :], w2[:, 0:HC, :].bitcast(F32), ALU.subtract).then_inc(w_lo, 1)
                dve.tensor_tensor(w2[S:2 * S, HC, :], w2_raw[S:2 * S, HC, :], w2[S:2 * S, HC, :].bitcast(F32), ALU.subtract).then_inc(w_lo, 1)
            SCORE = 9

            def body(s, j):
                n, r = s - 3, slot2(j - 3)
                gate, done = ok(n), SCORE * n
                if gate:
                    dve.wait_ge(hid_full, n + 1)
                    alone(dve, w.dve_waited)
                    dve.max(top[:, :], b_w1[0:PT, FE:FG]).then_inc(top_done, 1)
                    dve.wait_ge(top_done, n + 1)
                    need(dve, tanh_done, n)
                    dve.tensor_scalar(gap[:, :], b_w1[0:PT, FE:FG], top[:, 0:1], None, ALU.subtract).then_inc(gap_done, 1)
                    alone(dve, w.dve_waited)
                    dve.max_index(top_i[:, :], top[:, :], b_w1[0:PT, FE:FG]).then_inc(index_found, 1)
                m = s - 2
                if ok(m):
                    dve.wait_ge(ty_hi, m + 1)
                    dve.tensor_tensor(yt[1][:, slot2(j), :], b_ty[:, 0:C * PT], yt[0][:, slot2(j), :].bitcast(F32), ALU.subtract).then_inc(ty_lo, 1)
                if gate:
                    dve.wait_ge(index_found, n + 1)
                    dve.tensor_copy(top_f[:, :], top_i[:, 0:2]).then_inc(score_step, 1)
                    dve.wait_ge(tanh_done, n + 1)
                    dve.tensor_scalar(gap_low[:, :], th[:, :], -1.0, 1.0, ALU.mult, ALU.add).then_inc(score_step, 1)
                m, jm = s + 2, (j + 2) % J
                if ok(m):
                    dve.wait_ge(rden_done, m + 1)
                    need(dve, tq_full, m - 1)
                    dve.tensor_tensor(qn[:, jm % 2, :].rearrange("p (h r) -> p h r", h=H), qin[:, jm, :].rearrange("p (h r) -> p h r", h=H),
                                      rden[:, :].unsqueeze(2).broadcast_to([PT, H, R]), ALU.mult).then_inc(qn_done, 1)
                if gate:
                    dve.wait_ge(score_step, done + 1)
                    dve.tensor_scalar(is_first[:, :], expert[:, :], top_f[:, 0:1], None, ALU.is_equal).then_inc(score_step, 1)
                    dve.wait_ge(score_step, done + 2)
                    dve.reciprocal(gap_inv[:, :], gap_low[:, :]).then_inc(score_step, 1)
                m, rm = s - 1, slot2(j - 1)
                if ok(m):
                    dve.wait_ge(rstd_done, m + 1)
                    need(dve, y_done, m - 1)
                    dve.scalar_tensor_tensor(shift[:, rm:rm + 1], mv[:, rm, 0:1], -1.0, rstd[:, rm:rm + 1],
                                             ALU.mult, ALU.mult).then_inc(shift_done, 1)
                t, jt = s + 3, (j + 3) % J
                if ok(t):
                    dve.wait_ge(weighted_done, t + 1)
                    dve.tensor_reduce(den[:, :], weighted[:, jt % 2, :].rearrange("p (h r) -> p h r", h=H), AX.X, ALU.add).then_inc(den_done, 1)
                if gate:
                    dve.wait_ge(score_step, done + 3)
                    dve.scalar_tensor_tensor(chosen[:, :], expert[:, :], top_f[:, 1:2], is_first[:, :], ALU.is_equal, ALU.add).then_inc(score_step, 1)
                    dve.wait_ge(score_step, done + 4)
                    dve.scalar_tensor_tensor(ex[:, :], th[:, :], 1.0, gap_inv[:, :], ALU.add, ALU.mult,
                                             accum_out=ex_sum[:, :]).then_inc(score_step, 1)
                m = s + 1
                if ok(m):
                    dve.wait_ge(tq_hi, m + 1)
                    dve.tensor_tensor(qt[1][:, slot2(j + 1), :], b_tq[:, 0:C * PT], qt[0][:, slot2(j + 1), :].bitcast(F32), ALU.subtract).then_inc(tq_lo, 1)
                if gate:
                    dve.wait_ge(score_step, done + 6)
                    need(dve, ts_full, n - 1)
                    dve.scalar_tensor_tensor(sh[:, r, FE:FG], ex[:, :], 1.0, chosen[:, :], ALU.mult, ALU.mult, accum_out=top_sum[:, :]).then_inc(score_step, 1)
                m = s - 4
                if ok(m):
                    dve.wait_ge(out_full, m + 1)
                    dve.wait_ge(score_step, SCORE * (m + 1))
                    need(dve, o_out[j // 2], 32 * group(m, j))
                    dve.scalar_tensor_tensor(res[:, j, :], b_w2[0:PT, :], rweight[:, slot2(j):slot2(j) + 1], x2[:, j, :], ALU.mult, ALU.add).then_inc(res_done, 1)
                if gate:
                    dve.wait_ge(score_step, done + 7)
                    dve.tensor_copy(sh[:, r, FE:FH].rearrange("p (a e) -> p a e", e=S)[:, 1:3, 0:NE],
                                    sh[:, r, FE:FG].unsqueeze(1).broadcast_to([PT, 2, NE])).then_inc(sh_done, 1)
                    dve.wait_ge(gelu_done, n + 1)
                    dve.tensor_tensor(sh[:, r, 0:FE].rearrange("p (e f) -> p e f", e=NE), act_hid[:, :].rearrange("p (e f) -> p e f", e=NE),
                                      sh[:, r, FE:FG].unsqueeze(2).broadcast_to([PT, NE, HE]), ALU.mult).then_inc(sh_done, 1)
                    dve.scalar_tensor_tensor(weight[:, :], ex_sum[:, :], 1e-6, top_sum[:, :], ALU.mult, ALU.add).then_inc(score_step, 1)
                if ok(t):
                    dve.wait_ge(den_done, 2 * t + 1)
                    dve.tensor_scalar(den_eps[:, :], den[:, :], DEN_EPS, None, ALU.add).then_inc(den_done, 1)
                if gate:
                    dve.wait_ge(score_step, done + 8)
                    need(dve, res_done, n - 1)
                    dve.reciprocal(rweight[:, r:r + 1], weight[:, :]).then_inc(score_step, 1)
                if ok(t):
                    dve.wait_ge(den_done, 2 * t + 2)
                    need(dve, qn_done, t)
                    dve.reciprocal(rden[:, :], den_eps[:, :]).then_inc(rden_done, 1)
                if ok(s):
                    dve.wait_ge(mix_full, s + 1)
                    dve.wait_ge(xh_done, s + 1)
                    need(dve, res_done, s - J + 1)
                    dve.tensor_tensor(x2[:, j, :], b_mix[0:PT, :], xh[:, j % 2, :], ALU.add).then_inc(x2_done, 1)
                    dve.wait_ge(x2_done, s + 1)
                    dve.bn_stats(stat[:, :], x2[:, j, :]).then_inc(stat_done, 1)
                if ok(n):
                    dve.wait_ge(ts_hi, n + 1)
                    dve.tensor_tensor(st_lo[:, :], b_ts[:, 0:HC * PT], st[:, 0:HC * PT].bitcast(F32), ALU.subtract).then_inc(ts_lo, 1)
                    third = (slice(2 * S, 3 * S), slice(HC * PT, (HC + 1) * PT))
                    dve.tensor_tensor(st[third], b_ts[third], st[third].bitcast(F32), ALU.subtract).then_inc(ts_lo, 1)
                if ok(s):
                    dve.wait_ge(stat_done, s + 1)
                    alone(dve, w.dve_waited)
                    dve.bn_aggr(mv[:, j % 2, :], stat[:, :]).then_inc(aggr, 1)
                if isinstance(s, int) and s == 0:
                    hidden_weights()
                if isinstance(s, int) and s == 2:
                    output_weights()
            steps(dve, body)


_INS = ["x", "src", "dst", "L0_gnn_W_self", "L0_gnn_W_neigh", "L0_gnn_b", "L0_mix_Wq", "L0_mix_bq", "L0_mix_Wk",
        "L0_mix_bk", "L0_mix_Wv", "L0_mix_bv", "L0_mix_Wp", "L0_mix_bp", "L0_mix_gamma_q", "L0_mix_beta_q",
        "L0_mix_gamma_k", "L0_mix_beta_k", "L0_mix_qG1", "L0_mix_qG2", "L0_mix_kG1", "L0_mix_kG2", "L0_ffn_Wg",
        "L0_ffn_W1", "L0_ffn_b1", "L0_ffn_W2", "L0_ffn_b2"]


class Kept:
    pass


def build(nc, arg, out):
    N = arg["x"].shape[0]
    E = arg["src"].shape[0]
    T = E // PT
    G = N // GT
    assert arg["x"].shape[1] == D and N % GT == 0 and T % J == 0 and T > 2 * J and T == G
    k = Kept()

    def dram(name, shape, dt=F32):
        return nc.dram_tensor("kept_" + name, shape, dt, kind="Internal").ap()

    k.ps = [dram(f"p{l}", [N, D]) for l in range(3)]
    k.hs = [dram(f"h{l}", [N, D]) for l in range(3)]
    k.phi_q = dram("phi_q", [N, D])
    k.z = dram("z", [E, D])
    k.edges_sorted, k.dst_sorted = dram("edges_sorted", [E, 4]), dram("dst_sorted", [E + 2, 1])
    k.slot_map = dram("slot_map", [N + E, 1], I32)
    with ExitStack() as ctx:
        def sb(name, shape, dt=F32):
            return ctx.enter_context(nc.sbuf_tensor(name, shape, dt))

        k.ident, k.ones, k.minus_half = sb("ident", [P, P]), sb("ones", [P, P]), sb("minus_half", [P, 8])
        k.bias, k.bp = sb("bias", [P, 3, D]), sb("bp", [P, D])
        k.kacc = sb("kacc", [PT, D])
        k.src, k.dst, k.rdeg = sb("src", [PT, T], I32), sb("dst", [PT, T]), sb("rdeg", [PT, T])
        k.drow = sb("drow", [P, E + 2])
        k.edge_src, k.edge_dst, k.edge_low = (sb(n, [PT, T]) for n in ("edge_src", "edge_dst", "edge_low"))
        k.edge, k.earlier = sb("edge", [PT, 4]), sb("earlier", [PT, PT])
        k.slot_rows = sb("slot_rows", [PT, T, 2], I32)
        k.slots = sb("slots", [PT, G, J], I32)
        k.ksum = sb("ksum", [PT, D])
        build_constants(nc, k)
        with ExitStack() as held:
            acc = [held.enter_context(nc.psum_tensor(f"acc{c}", [P, 512], F32)) for c in range(C)]
            build_pass_a(nc, k, arg, N, E, acc)
            m_hi, m_lo = sb("m_hi", [P, C, D], F32R), sb("m_lo", [P, C, D], F32R)
            k.w_neigh, k.w_self = ([held.enter_context(nc.sbuf_tensor(f"{n}_{i}", [P, C, D], F32R)) for i in "hl"]
                                   for n in ("w_neigh", "w_self"))
            build_attention_matrix(nc, k, arg, acc, m_hi, m_lo, N, E)
            for l in range(3):
                build_neighbours(nc, k, arg, l, N, E)
                if l < 2:
                    build_layer(nc, k, arg, l + 1, N, E)
        build_pass_d(nc, k, arg, out, m_hi, m_lo, N, E)


def kernel(**inputs):
    import concourse.bacc as bacc
    from concourse.bass_utils import run_bass_kernel_spmd as run

    nc = bacc.Bacc("TRN2", target_bir_lowering=False, num_devices=1)
    arrays, arg = {}, {}
    for name in _INS:
        a = np.ascontiguousarray(inputs[name])
        arrays["in_" + name] = a
        arg[name] = nc.dram_tensor("in_" + name, a.shape, mybir.dt.from_np(a.dtype), kind="ExternalInput").ap()
    out = nc.dram_tensor("out", inputs["x"].shape, F32, kind="ExternalOutput").ap()
    build(nc, arg, out)
    return run(nc, [arrays], core_ids=[0]).results[0]["out"]
```
